# Optimizing a Trainium2 kernel written in Bass

```python
import numpy as np
import jax
import jax.numpy as jnp

def _softmax(x, axis=-1):
    return jax.nn.softmax(x, axis=axis)

def _gelu(x):
    return jax.nn.gelu(x, approximate=True)

def _silu(x):
    return jax.nn.silu(x)

def _sigmoid(x):
    return jax.nn.sigmoid(x)

def _layernorm(x, axis=-1, eps=1e-05):
    m = jnp.mean(x, axis=axis, keepdims=True)
    v = jnp.var(x, axis=axis, keepdims=True)
    return (x - m) / jnp.sqrt(v + eps)

def _scatter_add(tgt, idx, src, axis=0):
    return tgt.at[idx].add(src)

def _segment_sum(src, seg, n):
    return jax.ops.segment_sum(src, seg, n)
kernel_name = 'mk_gps_d4_gnn_r16_1f8160'

def setup_inputs(seed: int=0):
    np.random.seed(seed)
    _w = jnp.asarray

    def _rec_inputs():
        import jax
        import jax.numpy as jnp
        _gk = jax.random.key(seed)
        x = -0.0003713 + 1 * jax.random.normal(jax.random.fold_in(_gk, 1), (3125, 256), jnp.float32)
        src = jax.random.randint(jax.random.fold_in(_gk, 2), (50000,), 0, 3125, jnp.int32)
        dst = jnp.minimum((3125 * jax.random.uniform(jax.random.fold_in(_gk, 3), (50000,)) ** 2.0).astype(jnp.int32), 49999)
        _o = jnp.argsort(dst, stable=True)
        src = src[_o]
        dst = dst[_o]
        edge_weight = jax.random.uniform(jax.random.fold_in(_gk, 12), (50000,), jnp.float32, 0.0, 0.999998)
        return (x, src, dst, edge_weight)
    x, src, dst, edge_weight = _rec_inputs()

    def _L0_gnn_setup():
        import jax, jax.numpy as jnp
        import numpy as np
        N, F, H, C = (3125, 256, 4, 64)
        E = 50000
        NEG_SLOPE = 0.2
        LN_EPS = 1e-05
        key = jax.random.key(seed)
        ks = jax.random.split(key, 8)
        x = jax.random.normal(ks[0], (N, F), dtype=jnp.float32)
        edge_index = jax.random.randint(ks[1], (2, E), 0, N, dtype=jnp.int32)
        W = jax.random.normal(ks[2], (F, H * C), dtype=jnp.float32) / np.sqrt(F)
        att_src = jax.random.normal(ks[3], (H, C), dtype=jnp.float32) / np.sqrt(C)
        att_dst = jax.random.normal(ks[4], (H, C), dtype=jnp.float32) / np.sqrt(C)
        bias = jnp.zeros((H * C,), dtype=jnp.float32)
        gamma = jnp.ones((H * C,), dtype=jnp.float32)
        beta = jnp.zeros((H * C,), dtype=jnp.float32)
        return {'x': x, 'edge_index': edge_index, 'W': W, 'att_src': att_src, 'att_dst': att_dst, 'bias': bias, 'gamma': gamma, 'beta': beta}
    _L0_gnn_all = _L0_gnn_setup()
    _L0_gnn_in = {k: v for k, v in _L0_gnn_all.items() if k in ('W', 'att_src', 'att_dst', 'bias', 'gamma', 'beta')}
    del _L0_gnn_all

    def _L0_mix_setup():
        import jax, jax.numpy as jnp
        import numpy as np
        MIDC = 256
        HEADS = 8
        HEADC = MIDC // HEADS
        EPS = 1e-05

        def _ln(x, gamma, beta):
            mu = jnp.mean(x, axis=-1, keepdims=True)
            var = jnp.var(x, axis=-1, keepdims=True)
            return (x - mu) * jax.lax.rsqrt(var + EPS) * gamma + beta
        key = jax.random.key(seed)
        ks = jax.random.split(key, 8)
        B, HW, C = (8, 256, MIDC)
        s = 1.0 / np.sqrt(C)
        return {'x': jax.random.normal(ks[0], (B, HW, C), jnp.float32), 'w_qkv': jax.random.normal(ks[1], (C, 3 * C), jnp.float32) * s, 'b_qkv': jnp.zeros((3 * C,), jnp.float32), 'kln_g': jnp.ones((HEADC,), jnp.float32), 'kln_b': jnp.zeros((HEADC,), jnp.float32), 'vln_g': jnp.ones((HEADC,), jnp.float32), 'vln_b': jnp.zeros((HEADC,), jnp.float32), 'w1': jax.random.normal(ks[2], (C, C), jnp.float32) * s, 'b1': jnp.zeros((C,), jnp.float32), 'w2': jax.random.normal(ks[3], (C, C), jnp.float32) * s, 'b2': jnp.zeros((C,), jnp.float32)}
    _L0_mix_all = _L0_mix_setup()
    _L0_mix_in = {k: v for k, v in _L0_mix_all.items() if k in ('w_qkv', 'b_qkv', 'kln_g', 'kln_b', 'vln_g', 'vln_b', 'w1', 'b1', 'w2', 'b2')}
    del _L0_mix_all

    def _L0_ffn_setup():
        import jax, jax.numpy as jnp
        import numpy as np
        B, T, D, H, E = (16, 256, 256, 512, 8)
        key = jax.random.key(seed)
        ks = jax.random.split(key, 5)
        x = jax.random.normal(ks[0], (B, T, D), dtype=jnp.float32)
        gate_w = jax.random.normal(ks[1], (D, E), dtype=jnp.float32) * 0.02
        gate_b = jnp.zeros((E,), dtype=jnp.float32)
        W1 = jax.random.normal(ks[2], (E, D, H), dtype=jnp.float32) * 0.02
        b1 = jnp.zeros((E, H), dtype=jnp.float32)
        W2 = jax.random.normal(ks[3], (E, H, D), dtype=jnp.float32) * 0.02
        b2 = jnp.zeros((E, D), dtype=jnp.float32)
        return {'x': x, 'gate_w': gate_w, 'gate_b': gate_b, 'W1': W1, 'b1': b1, 'W2': W2, 'b2': b2}
    _L0_ffn_all = _L0_ffn_setup()
    _L0_ffn_in = {k: v for k, v in _L0_ffn_all.items() if k in ('gate_w', 'gate_b', 'W1', 'b1', 'W2', 'b2')}
    del _L0_ffn_all

    def _L1_gnn_setup():
        import jax, jax.numpy as jnp
        import numpy as np
        EPS = 1e-05

        def _bn(x, gamma, beta):
            m = jnp.mean(x, axis=0)
            v = jnp.mean((x - m) ** 2, axis=0)
            return gamma * (x - m) * jax.lax.rsqrt(v + EPS) + beta

        def _hconv(x, src, dst, ew, w1, b1, w2, b2, g, b):
            h = jax.nn.relu(x @ w1 + b1)
            msg = ew[:, None] * h[src]
            agg = jax.ops.segment_sum(msg, dst, num_segments=x.shape[0])
            h = agg @ w2 + b2
            return jax.nn.relu(_bn(h, g, b))
        N, C, E = (3125, 256, 18750)
        key = jax.random.key(seed)
        ks = jax.random.split(key, 16)
        s = 1.0 / np.sqrt(C)
        inp = {'x': jax.random.normal(ks[0], (N, C), dtype=jnp.float32), 'hyperedge_index': jax.random.randint(ks[1], (2, E), 0, N, dtype=jnp.int32), 'hyperedge_weight': jax.random.uniform(ks[2], (E,), dtype=jnp.float32), 'c1_w1': jax.random.normal(ks[3], (C, C), dtype=jnp.float32) * s, 'c1_b1': jnp.zeros((C,), jnp.float32), 'c1_w2': jax.random.normal(ks[4], (C, C), dtype=jnp.float32) * s, 'c1_b2': jnp.zeros((C,), jnp.float32), 'c1_g': jnp.ones((C,), jnp.float32), 'c1_b': jnp.zeros((C,), jnp.float32), 'bn1_g': jnp.ones((C,), jnp.float32), 'bn1_b': jnp.zeros((C,), jnp.float32), 'c2_w1': jax.random.normal(ks[5], (C, C), dtype=jnp.float32) * s, 'c2_b1': jnp.zeros((C,), jnp.float32), 'c2_w2': jax.random.normal(ks[6], (C, C), dtype=jnp.float32) * s, 'c2_b2': jnp.zeros((C,), jnp.float32), 'c2_g': jnp.ones((C,), jnp.float32), 'c2_b': jnp.zeros((C,), jnp.float32), 'bn2_g': jnp.ones((C,), jnp.float32), 'bn2_b': jnp.zeros((C,), jnp.float32)}
        return inp
    _L1_gnn_all = _L1_gnn_setup()
    _L1_gnn_in = {k: v for k, v in _L1_gnn_all.items() if k in ('c1_w1', 'c1_b1', 'c1_w2', 'c1_b2', 'c1_g', 'c1_b', 'bn1_g', 'bn1_b', 'c2_w1', 'c2_b1', 'c2_w2', 'c2_b2', 'c2_g', 'c2_b', 'bn2_g', 'bn2_b')}
    del _L1_gnn_all

    def _L1_mix_setup():
        import jax, jax.numpy as jnp
        import numpy as np
        HEADS = 4
        DIM_HEAD = 32
        key = jax.random.key(seed)
        k1, k2, k3 = jax.random.split(key, 3)
        B, L, D = (16, 512, 256)
        hidden = HEADS * DIM_HEAD
        x = jax.random.normal(k1, (B, L, D), dtype=jnp.float32)
        W_qkv = jax.random.normal(k2, (D, 3 * hidden), dtype=jnp.float32) * D ** (-0.5)
        W_out = jax.random.normal(k3, (hidden, D), dtype=jnp.float32) * hidden ** (-0.5)
        b_out = jnp.zeros((D,), dtype=jnp.float32)
        return {'x': x, 'W_qkv': W_qkv, 'W_out': W_out, 'b_out': b_out}
    _L1_mix_all = _L1_mix_setup()
    _L1_mix_in = {k: v for k, v in _L1_mix_all.items() if k in ('W_qkv', 'W_out', 'b_out')}
    del _L1_mix_all

    def _L1_ffn_setup():
        import jax, jax.numpy as jnp
        import numpy as np
        D_MODEL = 256
        EXPERT_DIM = 512
        NUM_EXPERTS = 8
        TOP_K = 2
        SEQ_LEN = 128
        BATCH = 2
        key = jax.random.key(seed)
        ks = jax.random.split(key, 8)
        s = 0.02
        x = jax.random.normal(ks[0], (SEQ_LEN, BATCH, D_MODEL), dtype=jnp.float32)
        Wg = jax.random.normal(ks[1], (D_MODEL, NUM_EXPERTS), dtype=jnp.float32) * s
        bg = jax.random.normal(ks[2], (NUM_EXPERTS,), dtype=jnp.float32) * s
        bias = jnp.zeros((NUM_EXPERTS,), dtype=jnp.float32)
        W1 = jax.random.normal(ks[3], (NUM_EXPERTS, D_MODEL, EXPERT_DIM), dtype=jnp.float32) * s
        b1 = jax.random.normal(ks[4], (NUM_EXPERTS, EXPERT_DIM), dtype=jnp.float32) * s
        W2 = jax.random.normal(ks[5], (NUM_EXPERTS, EXPERT_DIM, D_MODEL), dtype=jnp.float32) * s
        b2 = jax.random.normal(ks[6], (NUM_EXPERTS, D_MODEL), dtype=jnp.float32) * s
        return {'x': x, 'Wg': Wg, 'bg': bg, 'bias': bias, 'W1': W1, 'b1': b1, 'W2': W2, 'b2': b2}
    _L1_ffn_all = _L1_ffn_setup()
    _L1_ffn_in = {k: v for k, v in _L1_ffn_all.items() if k in ('Wg', 'bg', 'bias', 'W1', 'b1', 'W2', 'b2')}
    del _L1_ffn_all

    def _L2_gnn_setup():
        import jax, jax.numpy as jnp
        import numpy as np
        N, E = (3125, 50000)
        IN, H, C = (256, 8, 32)
        NEG_SLOPE = 0.2
        EPS = 1e-05
        key = jax.random.key(seed)
        ks = jax.random.split(key, 6)
        x = jax.random.normal(ks[0], (N, IN), jnp.float32)
        edge_index = jax.random.randint(ks[1], (2, E), 0, N, dtype=jnp.int32)
        W = jax.random.normal(ks[2], (IN, H * C), jnp.float32) / np.sqrt(IN).astype(np.float32)
        att_src = jax.random.normal(ks[3], (H, C), jnp.float32) * 0.1
        att_dst = jax.random.normal(ks[4], (H, C), jnp.float32) * 0.1
        bias = jnp.zeros((H * C,), jnp.float32)
        gamma = jnp.ones((H * C,), jnp.float32)
        beta = jnp.zeros((H * C,), jnp.float32)
        return {'x': x, 'edge_index': edge_index, 'W': W, 'att_src': att_src, 'att_dst': att_dst, 'bias': bias, 'gamma': gamma, 'beta': beta}
    _L2_gnn_all = _L2_gnn_setup()
    _L2_gnn_in = {k: v for k, v in _L2_gnn_all.items() if k in ('W', 'att_src', 'att_dst', 'bias', 'gamma', 'beta')}
    del _L2_gnn_all

    def _L2_mix_setup():
        import math
        import jax, jax.numpy as jnp
        import numpy as np
        EPS_DIV = 1e-07
        EPS_NORM = 1e-12

        def _l2_normalize(x, axis):
            n = jnp.sqrt(jnp.sum(x * x, axis=axis, keepdims=True))
            return x / jnp.maximum(n, EPS_NORM)
        key = jax.random.key(seed)
        ks = jax.random.split(key, 5)
        b, N, C = (8, 256, 256)
        x = jax.random.normal(ks[0], (b, N, C), dtype=jnp.float32)
        W_qkv = jax.random.normal(ks[1], (C, 3 * C), dtype=jnp.float32) * (1.0 / math.sqrt(C))
        b_qkv = jax.random.normal(ks[2], (3 * C,), dtype=jnp.float32) * 0.02
        W_out = jax.random.normal(ks[3], (C, C), dtype=jnp.float32) * (1.0 / math.sqrt(C))
        b_out = jax.random.normal(ks[4], (C,), dtype=jnp.float32) * 0.02
        return {'x': x, 'W_qkv': W_qkv, 'b_qkv': b_qkv, 'W_out': W_out, 'b_out': b_out}
    _L2_mix_all = _L2_mix_setup()
    _L2_mix_in = {k: v for k, v in _L2_mix_all.items() if k in ('W_qkv', 'b_qkv', 'W_out', 'b_out')}
    del _L2_mix_all

    def _L2_ffn_setup():
        import jax, jax.numpy as jnp
        import numpy as np
        B, S, D = (8, 256, 256)
        H = 4 * D
        CAPACITY = 0.5
        key = jax.random.key(seed)
        ks = jax.random.split(key, 6)
        x = jax.random.normal(ks[0], (B, S, D), dtype=jnp.float32)
        attention_mask = jnp.zeros((B, 1, 1, S), dtype=jnp.float32)
        wr = jax.random.normal(ks[1], (D, 1), dtype=jnp.float32) * 0.02
        br = jnp.zeros((1,), dtype=jnp.float32)
        w1 = jax.random.normal(ks[2], (D, H), dtype=jnp.float32) * 0.02
        b1 = jnp.zeros((H,), dtype=jnp.float32)
        w2 = jax.random.normal(ks[3], (H, D), dtype=jnp.float32) * 0.02
        b2 = jnp.zeros((D,), dtype=jnp.float32)
        return {'x': x, 'attention_mask': attention_mask, 'wr': wr, 'br': br, 'w1': w1, 'b1': b1, 'w2': w2, 'b2': b2}
    _L2_ffn_all = _L2_ffn_setup()
    _L2_ffn_in = {k: v for k, v in _L2_ffn_all.items() if k in ('attention_mask', 'wr', 'br', 'w1', 'b1', 'w2', 'b2')}
    del _L2_ffn_all

    def _L3_gnn_setup():
        import jax, jax.numpy as jnp
        import numpy as np
        N_NODES = 625
        N_EDGES = 10000
        IN_DIM, HID_DIM, OUT_DIM = (256, 512, 256)

        def gcn_conv(x, W, b, src, dst, dinv):
            h = x @ W
            norm = dinv[src] * dinv[dst]
            msg = h[src] * norm[:, None]
            agg = jnp.zeros_like(h).at[dst].add(msg)
            agg = agg + h * (dinv * dinv)[:, None]
            return agg + b
        key = jax.random.key(seed)
        ks = jax.random.split(key, 8)
        x = jax.random.normal(ks[0], (N_NODES, IN_DIM), dtype=jnp.float32)
        edge_index = jax.random.randint(ks[1], (2, N_EDGES), 0, N_NODES, dtype=jnp.int64)

        def glorot(k, fan_in, fan_out):
            s = jnp.sqrt(6.0 / (fan_in + fan_out)).astype(jnp.float32)
            return jax.random.uniform(k, (fan_in, fan_out), jnp.float32, -s, s)
        return {'x': x, 'W1': glorot(ks[2], IN_DIM, HID_DIM), 'b1': jnp.zeros((HID_DIM,), jnp.float32), 'W2': glorot(ks[3], HID_DIM, HID_DIM), 'b2': jnp.zeros((HID_DIM,), jnp.float32), 'W3': glorot(ks[4], HID_DIM, OUT_DIM), 'b3': jnp.zeros((OUT_DIM,), jnp.float32), 'edge_index': edge_index}
    _L3_gnn_all = _L3_gnn_setup()
    _L3_gnn_in = {k: v for k, v in _L3_gnn_all.items() if k in ('W1', 'b1', 'W2', 'b2', 'W3', 'b3')}
    del _L3_gnn_all

    def _L3_mix_setup():
        import jax, jax.numpy as jnp
        import numpy as np
        import math
        EMBED = 256
        HEADS = 4
        HEAD_DIM = EMBED // HEADS
        OUT_DIM = 256
        LN_EPS = 1e-05

        def _qkv_init(key):
            spread = math.sqrt(3.0 / EMBED)
            gain, delta = (0.01, 0.01)
            w = jax.random.uniform(key, (EMBED, EMBED), minval=-spread, maxval=spread) * gain
            return w + delta * jnp.eye(EMBED, dtype=w.dtype)

        def _layer_norm(x, g, b):
            mu = jnp.mean(x, axis=-1, keepdims=True)
            var = jnp.mean(jnp.square(x - mu), axis=-1, keepdims=True)
            return (x - mu) * jax.lax.rsqrt(var + LN_EPS) * g + b

        def _split_heads(x, B, S):
            return x.reshape(B, S, HEADS, HEAD_DIM).transpose(0, 2, 1, 3)
        key = jax.random.key(seed)
        ks = jax.random.split(key, 6)
        seq = jax.random.normal(ks[0], (4, 512, EMBED), dtype=jnp.float32)
        wq = _qkv_init(ks[1])
        wk = _qkv_init(ks[2])
        wv = _qkv_init(ks[3])
        bound = 1.0 / math.sqrt(EMBED)
        wo = jax.random.uniform(ks[4], (OUT_DIM, EMBED), minval=-bound, maxval=bound)
        bo = jax.random.uniform(ks[5], (OUT_DIM,), minval=-bound, maxval=bound)
        ln_k_g = jnp.ones((HEAD_DIM,), jnp.float32)
        ln_k_b = jnp.zeros((HEAD_DIM,), jnp.float32)
        ln_v_g = jnp.ones((HEAD_DIM,), jnp.float32)
        ln_v_b = jnp.zeros((HEAD_DIM,), jnp.float32)
        return {'seq': seq, 'wq': wq, 'wk': wk, 'wv': wv, 'wo': wo, 'bo': bo, 'ln_k_g': ln_k_g, 'ln_k_b': ln_k_b, 'ln_v_g': ln_v_g, 'ln_v_b': ln_v_b}
    _L3_mix_all = _L3_mix_setup()
    _L3_mix_in = {k: v for k, v in _L3_mix_all.items() if k in ('wq', 'wk', 'wv', 'wo', 'bo', 'ln_k_g', 'ln_k_b', 'ln_v_g', 'ln_v_b')}
    del _L3_mix_all

    def _L3_ffn_setup():
        import jax, jax.numpy as jnp
        import numpy as np
        TOP_K = 2
        LN_EPS = 1e-05
        key = jax.random.key(seed)
        ks = jax.random.split(key, 8)
        B, S, D, E, H = (16, 1024, 256, 8, 1024)
        x = jax.random.normal(ks[0], (B, S, D), dtype=jnp.float32)
        Wr = jax.random.normal(ks[1], (D, E), dtype=jnp.float32) * 0.1
        br = jnp.zeros((E,), dtype=jnp.float32)
        ln_g = jnp.ones((E, D), dtype=jnp.float32)
        ln_b = jnp.zeros((E, D), dtype=jnp.float32)
        W1 = jax.random.normal(ks[2], (E, D, H), dtype=jnp.float32) * (1.0 / np.sqrt(D))
        b1 = jnp.zeros((E, H), dtype=jnp.float32)
        W2 = jax.random.normal(ks[3], (E, H, D), dtype=jnp.float32) * (1.0 / np.sqrt(H))
        b2 = jnp.zeros((E, D), dtype=jnp.float32)
        return {'x': x, 'Wr': Wr, 'br': br, 'ln_g': ln_g, 'ln_b': ln_b, 'W1': W1, 'b1': b1, 'W2': W2, 'b2': b2}
    _L3_ffn_all = _L3_ffn_setup()
    _L3_ffn_in = {k: v for k, v in _L3_ffn_all.items() if k in ('Wr', 'br', 'ln_g', 'ln_b', 'W1', 'b1', 'W2', 'b2')}
    del _L3_ffn_all
    return {'x': x, 'src': src, 'dst': dst, 'edge_weight': edge_weight, 'L0_gnn_W': _L0_gnn_in['W'], 'L0_gnn_att_src': _L0_gnn_in['att_src'], 'L0_gnn_att_dst': _L0_gnn_in['att_dst'], 'L0_gnn_bias': _L0_gnn_in['bias'], 'L0_gnn_gamma': _L0_gnn_in['gamma'], 'L0_gnn_beta': _L0_gnn_in['beta'], 'L0_mix_w_qkv': _L0_mix_in['w_qkv'], 'L0_mix_b_qkv': _L0_mix_in['b_qkv'], 'L0_mix_kln_g': _L0_mix_in['kln_g'], 'L0_mix_kln_b': _L0_mix_in['kln_b'], 'L0_mix_vln_g': _L0_mix_in['vln_g'], 'L0_mix_vln_b': _L0_mix_in['vln_b'], 'L0_mix_w1': _L0_mix_in['w1'], 'L0_mix_b1': _L0_mix_in['b1'], 'L0_mix_w2': _L0_mix_in['w2'], 'L0_mix_b2': _L0_mix_in['b2'], 'L0_ffn_gate_w': _L0_ffn_in['gate_w'], 'L0_ffn_gate_b': _L0_ffn_in['gate_b'], 'L0_ffn_W1': _L0_ffn_in['W1'], 'L0_ffn_b1': _L0_ffn_in['b1'], 'L0_ffn_W2': _L0_ffn_in['W2'], 'L0_ffn_b2': _L0_ffn_in['b2'], 'L1_gnn_c1_w1': _L1_gnn_in['c1_w1'], 'L1_gnn_c1_b1': _L1_gnn_in['c1_b1'], 'L1_gnn_c1_w2': _L1_gnn_in['c1_w2'], 'L1_gnn_c1_b2': _L1_gnn_in['c1_b2'], 'L1_gnn_c1_g': _L1_gnn_in['c1_g'], 'L1_gnn_c1_b': _L1_gnn_in['c1_b'], 'L1_gnn_bn1_g': _L1_gnn_in['bn1_g'], 'L1_gnn_bn1_b': _L1_gnn_in['bn1_b'], 'L1_gnn_c2_w1': _L1_gnn_in['c2_w1'], 'L1_gnn_c2_b1': _L1_gnn_in['c2_b1'], 'L1_gnn_c2_w2': _L1_gnn_in['c2_w2'], 'L1_gnn_c2_b2': _L1_gnn_in['c2_b2'], 'L1_gnn_c2_g': _L1_gnn_in['c2_g'], 'L1_gnn_c2_b': _L1_gnn_in['c2_b'], 'L1_gnn_bn2_g': _L1_gnn_in['bn2_g'], 'L1_gnn_bn2_b': _L1_gnn_in['bn2_b'], 'L1_mix_W_qkv': _L1_mix_in['W_qkv'], 'L1_mix_W_out': _L1_mix_in['W_out'], 'L1_mix_b_out': _L1_mix_in['b_out'], 'L1_ffn_Wg': _L1_ffn_in['Wg'], 'L1_ffn_bg': _L1_ffn_in['bg'], 'L1_ffn_bias': _L1_ffn_in['bias'], 'L1_ffn_W1': _L1_ffn_in['W1'], 'L1_ffn_b1': _L1_ffn_in['b1'], 'L1_ffn_W2': _L1_ffn_in['W2'], 'L1_ffn_b2': _L1_ffn_in['b2'], 'L2_gnn_W': _L2_gnn_in['W'], 'L2_gnn_att_src': _L2_gnn_in['att_src'], 'L2_gnn_att_dst': _L2_gnn_in['att_dst'], 'L2_gnn_bias': _L2_gnn_in['bias'], 'L2_gnn_gamma': _L2_gnn_in['gamma'], 'L2_gnn_beta': _L2_gnn_in['beta'], 'L2_mix_W_qkv': _L2_mix_in['W_qkv'], 'L2_mix_b_qkv': _L2_mix_in['b_qkv'], 'L2_mix_W_out': _L2_mix_in['W_out'], 'L2_mix_b_out': _L2_mix_in['b_out'], 'L2_ffn_attention_mask': _L2_ffn_in['attention_mask'], 'L2_ffn_wr': _L2_ffn_in['wr'], 'L2_ffn_br': _L2_ffn_in['br'], 'L2_ffn_w1': _L2_ffn_in['w1'], 'L2_ffn_b1': _L2_ffn_in['b1'], 'L2_ffn_w2': _L2_ffn_in['w2'], 'L2_ffn_b2': _L2_ffn_in['b2'], 'L3_gnn_W1': _L3_gnn_in['W1'], 'L3_gnn_b1': _L3_gnn_in['b1'], 'L3_gnn_W2': _L3_gnn_in['W2'], 'L3_gnn_b2': _L3_gnn_in['b2'], 'L3_gnn_W3': _L3_gnn_in['W3'], 'L3_gnn_b3': _L3_gnn_in['b3'], 'L3_mix_wq': _L3_mix_in['wq'], 'L3_mix_wk': _L3_mix_in['wk'], 'L3_mix_wv': _L3_mix_in['wv'], 'L3_mix_wo': _L3_mix_in['wo'], 'L3_mix_bo': _L3_mix_in['bo'], 'L3_mix_ln_k_g': _L3_mix_in['ln_k_g'], 'L3_mix_ln_k_b': _L3_mix_in['ln_k_b'], 'L3_mix_ln_v_g': _L3_mix_in['ln_v_g'], 'L3_mix_ln_v_b': _L3_mix_in['ln_v_b'], 'L3_ffn_Wr': _L3_ffn_in['Wr'], 'L3_ffn_br': _L3_ffn_in['br'], 'L3_ffn_ln_g': _L3_ffn_in['ln_g'], 'L3_ffn_ln_b': _L3_ffn_in['ln_b'], 'L3_ffn_W1': _L3_ffn_in['W1'], 'L3_ffn_b1': _L3_ffn_in['b1'], 'L3_ffn_W2': _L3_ffn_in['W2'], 'L3_ffn_b2': _L3_ffn_in['b2']}

def reference(x, src, dst, edge_weight, L0_gnn_W, L0_gnn_att_src, L0_gnn_att_dst, L0_gnn_bias, L0_gnn_gamma, L0_gnn_beta, L0_mix_w_qkv, L0_mix_b_qkv, L0_mix_kln_g, L0_mix_kln_b, L0_mix_vln_g, L0_mix_vln_b, L0_mix_w1, L0_mix_b1, L0_mix_w2, L0_mix_b2, L0_ffn_gate_w, L0_ffn_gate_b, L0_ffn_W1, L0_ffn_b1, L0_ffn_W2, L0_ffn_b2, L1_gnn_c1_w1, L1_gnn_c1_b1, L1_gnn_c1_w2, L1_gnn_c1_b2, L1_gnn_c1_g, L1_gnn_c1_b, L1_gnn_bn1_g, L1_gnn_bn1_b, L1_gnn_c2_w1, L1_gnn_c2_b1, L1_gnn_c2_w2, L1_gnn_c2_b2, L1_gnn_c2_g, L1_gnn_c2_b, L1_gnn_bn2_g, L1_gnn_bn2_b, L1_mix_W_qkv, L1_mix_W_out, L1_mix_b_out, L1_ffn_Wg, L1_ffn_bg, L1_ffn_bias, L1_ffn_W1, L1_ffn_b1, L1_ffn_W2, L1_ffn_b2, L2_gnn_W, L2_gnn_att_src, L2_gnn_att_dst, L2_gnn_bias, L2_gnn_gamma, L2_gnn_beta, L2_mix_W_qkv, L2_mix_b_qkv, L2_mix_W_out, L2_mix_b_out, L2_ffn_attention_mask, L2_ffn_wr, L2_ffn_br, L2_ffn_w1, L2_ffn_b1, L2_ffn_w2, L2_ffn_b2, L3_gnn_W1, L3_gnn_b1, L3_gnn_W2, L3_gnn_b2, L3_gnn_W3, L3_gnn_b3, L3_mix_wq, L3_mix_wk, L3_mix_wv, L3_mix_wo, L3_mix_bo, L3_mix_ln_k_g, L3_mix_ln_k_b, L3_mix_ln_v_g, L3_mix_ln_v_b, L3_ffn_Wr, L3_ffn_br, L3_ffn_ln_g, L3_ffn_ln_b, L3_ffn_W1, L3_ffn_b1, L3_ffn_W2, L3_ffn_b2):
    import jax
    import jax.numpy as jnp

    def _L0_gnn_ref(x, edge_index, W, att_src, att_dst, bias, gamma, beta):
        import jax, jax.numpy as jnp
        import numpy as np
        N, F, H, C = (3125, 256, 4, 64)
        E = 50000
        NEG_SLOPE = 0.2
        LN_EPS = 1e-05
        n = x.shape[0]
        loops = jnp.arange(n, dtype=edge_index.dtype)
        src = jnp.concatenate([edge_index[0], loops])
        dst = jnp.concatenate([edge_index[1], loops])
        h = (x @ W).reshape(n, H, C)
        a_src = jnp.einsum('nhc,hc->nh', h, att_src)
        a_dst = jnp.einsum('nhc,hc->nh', h, att_dst)
        alpha = a_src[src] + a_dst[dst]
        alpha = jnp.where(alpha >= 0, alpha, NEG_SLOPE * alpha)
        seg_max = jax.ops.segment_max(alpha, dst, num_segments=n)
        alpha = jnp.exp(alpha - seg_max[dst])
        seg_sum = jax.ops.segment_sum(alpha, dst, num_segments=n)
        alpha = alpha / (seg_sum[dst] + 1e-16)
        msg = h[src] * alpha[:, :, None]
        out = jax.ops.segment_sum(msg, dst, num_segments=n)
        out = out.reshape(n, H * C) + bias
        mu = jnp.mean(out, axis=-1, keepdims=True)
        var = jnp.var(out, axis=-1, keepdims=True)
        out = (out - mu) * jax.lax.rsqrt(var + LN_EPS) * gamma + beta
        return out

    def _L0_mix_ref(x, w_qkv, b_qkv, kln_g, kln_b, vln_g, vln_b, w1, b1, w2, b2):
        import jax, jax.numpy as jnp
        import numpy as np
        MIDC = 256
        HEADS = 8
        HEADC = MIDC // HEADS
        EPS = 1e-05

        def _ln(x, gamma, beta):
            mu = jnp.mean(x, axis=-1, keepdims=True)
            var = jnp.var(x, axis=-1, keepdims=True)
            return (x - mu) * jax.lax.rsqrt(var + EPS) * gamma + beta
        B, HW, C = x.shape
        bias = x
        qkv = (x @ w_qkv + b_qkv).reshape(B, HW, HEADS, 3 * HEADC)
        qkv = qkv.transpose(0, 2, 1, 3)
        q, k, v = jnp.split(qkv, 3, axis=-1)
        k = _ln(k, kln_g, kln_b)
        v = _ln(v, vln_g, vln_b)
        kv = jnp.einsum('bhnd,bhne->bhde', k, v) / HW
        out = jnp.einsum('bhnd,bhde->bhne', q, kv)
        out = out.transpose(0, 2, 1, 3).reshape(B, HW, C)
        ret = out + bias
        h = jax.nn.gelu(ret @ w1 + b1, approximate=False)
        return h @ w2 + b2 + bias

    def _L0_ffn_ref(x, gate_w, gate_b, W1, b1, W2, b2):
        import jax, jax.numpy as jnp
        import numpy as np
        B, T, D, H, E = (16, 256, 256, 512, 8)
        Bb, Tt, Dd = x.shape
        Ee = gate_w.shape[1]
        xf = x.reshape(-1, Dd)
        N = xf.shape[0]
        logits = xf @ gate_w + gate_b
        probs = jax.nn.softmax(logits, axis=-1)
        top2_vals, top2_idx = jax.lax.top_k(probs, 2)
        cw = jnp.zeros((N, Ee), dtype=xf.dtype).at[jnp.arange(N)[:, None], top2_idx].add(top2_vals)

        def step(acc, params):
            w1, bb1, w2, bb2, we = params
            h = jax.nn.gelu(xf @ w1 + bb1, approximate=False)
            y = h @ w2 + bb2
            return (acc + we[:, None] * y, None)
        out, _ = jax.lax.scan(step, jnp.zeros_like(xf), (W1, b1, W2, b2, cw.T))
        return out.reshape(Bb, Tt, Dd)

    def _L1_gnn_ref(x, hyperedge_index, hyperedge_weight, c1_w1, c1_b1, c1_w2, c1_b2, c1_g, c1_b, bn1_g, bn1_b, c2_w1, c2_b1, c2_w2, c2_b2, c2_g, c2_b, bn2_g, bn2_b):
        import jax, jax.numpy as jnp
        import numpy as np
        EPS = 1e-05

        def _bn(x, gamma, beta):
            m = jnp.mean(x, axis=0)
            v = jnp.mean((x - m) ** 2, axis=0)
            return gamma * (x - m) * jax.lax.rsqrt(v + EPS) + beta

        def _hconv(x, src, dst, ew, w1, b1, w2, b2, g, b):
            h = jax.nn.relu(x @ w1 + b1)
            msg = ew[:, None] * h[src]
            agg = jax.ops.segment_sum(msg, dst, num_segments=x.shape[0])
            h = agg @ w2 + b2
            return jax.nn.relu(_bn(h, g, b))
        src, dst = (hyperedge_index[0], hyperedge_index[1])
        residual = x
        h = _hconv(x, src, dst, hyperedge_weight, c1_w1, c1_b1, c1_w2, c1_b2, c1_g, c1_b)
        h = jax.nn.relu(_bn(h, bn1_g, bn1_b))
        h = _hconv(h, src, dst, hyperedge_weight, c2_w1, c2_b1, c2_w2, c2_b2, c2_g, c2_b)
        h = _bn(h, bn2_g, bn2_b)
        return jax.nn.relu(h + residual)

    def _L1_mix_ref(x, W_qkv, W_out, b_out):
        import jax, jax.numpy as jnp
        import numpy as np
        HEADS = 4
        DIM_HEAD = 32
        B, L, D = x.shape
        scale = DIM_HEAD ** (-0.5)
        qkv = jnp.einsum('bld,df->blf', x, W_qkv)
        qkv = qkv.reshape(B, L, 3, HEADS, DIM_HEAD)
        q = jnp.transpose(qkv[:, :, 0], (0, 2, 1, 3)) * scale
        k = jax.nn.softmax(jnp.transpose(qkv[:, :, 1], (0, 2, 1, 3)), axis=2)
        v = jnp.transpose(qkv[:, :, 2], (0, 2, 1, 3))
        context = jnp.einsum('bhld,bhle->bhde', k, v)
        out = jnp.einsum('bhde,bhld->bhle', context, q)
        out = jnp.transpose(out, (0, 2, 1, 3)).reshape(B, L, HEADS * DIM_HEAD)
        return jnp.einsum('blf,fd->bld', out, W_out) + b_out

    def _L1_ffn_ref(x, Wg, bg, bias, W1, b1, W2, b2):
        import jax, jax.numpy as jnp
        import numpy as np
        D_MODEL = 256
        EXPERT_DIM = 512
        NUM_EXPERTS = 8
        TOP_K = 2
        SEQ_LEN = 128
        BATCH = 2
        x_flat = x.reshape(-1, D_MODEL)
        gate_logits = x_flat @ Wg + bg + bias
        topk_vals, topk_idx = jax.lax.top_k(gate_logits, TOP_K)
        topk_w = jax.nn.softmax(topk_vals, axis=-1)
        combine = (jax.nn.one_hot(topk_idx, NUM_EXPERTS, dtype=x.dtype) * topk_w[..., None]).sum(axis=1)
        h = jax.nn.relu(jnp.einsum('td,edh->teh', x_flat, W1) + b1)
        y = jnp.einsum('teh,ehd->ted', h, W2) + b2
        out = jnp.einsum('ted,te->td', y, combine)
        return out.reshape(x.shape)

    def _L2_gnn_ref(x, edge_index, W, att_src, att_dst, bias, gamma, beta):
        import jax, jax.numpy as jnp
        import numpy as np
        N, E = (3125, 50000)
        IN, H, C = (256, 8, 32)
        NEG_SLOPE = 0.2
        EPS = 1e-05
        n = x.shape[0]
        xl = (x @ W).reshape(n, H, C)
        a_src = jnp.einsum('nhc,hc->nh', xl, att_src)
        a_dst = jnp.einsum('nhc,hc->nh', xl, att_dst)
        loops = jnp.arange(n, dtype=edge_index.dtype)
        src = jnp.concatenate([edge_index[0], loops])
        dst = jnp.concatenate([edge_index[1], loops])
        logits = jax.nn.leaky_relu(a_src[src] + a_dst[dst], NEG_SLOPE)
        seg_max = jax.ops.segment_max(logits, dst, num_segments=n)
        ex = jnp.exp(logits - seg_max[dst])
        denom = jax.ops.segment_sum(ex, dst, num_segments=n)
        alpha = ex / denom[dst]
        msgs = xl[src] * alpha[:, :, None]
        out = jax.ops.segment_sum(msgs, dst, num_segments=n).reshape(n, H * C) + bias
        mu = jnp.mean(out, axis=-1, keepdims=True)
        var = jnp.var(out, axis=-1, keepdims=True)
        return (out - mu) / jnp.sqrt(var + EPS) * gamma + beta

    def _L2_mix_ref(x, W_qkv, b_qkv, W_out, b_out):
        import math
        import jax, jax.numpy as jnp
        import numpy as np
        EPS_DIV = 1e-07
        EPS_NORM = 1e-12

        def _l2_normalize(x, axis):
            n = jnp.sqrt(jnp.sum(x * x, axis=axis, keepdims=True))
            return x / jnp.maximum(n, EPS_NORM)
        b, N, C = x.shape
        qkv = x @ W_qkv + b_qkv
        q, k, v = jnp.split(qkv, 3, axis=2)
        q = q - jnp.mean(q, axis=2, keepdims=True)
        k = k - jnp.mean(k, axis=2, keepdims=True)
        q2 = q * q
        k2 = k * k
        q2s = jnp.sum(q2, axis=2, keepdims=True)
        k2s = jnp.sum(k2, axis=2, keepdims=True)
        k2 = _l2_normalize(k2 / (k2s + EPS_DIV), axis=-2)
        q2 = _l2_normalize(q2 / (q2s + EPS_DIV), axis=-1)
        kv = jnp.einsum('bnc,bnd->bcd', k2, v)
        t2 = jnp.einsum('bnc,bcd->bnd', q2, kv) / math.sqrt(N)
        attn = v + t2
        return attn @ W_out + b_out

    def _L2_ffn_ref(x, attention_mask, wr, br, w1, b1, w2, b2):
        import jax, jax.numpy as jnp
        import numpy as np
        B, S, D = (8, 256, 256)
        H = 4 * D
        CAPACITY = 0.5
        b, s, d = x.shape
        weights = (jnp.einsum('bsd,do->bso', x, wr) + br)[..., 0]
        k = max(1, int(CAPACITY * s))
        kk = k - 1 if k > 1 else 1
        _, idx = jax.lax.top_k(weights, k)
        sel_idx = idx[:, :kk]
        sel = jnp.take_along_axis(x, sel_idx[:, :, None], axis=1)
        h = jax.nn.gelu(jnp.einsum('bkd,dh->bkh', sel, w1) + b1)
        y = jnp.einsum('bkh,hd->bkd', h, w2) + b2
        w_sel = jnp.take_along_axis(weights, sel_idx, axis=1)
        y = y * w_sel[..., None]
        batch_idx = jnp.arange(b)[:, None]
        processed = jnp.zeros_like(x).at[batch_idx, sel_idx].set(y)
        return processed + x

    def _L3_gnn_ref(x, W1, b1, W2, b2, W3, b3, edge_index):
        import jax, jax.numpy as jnp
        import numpy as np
        N_NODES = 625
        N_EDGES = 10000
        IN_DIM, HID_DIM, OUT_DIM = (256, 512, 256)

        def gcn_conv(x, W, b, src, dst, dinv):
            h = x @ W
            norm = dinv[src] * dinv[dst]
            msg = h[src] * norm[:, None]
            agg = jnp.zeros_like(h).at[dst].add(msg)
            agg = agg + h * (dinv * dinv)[:, None]
            return agg + b
        src, dst = (edge_index[0], edge_index[1])
        n = x.shape[0]
        deg = jnp.zeros((n,), x.dtype).at[dst].add(1.0) + 1.0
        dinv = jax.lax.rsqrt(deg)
        h = jnp.tanh(gcn_conv(x, W1, b1, src, dst, dinv))
        h = jnp.tanh(gcn_conv(h, W2, b2, src, dst, dinv))
        out = gcn_conv(h, W3, b3, src, dst, dinv)
        return out

    def _L3_mix_ref(seq, wq, wk, wv, wo, bo, ln_k_g, ln_k_b, ln_v_g, ln_v_b):
        import jax, jax.numpy as jnp
        import numpy as np
        import math
        EMBED = 256
        HEADS = 4
        HEAD_DIM = EMBED // HEADS
        OUT_DIM = 256
        LN_EPS = 1e-05

        def _qkv_init(key):
            spread = math.sqrt(3.0 / EMBED)
            gain, delta = (0.01, 0.01)
            w = jax.random.uniform(key, (EMBED, EMBED), minval=-spread, maxval=spread) * gain
            return w + delta * jnp.eye(EMBED, dtype=w.dtype)

        def _layer_norm(x, g, b):
            mu = jnp.mean(x, axis=-1, keepdims=True)
            var = jnp.mean(jnp.square(x - mu), axis=-1, keepdims=True)
            return (x - mu) * jax.lax.rsqrt(var + LN_EPS) * g + b

        def _split_heads(x, B, S):
            return x.reshape(B, S, HEADS, HEAD_DIM).transpose(0, 2, 1, 3)
        B, S, _ = seq.shape
        q = _split_heads(seq @ wq.T, B, S)
        k = _split_heads(seq @ wk.T, B, S)
        v = _split_heads(seq @ wv.T, B, S)
        k = _layer_norm(k, ln_k_g, ln_k_b)
        v = _layer_norm(v, ln_v_g, ln_v_b)
        kv = jnp.einsum('bhsd,bhse->bhde', k, v) / S
        ga = jnp.einsum('bhsd,bhde->bhse', q, kv)
        ga = ga.transpose(0, 2, 1, 3).reshape(B, S, EMBED)
        return ga @ wo.T + bo

    def _L3_ffn_ref(x, Wr, br, ln_g, ln_b, W1, b1, W2, b2):
        import jax, jax.numpy as jnp
        import numpy as np
        TOP_K = 2
        LN_EPS = 1e-05
        B, S, D = x.shape
        N = B * S
        xt = x.reshape(N, D)
        logits = xt @ Wr + br
        probs = jax.nn.softmax(logits, axis=-1)
        top_p, top_idx = jax.lax.top_k(probs, TOP_K)
        weights = top_p / top_p.sum(axis=-1, keepdims=True)
        mu = xt.mean(axis=-1, keepdims=True)
        var = ((xt - mu) ** 2).mean(axis=-1, keepdims=True)
        xn = (xt - mu) * jax.lax.rsqrt(var + LN_EPS)
        xe = xn[None, :, :] * ln_g[:, None, :] + ln_b[:, None, :]
        h = jax.nn.gelu(jnp.einsum('end,edh->enh', xe, W1) + b1[:, None, :], approximate=False)
        y = jnp.einsum('enh,ehd->end', h, W2) + b2[:, None, :]
        y_tok = jnp.transpose(y, (1, 0, 2))
        sel = jnp.take_along_axis(y_tok, top_idx[:, :, None], axis=1)
        out = (weights[:, :, None] * sel).sum(axis=1)
        return out.reshape(B, S, D)
    edge_index = jnp.stack([src, dst])
    xn = _layernorm(x, axis=-1)
    x = x + _L0_gnn_ref(xn, edge_index, L0_gnn_W, L0_gnn_att_src, L0_gnn_att_dst, L0_gnn_bias, L0_gnn_gamma, L0_gnn_beta) + _L0_mix_ref(xn[None], L0_mix_w_qkv, L0_mix_b_qkv, L0_mix_kln_g, L0_mix_kln_b, L0_mix_vln_g, L0_mix_vln_b, L0_mix_w1, L0_mix_b1, L0_mix_w2, L0_mix_b2)[0]
    x = x + _L0_ffn_ref(_layernorm(x, axis=-1)[None], L0_ffn_gate_w, L0_ffn_gate_b, L0_ffn_W1, L0_ffn_b1, L0_ffn_W2, L0_ffn_b2)[0]
    xn = _layernorm(x, axis=-1)
    x = x + _L1_gnn_ref(xn, edge_index, edge_weight, L1_gnn_c1_w1, L1_gnn_c1_b1, L1_gnn_c1_w2, L1_gnn_c1_b2, L1_gnn_c1_g, L1_gnn_c1_b, L1_gnn_bn1_g, L1_gnn_bn1_b, L1_gnn_c2_w1, L1_gnn_c2_b1, L1_gnn_c2_w2, L1_gnn_c2_b2, L1_gnn_c2_g, L1_gnn_c2_b, L1_gnn_bn2_g, L1_gnn_bn2_b) + _L1_mix_ref(xn[None], L1_mix_W_qkv, L1_mix_W_out, L1_mix_b_out)[0]
    x = x + _L1_ffn_ref(_layernorm(x, axis=-1)[None], L1_ffn_Wg, L1_ffn_bg, L1_ffn_bias, L1_ffn_W1, L1_ffn_b1, L1_ffn_W2, L1_ffn_b2)[0]
    xn = _layernorm(x, axis=-1)
    x = x + _L2_gnn_ref(xn, edge_index, L2_gnn_W, L2_gnn_att_src, L2_gnn_att_dst, L2_gnn_bias, L2_gnn_gamma, L2_gnn_beta) + _L2_mix_ref(xn[None], L2_mix_W_qkv, L2_mix_b_qkv, L2_mix_W_out, L2_mix_b_out)[0]
    x = x + _L2_ffn_ref(_layernorm(x, axis=-1)[None], L2_ffn_attention_mask, L2_ffn_wr, L2_ffn_br, L2_ffn_w1, L2_ffn_b1, L2_ffn_w2, L2_ffn_b2)[0]
    xn = _layernorm(x, axis=-1)
    x = x + _L3_gnn_ref(xn, L3_gnn_W1, L3_gnn_b1, L3_gnn_W2, L3_gnn_b2, L3_gnn_W3, L3_gnn_b3, edge_index) + _L3_mix_ref(xn[None], L3_mix_wq, L3_mix_wk, L3_mix_wv, L3_mix_wo, L3_mix_bo, L3_mix_ln_k_g, L3_mix_ln_k_b, L3_mix_ln_v_g, L3_mix_ln_v_b)[0]
    x = x + _L3_ffn_ref(_layernorm(x, axis=-1)[None], L3_ffn_Wr, L3_ffn_br, L3_ffn_ln_g, L3_ffn_ln_b, L3_ffn_W1, L3_ffn_b1, L3_ffn_W2, L3_ffn_b2)[0]
    return x

_drawn_inputs = setup_inputs


def setup_inputs(seed=0):
    import zlib

    import numpy as np

    out = dict(_drawn_inputs(seed))
    spreads = {'L0_gnn_bias': (0.0, 0.1),
     'L0_gnn_gamma': (1.0, 0.2),
     'L0_gnn_beta': (0.0, 0.1),
     'L0_mix_b_qkv': (0.0, 0.1),
     'L0_mix_kln_g': (1.0, 0.6),
     'L0_mix_kln_b': (0.0, 0.484),
     'L0_mix_vln_g': (1.0, 0.6),
     'L0_mix_vln_b': (0.0, 0.429),
     'L0_mix_b1': (0.0, 0.1),
     'L0_mix_b2': (0.0, 0.1),
     'L0_ffn_gate_b': (0.0, 0.717),
     'L0_ffn_b1': (0.0, 0.8),
     'L0_ffn_b2': (0.0, 0.431),
     'L1_gnn_c1_b1': (0.0, 0.1),
     'L1_gnn_c1_b2': (0.0, 2.0),
     'L1_gnn_c1_g': (1.0, 0.6),
     'L1_gnn_c1_b': (0.0, 0.381),
     'L1_gnn_bn1_g': (1.0, 0.2),
     'L1_gnn_bn1_b': (0.0, 0.269),
     'L1_gnn_c2_b1': (0.0, 0.1),
     'L1_gnn_c2_b2': (0.0, 2.0),
     'L1_gnn_c2_g': (1.0, 0.6),
     'L1_gnn_c2_b': (0.0, 0.334),
     'L1_gnn_bn2_g': (1.0, 0.2),
     'L1_gnn_bn2_b': (0.0, 0.1),
     'L1_mix_b_out': (0.0, 0.1),
     'L1_ffn_bias': (0.0, 0.674),
     'L2_gnn_bias': (0.0, 0.1),
     'L2_gnn_gamma': (1.0, 0.2),
     'L2_gnn_beta': (0.0, 0.271),
     'L2_ffn_b1': (0.0, 0.8),
     'L2_ffn_b2': (0.0, 0.8),
     'L3_gnn_b1': (0.0, 1.523),
     'L3_gnn_b2': (0.0, 1.309),
     'L3_gnn_b3': (0.0, 1.284),
     'L3_mix_ln_k_g': (1.0, 0.6),
     'L3_mix_ln_k_b': (0.0, 0.8),
     'L3_mix_ln_v_g': (1.0, 0.6),
     'L3_mix_ln_v_b': (0.0, 0.8),
     'L3_ffn_br': (0.0, 1.826),
     'L3_ffn_ln_g': (1.0, 0.6),
     'L3_ffn_ln_b': (0.0, 2.0),
     'L3_ffn_b1': (0.0, 2.0),
     'L3_ffn_b2': (0.0, 1.645)}
    factors = {'L0_ffn_gate_w': 4.816,
     'L0_ffn_W1': 6.136,
     'L0_ffn_W2': 5.393,
     'L1_ffn_Wg': 2.794,
     'L1_ffn_bg': 8.0,
     'L1_ffn_W1': 2.852,
     'L1_ffn_b1': 8.0,
     'L1_ffn_b2': 6.387,
     'L2_mix_b_out': 8.0,
     'L2_ffn_wr': 5.605,
     'L2_ffn_w1': 8.0,
     'L2_ffn_w2': 8.0,
     'L3_mix_wq': 8.0,
     'L3_mix_wk': 8.0,
     'L3_mix_wv': 7.379,
     'L3_mix_wo': 6.501,
     'L3_mix_bo': 24.459}
    for name, (base, spread) in spreads.items():
        noise = np.random.default_rng([zlib.crc32(name.encode()), seed]).standard_normal(out[name].shape)
        drawn = base * np.exp(spread * noise) if base else spread * noise
        out[name] = jnp.asarray(drawn.astype(out[name].dtype))
    for name, factor in factors.items():
        out[name] = (out[name] * factor).astype(out[name].dtype)
    return out
```

```python
import numpy as np
import concourse.bass as bass
from concourse import mybir
from contextlib import ExitStack

F32 = mybir.dt.float32
BF16 = mybir.dt.bfloat16
U16 = mybir.dt.uint16
I32 = mybir.dt.int32
ALU = mybir.AluOpType
ACT = mybir.ActivationFunctionType
AX = mybir.AxisListType.X

N, D, E = 3125, 256, 50000
P, T = 125, 25
CH = [(c * 500, 500 if c < 6 else 125) for c in range(7)]
NB, NQ = 100, 4
BIG = 1e30
WORDS = 51200


class Queue:

    def __init__(self, new_sem, name):
        self.new_sem, self.name = new_sem, name
        self.items, self.seen = [], {}
        self.turn()

    def turn(self):
        self.sem, self.count, self.last = self.new_sem(), 0, None

    def wait(self, *tokens):
        for t in tokens:
            if t is None:
                continue
            if isinstance(t, list):
                self.wait(*t)
                continue
            sem, value = t
            if self.seen.get(id(sem), 0) < value:
                self.seen[id(sem)] = value
                self.items.append((None, sem, value))

    def __call__(self, fn, *tokens, inc=True):
        self.wait(*tokens)
        if not inc:
            self.items.append((fn, None, 0))
            return None
        if self.count >= 30000:
            self.turn()
        self.count += 1
        self.items.append((fn, self.sem, 1))
        self.last = (self.sem, self.count)
        return self.last

    def emit(self, eng):
        for fn, sem, value in self.items:
            if fn is None:
                eng.wait_ge(sem, value)
            else:
                ins = fn(eng)
                if sem is not None:
                    ins.then_inc(sem, value)


def program(nc, inp, out, stop=None):
    dram = {}
    ctx = ExitStack()
    nsem = [0]

    def new_sem():
        nsem[0] += 1
        return ctx.enter_context(nc.semaphore(f"s{nsem[0]}"))

    pe, act, dve, pool, sp = (Queue(new_sem, n) for n in ("pe", "act", "dve", "pool", "sp"))
    engines = [pe, act, dve, pool, sp]
    channels = {}
    once = []

    def dma(eng, dst, src, ch, *tokens, make=None):
        if ch is None:
            once.append(dma(eng, dst, src, "once%d" % len(once), *tokens, make=make))
            return list(once)
        if ch not in channels:
            channels[ch] = [new_sem(), 0]
        c = channels[ch]
        if c[1] >= 30000:
            c[0], c[1] = new_sem(), 0
        eng.wait(*tokens)
        c[1] += 16
        eng.items.append((make or (lambda e: e.dma_start(dst, src)), c[0], 16))
        return (c[0], c[1])

    def load(dst, src, ch, *tokens):
        return dma(sp, dst, src, ch, *tokens)

    def barrier():
        marks = [e.last for e in engines] + [(c[0], c[1]) for c in channels.values() if c[1]]
        for e in engines:
            e.wait(*marks)
        for i in range(8):
            free[i] = None
        once.clear()

    arena = ctx.enter_context(nc.sbuf_tensor("arena", [128, WORDS], F32))
    banks = [ctx.enter_context(nc.psum_tensor(f"bank{i}", [128, 512], F32)) for i in range(8)]
    free = [None] * 8

    def at(off, *dims, p=P, dt=F32):
        n = int(np.prod(dims))
        words = n if dt in (F32, I32) else (n + 1) // 2
        assert off + words <= WORDS, (off, words)
        v = arena[0:p, off:off + words]
        if dt != F32:
            v = v.bitcast(dt)
            v = v[:, 0:n]
        if len(dims) == 2:
            v = v.rearrange("p (a b) -> p a b", a=dims[0])
        elif len(dims) == 3:
            v = v.rearrange("p (a b c) -> p a b c", a=dims[0], b=dims[1])
        return v

    def rows(v, n):
        return v.rearrange("(t p) f -> p t f", p=n)

    ring = [0]

    def bank(pool_of=(0, 8)):
        ring[0] += 1
        i = pool_of[0] + ring[0] % (pool_of[1] - pool_of[0])
        return i

    X0, XN0, S0 = 0, 6400, 12800
    K0 = 49700
    X = at(X0, T, D)
    XN = at(XN0, T, D)
    ident = at(K0, 128, p=128)
    ones = at(K0 + 128, 128, p=128)
    iota8 = at(K0 + 256, 8)
    bmask32 = at(K0 + 264, 128, p=128)
    bmask64 = at(K0 + 392, 128, p=128)
    tri = at(K0 + 520, 125)
    SM = K0 + 645
    st6 = at(SM, T, 6)
    mv = at(SM + 150, T, 2)
    rs = at(SM + 200, T)
    rs2 = at(SM + 225, T)
    PV = SM + 250

    def dd(name, shape, dt=F32):
        return nc.dram_tensor(name, shape, dt, kind="Internal").ap()

    G = dd("G", [N * N + 500, 2])
    C16 = dd("C16", [N, N], U16)
    WT = dd("WT", [N, N])
    MK = dd("MK", [N, N], BF16)
    KEY = dd("KEY", [1, E])
    DEG = dd("DEG", [1, N])
    ROW = dd("ROW", [24 * T, P])

    pm = pool(lambda e: e.memset(ident, 0.0))
    pm1 = pool(lambda e: e.memset(ones, 1.0))
    t_id = pool(lambda e: e.affine_select(out=ident, in_=ident, compare_op=ALU.not_equal, fill=1.0, base=0,
                                          pattern=[[-1, 128]], channel_multiplier=1), pm)
    t_tri = pool(lambda e: e.affine_select(out=tri, in_=ones[0:P, 0:P], compare_op=ALU.is_gt, fill=0.0, base=0,
                                           pattern=[[-1, P]], channel_multiplier=1), pm1)
    for e8 in range(8):
        pool(lambda e, e8=e8: e.memset(iota8[:, e8:e8 + 1], float(8 - e8)))

    def block_mask(m, c):
        a = pool(lambda e: e.memset(m, 1.0))
        v = m.rearrange("p (b c) -> p b c", c=c)
        a = pool(lambda e: e.affine_select(out=v, in_=v, compare_op=ALU.is_ge, fill=0.0, base=0,
                                           pattern=[[-c, 128 // c], [0, c]], channel_multiplier=1), a)
        return pool(lambda e: e.affine_select(out=v, in_=v, compare_op=ALU.is_ge, fill=0.0, base=c - 1,
                                              pattern=[[c, 128 // c], [0, c]], channel_multiplier=-1), a)

    block_mask(bmask32, 32)
    block_mask(bmask64, 64)
    load(X, rows(inp["x"], P), "x")
    barrier()

    def evac(i, fn_act, fn_dve, *tokens):
        return act(fn_act, *tokens) if i % 2 else dve(fn_dve, *tokens)

    def copy_out(i, dst, src, *tokens):
        return evac(i, lambda e: e.activation(dst, src, ACT.Copy), lambda e: e.tensor_copy(dst, src), *tokens)

    def bcast(v, n, k=1):
        s = list(v.shape)
        return v.unsqueeze(k).broadcast_to(s[:k] + [n] + s[k:])

    def param_n(name, off, w=D):
        dst = at(off, w)
        src = inp[name] if len(inp[name].shape) == 1 else inp[name].rearrange("a b -> (a b)")
        return dst, load(dst, src.partition_broadcast(P), None)

    def param_t(name, off, k=2, src=None):
        dst = at(off, k, p=128)
        src = inp[name] if src is None else src
        return dst, dma(sp, dst, None, None, make=lambda e: e.dma_start(
            dst, src.rearrange("(k p) -> p k", p=128), allow_slow_non_contiguous=True))

    def weight(name, off, k, f, src=None, ch=None, tokens=()):
        dst = at(off, k, f, p=128)
        src = inp[name] if src is None else src
        return dst, load(dst, src.rearrange("(k p) f -> p k f", p=128), ch, *tokens)

    def rstd(var, dst, tmp, *tokens, eps=1e-5):
        a = dve(lambda e: e.tensor_scalar(tmp, var, eps, None, ALU.add), *tokens)
        b = act(lambda e: e.activation(dst, tmp, ACT.Sqrt), a)
        return dve(lambda e: e.reciprocal(dst, dst), b)

    def norm_tiles(src, dst, *tokens):
        dve.wait(*tokens)
        for t in range(T):
            a = dve(lambda e, t=t: e.bn_stats(st6[:, t, :], src[:, t, :]))
        dve.wait(a)
        for t in range(T):
            a = dve(lambda e, t=t: e.bn_aggr(mv[:, t, :], st6[:, t, :]))
        r = rstd(mv[:, :, 1], rs, rs2, a)
        dve.wait(r)
        return [dve(lambda e, t=t: e.tensor_scalar(dst[:, t, :], src[:, t, :], mv[:, t, 0:1], rs[:, t:t + 1],
                                                   ALU.subtract, ALU.mult)) for t in range(T)]

    def to_T(src, dst, ready, k=2):
        last = []
        n = 0
        for c, (n0, w) in enumerate(CH):
            for kk in range(k):
                b = bank()
                m = w // P
                for i in range(m):
                    t = n0 // P + i
                    a = pe(lambda e, t=t, i=i, b=b, kk=kk: e.transpose(
                        banks[b][:, i * P:(i + 1) * P], src[:, t, kk * 128:(kk + 1) * 128], ident[0:P, 0:P]),
                        free[b], ready[t] if isinstance(ready, list) else ready, inc=(i == m - 1))
                free[b] = copy_out(n, dst[:, kk, n0:n0 + w], banks[b][:, 0:w], a)
                last.append(free[b])
                n += 1
        return last[-2:]

    def add_from_T(src, k, n0, w, *tokens):
        for i in range(w // P):
            t = n0 // P + i
            b = bank()
            for kk in range(k):
                a = pe(lambda e, kk=kk, i=i, b=b: e.transpose(
                    banks[b][0:P, kk * 128:(kk + 1) * 128], src[:, kk, i * P:(i + 1) * P], ident[:, :]),
                    free[b], *tokens, inc=(kk == k - 1))
            free[b] = dve(lambda e, t=t, b=b: e.tensor_tensor(X[:, t, :], banks[b][0:P, 0:D], X[:, t, :], ALU.add), a)
        return a

    def lin_N(srcT, k, W, f, sink, *tokens, f0=0):
        out_t = []
        for t in range(T):
            b = bank()
            for kk in range(k):
                a = pe(lambda e, t=t, kk=kk, b=b: e.matmul(
                    banks[b][0:P, 0:f], srcT[:, kk, t * P:(t + 1) * P], W[:, kk, f0:f0 + f],
                    start=(kk == 0), stop=(kk == k - 1)), free[b], *tokens, inc=(kk == k - 1))
            free[b] = sink(t, banks[b][0:P, 0:f], a)
            out_t.append(free[b])
        return out_t

    def lin_T(W, srcT, k, o, sink, *tokens, chunks=CH, base=0):
        last = []
        for n0, w in chunks:
            for oo in range(o):
                b = bank()
                for kk in range(k):
                    a = pe(lambda e, kk=kk, b=b, oo=oo, n0=n0, w=w: e.matmul(
                        banks[b][:, 0:w], W[:, kk, oo * 128:(oo + 1) * 128], srcT[:, kk, n0 - base:n0 - base + w],
                        start=(kk == 0), stop=(kk == k - 1)), free[b], *tokens, inc=(kk == k - 1))
                free[b] = sink(oo, n0, w, banks[b][:, 0:w], a)
                last.append(free[b])
        return last[-4:]

    def head_norm(v, tmp, sm, heads, g, bb, *tokens):
        c = D // heads
        n = T * heads
        s1, s2, s3 = (at(sm + i * n, n) for i in range(3))
        vv = v.rearrange("p t (h c) -> p (t h) c", c=c)
        tt = tmp.rearrange("p t (h c) -> p (t h) c", c=c)
        a = dve(lambda e: e.tensor_reduce(s1, vv, AX, ALU.add), *tokens)
        a = dve(lambda e: e.tensor_scalar(s1, s1, 1.0 / c, None, ALU.mult), a)
        a = dve(lambda e: e.tensor_tensor(vv, vv, bcast(s1, c, 2), ALU.subtract), a)
        a = act(lambda e: e.activation(tmp, v, ACT.Square), a)
        a = dve(lambda e: e.tensor_reduce(s2, tt, AX, ALU.add), a)
        a = dve(lambda e: e.tensor_scalar(s2, s2, 1.0 / c, 1e-5, ALU.mult, ALU.add), a)
        a = act(lambda e: e.activation(s3, s2, ACT.Sqrt), a)
        a = dve(lambda e: e.reciprocal(s3, s3), a)
        a = dve(lambda e: e.tensor_tensor(vv, vv, bcast(s3, c, 2), ALU.mult), a)
        a = dve(lambda e: e.tensor_tensor(vv, vv, bcast(g, n), ALU.mult), a)
        return dve(lambda e: e.tensor_tensor(vv, vv, bcast(bb, n), ALU.add), a)

    def rows_out(src, m, row0, tmp_off, ch, *tokens):
        b = bank()
        tmp = at(tmp_off, P, p=m)
        a = pe(lambda e: e.transpose(banks[b][0:m, 0:P], src, ident[0:P, 0:P]), free[b], *tokens)
        free[b] = dve(lambda e: e.tensor_copy(tmp, banks[b][0:m, 0:P]), a)
        return load(ROW[row0:row0 + m, :], tmp, ch, free[b])

    def row_bcast(dst, row0, n0, w, ch, *tokens):
        src = ROW[row0:row0 + T, :].rearrange("t p -> (t p)")[n0:n0 + w]
        return load(dst, src.partition_broadcast(P), ch, *tokens)

    def graph():
        zero = at(S0, 6250)
        z = dve(lambda e: e.memset(zero, 0.0))
        gz = G[0:N * N, :].rearrange("(s p n) c -> s p (n c)", p=P, n=N)
        for s in range(T):
            zt = dma(sp if s % 2 else act, gz[s], zero, "gz%d" % (s % 2), z)
        load(G[N * N:N * N + 500, :].rearrange("(p n) c -> p (n c)", p=P), zero[:, 0:8], "gz1", z)
        b0 = S0 + 6250
        si, di, sf, df = (at(b0 + i * 500, 500, p=NB, dt=I32 if i < 2 else F32) for i in range(4))
        a = load(si, inp["src"].rearrange("(b j) -> b j", b=NB), "ed")
        a = load(di, inp["dst"].rearrange("(b j) -> b j", b=NB), "ed")
        c1 = dve(lambda e: e.tensor_copy(sf, si), a)
        c2 = dve(lambda e: e.tensor_copy(df, di))
        c3 = dve(lambda e: e.scalar_tensor_tensor(out=sf, in0=sf, scalar=float(N), in1=df, op0=ALU.mult,
                                                  op1=ALU.add), c2)
        kd = load(KEY.rearrange("o (b j) -> (o b) j", b=NB), sf, "key", c3)
        b1 = b0 + 2000
        K = at(b1, NQ, NB)
        CT = at(b1 + 400, NQ, NB)
        IDF = at(b1 + 800, NQ, NB)
        IDX = at(b1 + 1200, NQ, NB, dt=I32)
        LD = at(b1 + 1600, NQ, NB)
        DM = at(b1 + 2000, NQ)
        DMI = at(b1 + 2004, NQ, dt=I32)
        VAL = at(b1 + 2010, NQ * NB * 2)
        val = VAL.rearrange("p (q b c) -> p q b c", q=NQ, c=2)
        TR = at(b1 + 2810, NQ, 500)
        b2 = b1 + 4810
        KR = [at(b2 + i * 2500, 5, 500) for i in range(2)]
        WR = [at(b2 + 5000 + i * 2500, 5, 500) for i in range(2)]
        JK = [at(b2 + 10000 + i * 500, 500) for i in range(2)]
        p1 = pool(lambda e: e.iota(DMI, pattern=[[P, NQ]], base=N * N, channel_multiplier=1))
        dm = dve(lambda e: e.tensor_copy(DM, DMI), p1)
        p2 = pool(lambda e: e.memset(TR, 1025.0))
        trt = pool(lambda e: e.affine_select(out=TR, in_=TR, compare_op=ALU.is_gt, fill=1.0, base=0,
                                             pattern=[[P, NQ], [-1, 500]], channel_multiplier=1), p2)
        kt = None
        for q in range(NQ):
            b = bank()
            a = pe(lambda e, q=q, b=b: e.transpose(banks[b][0:P, 0:NB], sf[:, q * P:(q + 1) * P],
                                                   ident[0:NB, 0:NB]), c3)
            kt = dve(lambda e, q=q, b=b: e.tensor_copy(K[:, q, :], banks[b][0:P, 0:NB]), a)
        dve.wait(kt, trt, dm)
        used = [None, None]
        chain = [channels["gz0"], channels["gz1"]]
        chain = [(c[0], c[1]) for c in chain]
        jt = [None, None]
        for g in range(NB // 5):
            i = g % 2
            l1 = load(KR[i], KEY[0, g * 2500:(g + 1) * 2500].rearrange("(b j) -> b j", b=5).partition_broadcast(P),
                      "kr%d" % i, kd, used[i])
            l2 = load(WR[i], inp["edge_weight"][g * 2500:(g + 1) * 2500].rearrange("(b j) -> b j", b=5)
                      .partition_broadcast(P), "kr%d" % i)
            dve.wait(l2)
            for bb in range(5):
                b = g * 5 + bb
                for q in range(NQ):
                    a1 = dve(lambda e, i=i, bb=bb, b=b, q=q: e.scalar_tensor_tensor(
                        out=JK[0], in0=KR[i][:, bb, :], scalar=K[:, q, b:b + 1], in1=TR[:, q, :],
                        op0=ALU.is_equal, op1=ALU.mult, accum_out=CT[:, q, b:b + 1]), jt[0])
                    jt[0] = a1
                    a2 = dve(lambda e, i=i, bb=bb, b=b, q=q: e.scalar_tensor_tensor(
                        out=JK[1], in0=KR[i][:, bb, :], scalar=K[:, q, b:b + 1], in1=WR[i][:, bb, :],
                        op0=ALU.is_equal, op1=ALU.mult, accum_out=val[:, q, b, 1:2]), jt[1])
                    jt[1] = a2
            used[i] = a2
            bs = slice(g * 5, g * 5 + 5)
            a = dve(lambda e, bs=bs: e.tensor_scalar(LD[:, :, bs], CT[:, :, bs], 1024.0, None, ALU.is_lt), a2)
            a = dve(lambda e, bs=bs: e.tensor_copy(val[:, :, bs, 0], CT[:, :, bs]))
            a = dve(lambda e, bs=bs: e.tensor_tensor(IDF[:, :, bs], K[:, :, bs], bcast(DM, 5, 2), ALU.subtract))
            a = dve(lambda e, bs=bs: e.tensor_tensor(IDF[:, :, bs], IDF[:, :, bs], LD[:, :, bs], ALU.mult), a)
            a = dve(lambda e, bs=bs: e.tensor_tensor(IDF[:, :, bs], IDF[:, :, bs], bcast(DM, 5, 2), ALU.add), a)
            a = dve(lambda e, bs=bs: e.tensor_copy(IDX[:, :, bs], IDF[:, :, bs]), a)
            for bb in range(5):
                b = g * 5 + bb
                for q in range(NQ):
                    t = dma(pool, None, None, "sc", a, chain, make=lambda e, q=q, b=b: e.indirect_dma_start(
                        out=G[:, :], out_offset=bass.IndirectOffsetOnAxis(ap=IDX[:, q, b:b + 1], axis=0),
                        in_=val[:, q, b, :], in_offset=None, compute_op=ALU.add))
                chain = t
        barrier()
        o = S0
        GT = [at(o + i * 6250, N, 2) for i in range(2)]
        o += 12500
        CO = [at(o + i * 1563, N, dt=U16) for i in range(2)]
        o += 3126
        WO = [at(o + i * 3125, N) for i in range(2)]
        o += 6250
        MB = [at(o + i * 1563, N, dt=BF16) for i in range(2)]
        o += 3126
        idb = at(o, 126, dt=BF16)
        o += 63
        MS = at(o, T, 625, dt=BF16)
        o += 7813
        assert o <= K0
        ib = dve(lambda e: e.tensor_copy(idb[:, 0:P], ident[0:P, 0:P]))
        gt = G[0:N * N, :].rearrange("(s p n) c -> s p n c", p=P, n=N)
        gfree = [None, None]
        cw = [None, None]
        ww = [None, None]
        mused = [None, None]
        msw = None
        tb = banks[7]
        tbv = tb[0:P, :].bitcast(BF16)
        for s in range(T):
            i = s % 2
            l = load(GT[i], gt[s], "gt%d" % i, gfree[i])
            d = dve(lambda e, i=i, s=s: e.tensor_tensor(GT[i][:, s * P:(s + 1) * P, 0], GT[i][:, s * P:(s + 1) * P, 0],
                                                        ident[0:P, 0:P], ALU.add), l)
            c = act(lambda e, i=i: e.activation(CO[i], GT[i][:, :, 0], ACT.Copy), d, cw[i])
            w = act(lambda e, i=i: e.activation(WO[i], GT[i][:, :, 1], ACT.Copy), ww[i])
            m = dve(lambda e, i=i: e.tensor_scalar(MB[i], GT[i][:, :, 0], 1.0, None, ALU.min), d, mused[i])
            cw[i] = load(C16[s * P:(s + 1) * P, :], CO[i], "co%d" % i, c)
            ww[i] = load(WT[s * P:(s + 1) * P, :], WO[i], "wo%d" % i, w)
            for cc, (n0, wd) in enumerate(CH):
                a = pe(lambda e, cc=cc, n0=n0, wd=wd, i=i, s=s: e.matmul(
                    banks[cc][:, 0:wd], ones[0:P, :], GT[i][:, n0:n0 + wd, 0], start=(s == 0), stop=(s == T - 1)),
                    d)
            gfree[i] = [a, m, w, c]
            for j0 in range(0, T, 8):
                nj = min(8, T - j0)
                for j in range(nj):
                    a = pe(lambda e, j=j, j0=j0, i=i: e.transpose(
                        tbv[:, j * 128:j * 128 + P], MB[i][:, (j0 + j) * P:(j0 + j + 1) * P], idb[:, 0:P]),
                        m, ib, free[7], inc=(j == nj - 1))
                sl = s % 5
                free[7] = dve(lambda e, j0=j0, nj=nj, sl=sl: e.tensor_scalar(
                    MS[:, j0:j0 + nj, sl * P:(sl + 1) * P],
                    tbv[:, 0:nj * 128].rearrange("p (j c) -> p j c", c=128)[:, :, 0:P],
                    -1.0, BIG, ALU.add, ALU.mult), a, msw if sl == 0 else None)
            mused[i] = a
            if s % 5 == 4:
                msw = load(MK[:, (s - 4) * P:(s + 1) * P].rearrange("(j p) c -> p j c", p=P), MS, "ms", free[7])
        dr = WO[0]
        for cc, (n0, wd) in enumerate(CH):
            a = dve(lambda e, cc=cc, n0=n0, wd=wd: e.tensor_copy(dr[0:1, n0:n0 + wd], banks[cc][0:1, 0:wd]),
                    pe.last, ww[0])
        load(DEG, dr[0:1, :], "deg", a)
        barrier()

    def gat(pre, H, C, eps, XT):
        R0 = S0
        H1o, OUTo = S0 + 8000, S0 + 14600
        B0 = S0 + 21000
        S1 = S0 + 33500
        CW = C + 1
        h1 = at(H1o, T, H, CW) if True else None
        outN = at(OUTo, T, D)
        W, tw = weight(pre + "_W", B0, 2, D)
        ats, ta = param_n(pre + "_att_src", B0 + 512)
        atd, ta = param_n(pre + "_att_dst", B0 + 768)
        asN, as2, adN, mx, u, m, r1, r2 = (at(S1 + i * 200, H, T) for i in range(8))
        one = pool(lambda e: e.memset(h1[:, :, :, C], 1.0))

        def sink(t, ps, a):
            return evac(t, lambda e: e.activation(h1[:, t, :, 0:C], ps.rearrange("p (h c) -> p h c", c=C), ACT.Copy),
                        lambda e: e.tensor_copy(h1[:, t, :, 0:C], ps.rearrange("p (h c) -> p h c", c=C)), a)

        ts = lin_N(XT, 2, W, D, sink, tw)
        tmp = outN.rearrange("p t (h c) -> p t h c", c=C)
        a = None
        for att, dst in ((ats, asN), (atd, adN)):
            for h in range(H):
                a = dve(lambda e, att=att, h=h: e.tensor_tensor(
                    tmp[:, :, h, :], h1[:, :, h, 0:C], bcast(att[:, h * C:(h + 1) * C], T), ALU.mult), ts, ta, a)
            a = dve(lambda e, dst=dst: e.tensor_reduce(dst.rearrange("p h t -> p t h"), tmp, AX, ALU.add), a)
        a = dve(lambda e: e.tensor_scalar(as2, asN, 0.2, None, ALU.mult), a)
        for g in range(H // 4):
            fl = asN[:, 4 * g:4 * g + 4, :].rearrange("p h t -> p (h t)")
            ro = rows_out(fl, 100, 100 * g, B0 + 1024 + 125 * g, "ro", a)
        barrier()
        asr = at(B0, 4, N)
        jk = at(R0, N)
        ml = [at(R0 + 3125 + i * 1563, N, dt=BF16) for i in range(2)]
        for g in range(H // 4):
            for h in range(4):
                l = row_bcast(asr[:, h, :], 100 * g + 25 * h, 0, N, "asr", a if g else None)
            mu = [None, None]
            for j in range(T):
                i = j % 2
                lm = load(ml[i], MK[j * P:(j + 1) * P, :], "mk%d" % i, mu[i])
                for h in range(4):
                    a = dve(lambda e, i=i, h=h, g=g, j=j: e.tensor_tensor_reduce(
                        out=jk, in0=ml[i], in1=asr[:, h, :], scale=1.0, scalar=-3e38, op0=ALU.add, op1=ALU.max,
                        accum_out=mx[:, 4 * g + h, j:j + 1]), lm, l, a)
                mu[i] = a
        a = dve(lambda e: e.tensor_tensor(u, mx, adN, ALU.add), a)
        a = dve(lambda e: e.scalar_tensor_tensor(out=m, in0=u, scalar=0.2, in1=u, op0=ALU.mult, op1=ALU.max), a)
        a = dve(lambda e: e.tensor_tensor(r1, adN, m, ALU.subtract), a)
        a = dve(lambda e: e.scalar_tensor_tensor(out=r2, in0=adN, scalar=0.2, in1=m, op0=ALU.mult, op1=ALU.subtract), a)
        for g in range(H // 4):
            for k, r in enumerate((r1, r2)):
                fl = r[:, 4 * g:4 * g + 4, :].rearrange("p h t -> p (h t)")
                rows_out(fl, 100, 200 * g + 100 * k, B0 + 125 * (2 * g + k), "ro", a)
        barrier()
        Rb = [at(R0 + i * 4000, 2, 4, 500) for i in range(2)]
        Cb = [at(B0 + i * 1250, 5, 500, dt=U16) for i in range(2)]
        Tb = [at(B0 + 2500 + i * 2000, 4, 500) for i in range(2)]
        Xb = [at(B0 + 6500 + i * 2000, 4, 500) for i in range(2)]
        AC = at(B0 + 10500, 4, 500, p=128)
        rused = [None, None]
        cused = [None, None]
        xused = [None, None]
        tused = [None, None]
        acused = None
        nr = nc_ = it = 0
        rc = S1 + 1600
        rcp = at(rc, 4)
        c16v = C16.rearrange("(s p) d -> p s d", p=P)
        for g in range(H // 4):
            for n0, w in CH:
                i = nr % 2
                nr += 1
                for k in range(2):
                    for h in range(4):
                        lr = row_bcast(Rb[i][:, k, h, 0:w], 200 * g + 100 * k + 25 * h, n0, w, "rb%d" % i, rused[i])
                for s in range(T):
                    if s % 5 == 0:
                        ci = nc_ % 2
                        nc_ += 1
                        lc = load(Cb[ci][:, :, 0:w], c16v[:, s:s + 5, n0:n0 + w], "cb%d" % ci, cused[ci])
                    j = it % 2
                    it += 1
                    tt = None
                    for h in range(4):
                        tt = act(lambda e, j=j, i=i, h=h, s=s, w=w, g=g: e.activation(
                            Tb[j][:, h, 0:w], Rb[i][:, 1, h, 0:w], ACT.Identity,
                            bias=as2[:, 4 * g + h, s:s + 1]), lr, tused[j])
                    for h in range(4):
                        x = dve(lambda e, j=j, i=i, h=h, s=s, w=w, g=g: e.scalar_tensor_tensor(
                            out=Xb[j][:, h, 0:w], in0=Rb[i][:, 0, h, 0:w], scalar=asN[:, 4 * g + h, s:s + 1],
                            in1=Tb[j][:, h, 0:w], op0=ALU.add, op1=ALU.max), tt, lr, xused[j])
                    tused[j] = x
                    ex = act(lambda e, j=j, w=w: e.activation(Xb[j][:, :, 0:w], Xb[j][:, :, 0:w], ACT.Exp), x)
                    pr = dve(lambda e, j=j, ci=ci, s=s, w=w: e.tensor_tensor(
                        Xb[j][:, :, 0:w], Xb[j][:, :, 0:w], bcast(Cb[ci][:, s % 5, 0:w], 4), ALU.mult), ex, lc)
                    for h in range(4):
                        a = pe(lambda e, j=j, h=h, s=s, w=w, g=g: e.matmul(
                            banks[h][0:CW, 0:w], h1[:, s, 4 * g + h, :], Xb[j][:, h, 0:w],
                            start=(s == 0), stop=(s == T - 1)), pr, free[h])
                    xused[j] = a
                    cused[ci] = pr
                rused[i] = [x, tt]
                for h in range(4):
                    free[h] = copy_out(h, AC[0:CW, h, 0:w], banks[h][0:CW, 0:w], a, acused)
                cp = [free[2], free[3]]
                for k in range(w // P):
                    t = n0 // P + k
                    b = bank((4, 8))
                    for h in range(4):
                        a = pe(lambda e, h=h, k=k, b=b: e.transpose(
                            banks[b][0:P, h * CW:(h + 1) * CW], AC[0:CW, h, k * P:(k + 1) * P],
                            ident[0:CW, 0:CW]), cp, free[b], inc=(h == 3))
                    v = banks[b][0:P, 0:4 * CW].rearrange("p (h c) -> p h c", c=CW)
                    z = dve(lambda e, v=v: e.tensor_scalar(rcp, v[:, :, C], eps, None, ALU.add), a, dve.last)
                    z = dve(lambda e: e.reciprocal(rcp, rcp), z)
                    o = outN[:, t, 4 * g * C:4 * (g + 1) * C].rearrange("p (h c) -> p h c", c=C)
                    free[b] = dve(lambda e, v=v, o=o: e.tensor_tensor(
                        o, v[:, :, 0:C], bcast(rcp, C, 2), ALU.mult), z)
                acused = a
        barrier()
        bi, t1 = param_n(pre + "_bias", B0)
        ga, t1 = param_n(pre + "_gamma", B0 + 256)
        be, t1 = param_n(pre + "_beta", B0 + 512)
        a = dve(lambda e: e.tensor_tensor(outN, outN, bcast(bi, T), ALU.add), t1)
        nt = norm_tiles(outN, outN, a)
        a = dve(lambda e: e.tensor_tensor(outN, outN, bcast(ga, T), ALU.mult), nt)
        a = dve(lambda e: e.tensor_tensor(outN, outN, bcast(be, T), ALU.add), a)
        dve(lambda e: e.tensor_tensor(X, X, outN, ALU.add), a)
        barrier()

    def mix_ln(XT, Wq, bq, Wk, bk, Wv, bv, gk, bk2, gv, bv2, heads, tail):
        A0 = S0 + 6250
        kN, vN, tm = (at(A0 + i * 6400, T, D) for i in range(3))
        o = A0 + 19200
        c = D // heads
        mask = bmask32 if c == 32 else bmask64
        wq, tq = weight(Wq, o, 2, D)
        wk, tk = weight(Wk, o + 512, 2, D)
        wv, tv = weight(Wv, o + 1024, 2, D)
        o += 1536
        small = o
        o += 600
        prm = []
        for nme in (gk, bk2, gv, bv2):
            v, t1 = param_n(nme, o, c)
            prm.append(v)
            o += c
        bkn = bvn = bqt = None
        if bq is not None:
            bkn, t1 = param_n(bk, o)
            bvn, t1 = param_n(bv, o + 256)
            bqt, t1 = param_t(bq, o + 512)
        o += 520
        kvs = at(o, 2, 128, p=128)
        o += 256

        def sink_for(dst, bn):
            def sink(t, ps, a):
                if bn is not None:
                    return dve(lambda e: e.tensor_tensor(dst[:, t, :], ps, bn, ALU.add), a, t1)
                return copy_out(t, dst[:, t, :], ps, a)
            return sink

        tk2 = lin_N(XT, 2, wk, D, sink_for(kN, bkn), tk, tv)
        tv2 = lin_N(XT, 2, wv, D, sink_for(vN, bvn), tv)
        a = head_norm(kN, tm, small, heads, prm[0], prm[1], tk2, t1)
        a = head_norm(vN, tm, small, heads, prm[2], prm[3], tv2, a)
        bk_ = [bank(), bank()]
        for k in range(2):
            b = bk_[k]
            for t in range(T):
                m = pe(lambda e, b=b, k=k, t=t: e.matmul(
                    banks[b][:, 0:128], kN[:, t, k * 128:(k + 1) * 128], vN[:, t, k * 128:(k + 1) * 128],
                    start=(t == 0), stop=(t == T - 1)), a, free[b], inc=(t == T - 1))
            free[b] = dve(lambda e, b=b, k=k: e.scalar_tensor_tensor(
                out=kvs[:, k, :], in0=banks[b][:, 0:128], scalar=1.0 / N, in1=mask, op0=ALU.mult, op1=ALU.mult), m)
        kt = free[bk_[1]]
        qc = [at(A0 + i * 1000, 2, 500, p=128) for i in range(2)]
        qused = [None, None]
        for ci, (n0, w) in enumerate(CH):
            i = ci % 2
            ql = []
            for oo in range(2):
                b = bank()
                for kk in range(2):
                    a = pe(lambda e, b=b, oo=oo, kk=kk, n0=n0, w=w: e.matmul(
                        banks[b][:, 0:w], wq[:, kk, oo * 128:(oo + 1) * 128], XT[:, kk, n0:n0 + w],
                        start=(kk == 0), stop=(kk == 1)), free[b], tq, inc=(kk == 1))
                if bqt is not None:
                    free[b] = act(lambda e, b=b, oo=oo, i=i, w=w: e.activation(
                        qc[i][:, oo, 0:w], banks[b][:, 0:w], ACT.Identity, bias=bqt[:, oo:oo + 1]), a, kt, qused[i])
                else:
                    free[b] = act(lambda e, b=b, oo=oo, i=i, w=w: e.activation(
                        qc[i][:, oo, 0:w], banks[b][:, 0:w], ACT.Copy), a, kt, qused[i])
                ql.append(free[b])
            qused[i] = tail(ci, n0, w, qc[i], kvs, ql, o)
        barrier()

    def l0_mix(XT):
        w1, t1 = weight("L0_mix_w1", S0 + 30000, 2, D)
        w2, t1 = weight("L0_mix_w2", S0 + 30512, 2, D)
        b1, t1 = param_t("L0_mix_b1", S0 + 31024)
        b2, t2 = param_n("L0_mix_b2", S0 + 31040)
        rc = [at(S0 + 31300 + i * 1000, 2, 500, p=128) for i in range(2)]
        hc = [at(S0 + 33300 + i * 1000, 2, 500, p=128) for i in range(2)]
        rused = [None, None]
        hused = [None, None]

        def tail(ci, n0, w, q, kvs, ql, o):
            assert o <= S0 + 30000
            i = ci % 2
            rl = []
            for k in range(2):
                b = bank()
                a = pe(lambda e, b=b, k=k: e.matmul(banks[b][:, 0:w], kvs[:, k, :], q[:, k, 0:w], start=True,
                                                    stop=True), free[b], ql)
                free[b] = dve(lambda e, b=b, k=k: e.tensor_tensor(rc[i][:, k, 0:w], banks[b][:, 0:w],
                                                                  XT[:, k, n0:n0 + w], ALU.add), a, rused[i])
                rl.append(free[b])
            done = a
            hl = []
            for oo in range(2):
                b = bank()
                for k in range(2):
                    a = pe(lambda e, b=b, k=k, oo=oo: e.matmul(
                        banks[b][:, 0:w], w1[:, k, oo * 128:(oo + 1) * 128], rc[i][:, k, 0:w],
                        start=(k == 0), stop=(k == 1)), free[b], rl, t1, inc=(k == 1))
                free[b] = act(lambda e, b=b, oo=oo: e.activation(
                    hc[i][:, oo, 0:w], banks[b][:, 0:w], ACT.Gelu, bias=b1[:, oo:oo + 1]), a, t2, hused[i])
                hl.append(free[b])
            rused[i] = a
            for j in range(w // P):
                t = n0 // P + j
                b = bank()
                for k in range(2):
                    a = pe(lambda e, b=b, k=k, j=j: e.matmul(
                        banks[b][0:P, 0:D], hc[i][:, k, j * P:(j + 1) * P], w2[:, k, :],
                        start=(k == 0), stop=(k == 1)), free[b], hl, inc=(k == 1))
                free[b] = dve(lambda e, b=b, t=t: e.tensor_tensor(X[:, t, :], banks[b][0:P, 0:D], X[:, t, :],
                                                                  ALU.add), a)
            hused[i] = a
            return done

        a = dve(lambda e: e.tensor_tensor(X, X, XN, ALU.add))
        a = dve(lambda e: e.tensor_tensor(X, X, bcast(b2, T), ALU.add), a, t2)
        dve.wait(a)
        mix_ln(XT, "wq0", "bq0", "wk0", "bk0", "wv0", "bv0", "L0_mix_kln_g", "L0_mix_kln_b",
               "L0_mix_vln_g", "L0_mix_vln_b", 8, tail)

    def l3_mix(XT):
        wo, t1 = weight("woT", S0 + 30000, 2, D)
        bo, t2 = param_n("L3_mix_bo", S0 + 31040)
        rc = [at(S0 + 31300 + i * 1000, 2, 500, p=128) for i in range(2)]
        rused = [None, None]

        def tail(ci, n0, w, q, kvs, ql, o):
            assert o <= S0 + 30000
            i = ci % 2
            rl = []
            for k in range(2):
                b = bank()
                a = pe(lambda e, b=b, k=k: e.matmul(banks[b][:, 0:w], kvs[:, k, :], q[:, k, 0:w], start=True,
                                                    stop=True), free[b], ql)
                free[b] = dve(lambda e, b=b, k=k: e.tensor_copy(rc[i][:, k, 0:w], banks[b][:, 0:w]), a, rused[i])
                rl.append(free[b])
            done = a
            for j in range(w // P):
                t = n0 // P + j
                b = bank()
                for k in range(2):
                    a = pe(lambda e, b=b, k=k, j=j: e.matmul(
                        banks[b][0:P, 0:D], rc[i][:, k, j * P:(j + 1) * P], wo[:, k, :],
                        start=(k == 0), stop=(k == 1)), free[b], rl, t1, inc=(k == 1))
                free[b] = dve(lambda e, b=b, t=t: e.tensor_tensor(X[:, t, :], banks[b][0:P, 0:D], X[:, t, :],
                                                                  ALU.add), a)
            rused[i] = a
            return done

        a = dve(lambda e: e.tensor_tensor(X, X, bcast(bo, T), ALU.add), t2)
        dve.wait(a)
        mix_ln(XT, "wqT", None, "wkT", None, "wvT", None, "L3_mix_ln_k_g", "L3_mix_ln_k_b",
               "L3_mix_ln_v_g", "L3_mix_ln_v_b", 4, tail)

    def l1_mix(XT):
        o = S0 + 6250
        W, tw = weight("L1_mix_W_qkv", o, 2, 384)
        o += 768
        Wo = at(o, D, p=128)
        tw = load(Wo, inp["L1_mix_W_out"], None)
        o += 256
        bo, tb = param_n("L1_mix_b_out", o)
        o += 256
        kT = at(o, N, p=128)
        o += 3125
        kN = at(o, T, 128)
        o += 3200
        vN = at(o, T, 128)
        o += 3200
        ctx_ = at(o, 128, p=128)
        o += 128
        sm = at(o, 8, p=128)
        o += 8
        qc = [at(o + i * 500, 500, p=128) for i in range(2)]
        o += 1000
        oc = [at(o + i * 500, 500, p=128) for i in range(2)]
        o += 1000
        assert o <= K0
        a = dve(lambda e: e.tensor_tensor(X, X, bcast(bo, T), ALU.add), tb)
        dve.wait(a)
        last = []
        for ci, (n0, w) in enumerate(CH):
            b = bank()
            for kk in range(2):
                a = pe(lambda e, b=b, kk=kk, n0=n0, w=w: e.matmul(
                    banks[b][:, 0:w], W[:, kk, 128:256], XT[:, kk, n0:n0 + w], start=(kk == 0), stop=(kk == 1)),
                    free[b], tw, inc=(kk == 1))
            free[b] = copy_out(ci, kT[:, n0:n0 + w], banks[b][:, 0:w], a)
            last.append(free[b])
        a = dve(lambda e: e.tensor_reduce(sm[:, 0:1], kT, AX, ALU.max, negate=True), last)
        ek = act(lambda e: e.activation(kT, kT, ACT.Exp, bias=sm[:, 0:1], accum_out=sm[:, 1:2]), a)
        rr = dve(lambda e: e.reciprocal(sm[:, 2:3], sm[:, 1:2]), ek)
        rr = dve(lambda e: e.tensor_scalar(sm[:, 2:3], sm[:, 2:3], 32.0 ** -0.5, None, ALU.mult), rr)

        def sinkv(t, ps, a):
            return copy_out(t, vN[:, t, :], ps, a)

        tv = lin_N(XT, 2, W, 128, sinkv, tw, f0=256)
        tk = []
        for t in range(T):
            b = bank()
            a = pe(lambda e, t=t, b=b: e.transpose(banks[b][0:P, 0:128], kT[:, t * P:(t + 1) * P], ident[:, :]),
                   ek, free[b])
            free[b] = copy_out(t, kN[:, t, :], banks[b][0:P, 0:128], a)
            tk.append(free[b])
        b = bank()
        for t in range(T):
            a = pe(lambda e, t=t, b=b: e.matmul(banks[b][:, 0:128], kN[:, t, :], vN[:, t, :], start=(t == 0),
                                                stop=(t == T - 1)), free[b], tk, tv, inc=(t == T - 1))
        free[b] = dve(lambda e, b=b: e.scalar_tensor_tensor(
            out=ctx_, in0=banks[b][:, 0:128], scalar=sm[:, 2:3], in1=bmask32, op0=ALU.mult, op1=ALU.mult), a, rr)
        ct = free[b]
        qu, ou = [None, None], [None, None]
        for ci, (n0, w) in enumerate(CH):
            i = ci % 2
            b = bank()
            for kk in range(2):
                a = pe(lambda e, b=b, kk=kk, n0=n0, w=w: e.matmul(
                    banks[b][:, 0:w], W[:, kk, 0:128], XT[:, kk, n0:n0 + w], start=(kk == 0), stop=(kk == 1)),
                    free[b], inc=(kk == 1))
            free[b] = q1 = act(lambda e, b=b, i=i, w=w: e.activation(qc[i][:, 0:w], banks[b][:, 0:w], ACT.Copy), a, qu[i])
            b = bank()
            a = pe(lambda e, b=b, i=i, w=w: e.matmul(banks[b][:, 0:w], ctx_, qc[i][:, 0:w], start=True, stop=True),
                   q1, ct, free[b])
            qu[i] = a
            free[b] = o1 = act(lambda e, b=b, i=i, w=w: e.activation(oc[i][:, 0:w], banks[b][:, 0:w], ACT.Copy), a, ou[i])
            for j in range(w // P):
                t = n0 // P + j
                b = bank()
                a = pe(lambda e, b=b, i=i, j=j: e.matmul(banks[b][0:P, 0:D], oc[i][:, j * P:(j + 1) * P], Wo,
                                                         start=True, stop=True), o1, free[b])
                free[b] = dve(lambda e, b=b, t=t: e.tensor_tensor(X[:, t, :], banks[b][0:P, 0:D], X[:, t, :],
                                                                  ALU.add), a)
            ou[i] = a
        barrier()

    def l2_mix(XT):
        o = S0 + 6250
        W, tw = weight("L2_mix_W_qkv", o, 2, 768)
        o += 1536
        Wo, tw = weight("L2_mix_W_out", o, 2, D)
        o += 512
        bqkv = at(o, 768)
        load(bqkv, inp["L2_mix_b_qkv"].partition_broadcast(P), None)
        o += 768
        bo, tb = param_n("L2_mix_b_out", o)
        o += 256
        bvt, tb = param_t("L2_mix_b_qkv", o, src=inp["L2_mix_b_qkv"][512:768])
        o += 2
        kN, vN = (at(o + i * 6400, T, D) for i in range(2))
        o += 12800
        q2T = at(o, 2, N, p=128)
        o += 6250
        kv = at(o, 2, D, p=128)
        o += 512
        cn = at(o, 8, p=128)
        o += 8
        sm = [at(o + i * 25, T) for i in range(6)]
        o += 150
        sq = at(o, 2, D)
        o += 512
        assert o <= K0 - 2000, o
        vc = [at(o + i * 1000, 2, 500, p=128) for i in range(2)]
        a = dve(lambda e: e.tensor_tensor(X, X, bcast(bo, T), ALU.add), tb)
        dve.wait(a)

        def sink_for(dst, f):
            def sink(t, ps, a):
                return dve(lambda e: e.tensor_tensor(dst[:, t, :], ps, bqkv[:, f:f + D], ALU.add), a, tb)
            return sink

        def squares(v, ready):
            vf = v
            a = dve(lambda e: e.tensor_reduce(sm[0], vf, AX, ALU.add), ready)
            a = dve(lambda e: e.tensor_scalar(sm[0], sm[0], 1.0 / D, None, ALU.mult), a)
            a = dve(lambda e: e.tensor_tensor(vf, vf, bcast(sm[0], D, 2), ALU.subtract), a)
            a = act(lambda e: e.activation(vf, vf, ACT.Square), a)
            a = dve(lambda e: e.tensor_reduce(sm[1], vf, AX, ALU.add), a)
            a = dve(lambda e: e.tensor_scalar(sm[1], sm[1], 1e-7, None, ALU.add), a)
            a = dve(lambda e: e.reciprocal(sm[1], sm[1]), a)
            return dve(lambda e: e.tensor_tensor(vf, vf, bcast(sm[1], D, 2), ALU.mult), a)

        tq = lin_N(XT, 2, W, D, sink_for(vN, 0), tw, f0=0)
        a = squares(vN, tq)
        for t in range(T):
            a = dve(lambda e, t=t: e.scalar_tensor_tensor(out=sq[:, 0, :], in0=vN[:, t, :], scalar=1.0,
                                                          in1=vN[:, t, :], op0=ALU.mult, op1=ALU.mult,
                                                          accum_out=sm[2][:, t:t + 1]), a)
        a = act(lambda e: e.activation(sm[3], sm[2], ACT.Sqrt), a)
        a = dve(lambda e: e.tensor_scalar(sm[3], sm[3], 1e-12, None, ALU.max), a)
        a = dve(lambda e: e.reciprocal(sm[3], sm[3]), a)
        a = dve(lambda e: e.tensor_tensor(vN, vN, bcast(sm[3], D, 2), ALU.mult), a)
        qt = to_T(vN, q2T, a)
        tk = lin_N(XT, 2, W, D, sink_for(kN, D), f0=D)
        ka = squares(kN, [tk, a])
        dve.wait(qt, pe.last)
        tv = lin_N(XT, 2, W, D, sink_for(vN, 2 * D), f0=2 * D)
        b0, b1, b2 = bank(), bank(), bank()
        su = [None, None]
        for t in range(T):
            i = t % 2
            s_ = dve(lambda e, t=t, i=i: e.tensor_tensor(sq[:, i, :], kN[:, t, :], kN[:, t, :], ALU.mult), ka, su[i])
            for k in range(2):
                a = pe(lambda e, k=k, t=t, b=(b0, b1)[k]: e.matmul(banks[b][:, 0:D], kN[:, t, k * 128:(k + 1) * 128],
                                                                 vN[:, t, :], start=(t == 0), stop=(t == T - 1)),
                       ka, tv, free[(b0, b1)[k]])
            a = pe(lambda e, t=t, i=i: e.matmul(banks[b2][0:1, 0:D], ones[0:P, 0:1], sq[:, i, :], start=(t == 0),
                                                stop=(t == T - 1)), s_, free[b2])
            su[i] = a
        rowt = sq[0:1, 0, :]
        r = dve(lambda e: e.tensor_copy(rowt, banks[b2][0:1, 0:D]), a)
        free[b2] = r
        b3 = bank()
        for k in range(2):
            a = pe(lambda e, k=k: e.matmul(banks[b3][:, k:k + 1], sq[0:1, 0, k * 128:(k + 1) * 128], ones[0:1, 0:1],
                                           start=True, stop=True), r, free[b3])
        r = dve(lambda e: e.tensor_copy(cn[:, 0:2], banks[b3][:, 0:2]), a)
        free[b3] = r
        r = act(lambda e: e.activation(cn[:, 0:2], cn[:, 0:2], ACT.Sqrt), r)
        r = dve(lambda e: e.tensor_scalar(cn[:, 0:2], cn[:, 0:2], 1e-12, None, ALU.max), r)
        r = dve(lambda e: e.reciprocal(cn[:, 2:4], cn[:, 0:2]), r)
        r = dve(lambda e: e.tensor_scalar(cn[:, 4:6], cn[:, 2:4], float(N) ** -0.5, None, ALU.mult), r)
        for k, b in enumerate((b0, b1)):
            free[b] = r = dve(lambda e, k=k, b=b: e.tensor_scalar(kv[:, k, :], banks[b][:, 0:D], cn[:, 4 + k:5 + k],
                                                                  None, ALU.mult), r, a)
        vu = [None, None]
        for ci, (n0, w) in enumerate(CH):
            i = ci % 2
            al = []
            for oo in range(2):
                b = bank()
                for kk in range(4):
                    lhs = (kv[:, kk, oo * 128:(oo + 1) * 128] if kk < 2
                           else W[:, kk - 2, 512 + oo * 128:512 + (oo + 1) * 128])
                    rhs = q2T[:, kk, n0:n0 + w] if kk < 2 else XT[:, kk - 2, n0:n0 + w]
                    a = pe(lambda e, b=b, lhs=lhs, rhs=rhs, kk=kk, w=w: e.matmul(
                        banks[b][:, 0:w], lhs, rhs, start=(kk == 0), stop=(kk == 3)), free[b], r, qt, inc=(kk == 3))
                free[b] = act(lambda e, b=b, oo=oo, i=i, w=w: e.activation(
                    vc[i][:, oo, 0:w], banks[b][:, 0:w], ACT.Identity, bias=bvt[:, oo:oo + 1]), a, vu[i])
                al.append(free[b])
            for j in range(w // P):
                t = n0 // P + j
                b = bank()
                for k in range(2):
                    a = pe(lambda e, b=b, k=k, j=j, i=i: e.matmul(
                        banks[b][0:P, 0:D], vc[i][:, k, j * P:(j + 1) * P], Wo[:, k, :],
                        start=(k == 0), stop=(k == 1)), free[b], al, inc=(k == 1))
                free[b] = dve(lambda e, b=b, t=t: e.tensor_tensor(X[:, t, :], banks[b][0:P, 0:D], X[:, t, :],
                                                                  ALU.add), a)
            vu[i] = a
        barrier()

    def top2(V, o):
        m1, eq, x1, o1, V2, sel = at(o, T), at(o + 25, T, 8), at(o + 225, T), at(o + 250, T, 8), at(o + 450, T, 8), \
            at(o + 650, T, 8)
        w8 = bcast(iota8, T)
        a = dve.last
        src = V
        for r in range(2):
            dst = sel if r == 0 else o1
            mm_ = m1 if r == 0 else x1
            a = dve(lambda e, src=src, mm_=mm_: e.tensor_reduce(mm_, src, AX, ALU.max), a)
            a = dve(lambda e, src=src, mm_=mm_: e.tensor_tensor(eq, src, bcast(mm_, 8, 2), ALU.is_equal), a)
            a = dve(lambda e: e.tensor_tensor(eq, eq, w8, ALU.mult), a)
            a = dve(lambda e: e.tensor_reduce(x1, eq, AX, ALU.max), a)
            a = dve(lambda e, dst=dst: e.tensor_tensor(dst, eq, bcast(x1, 8, 2), ALU.is_equal), a)
            if r == 0:
                a = dve(lambda e: e.scalar_tensor_tensor(out=V2, in0=sel, scalar=-3e38, in1=V, op0=ALU.mult,
                                                         op1=ALU.add), a)
                src = V2
        a = dve(lambda e: e.tensor_tensor(sel, sel, o1, ALU.add), a)
        return sel, m1, a

    def gate(XT, Wg, biases, kind, o, L, cw):
        W = at(o, 2, 8, p=128)
        t0 = dma(sp, None, None, None, make=lambda e: e.dma_start(
            W, inp[Wg].rearrange("(k p) f -> p k f", p=128)))
        bs = []
        for i, nme in enumerate(biases):
            v, t0 = param_n(nme, o + 16 + 8 * i, 8)
            bs.append(v)
        b = bank()
        for t in range(T):
            for k in range(2):
                a = pe(lambda e, t=t, k=k: e.matmul(banks[b][0:P, t * 8:t * 8 + 8], XT[:, k, t * P:(t + 1) * P],
                                                    W[:, k, :], start=(k == 0), stop=(k == 1)), t0, free[b],
                       inc=(k == 1 and t == T - 1))
        ps = banks[b][0:P, 0:200].rearrange("p (t e) -> p t e", e=8)
        for i, v in enumerate(bs):
            a = dve(lambda e, i=i, v=v: e.tensor_tensor(L, ps if i == 0 else L, bcast(v, T), ALU.add), a)
            if i == 0:
                free[b] = a
        w0 = o + 64
        mx, s = at(w0, T), at(w0 + 25, T)
        if kind != "two":
            a = dve(lambda e: e.tensor_reduce(mx, L, AX, ALU.max), a)
            a = dve(lambda e: e.tensor_tensor(L, L, bcast(mx, 8, 2), ALU.subtract), a)
            a = act(lambda e: e.activation(L, L, ACT.Exp), a)
            a = dve(lambda e: e.tensor_reduce(s, L, AX, ALU.add), a)
            a = dve(lambda e: e.reciprocal(s, s), a)
            a = dve(lambda e: e.tensor_tensor(L, L, bcast(s, 8, 2), ALU.mult), a)
            sel, m1, a = top2(L, w0 + 50)
            a = dve(lambda e: e.tensor_tensor(cw, L, sel, ALU.mult), a)
        else:
            sel, m1, a = top2(L, w0 + 50)
            a = dve(lambda e: e.tensor_tensor(L, L, bcast(m1, 8, 2), ALU.subtract), a)
            a = act(lambda e: e.activation(L, L, ACT.Exp), a)
            a = dve(lambda e: e.tensor_tensor(cw, L, sel, ALU.mult), a)
        if kind != "all":
            a = dve(lambda e: e.tensor_reduce(s, cw, AX, ALU.add), a)
            a = dve(lambda e: e.reciprocal(s, s), a)
            a = dve(lambda e: e.tensor_tensor(cw, cw, bcast(s, 8, 2), ALU.mult), a)
        return a

    def ffn(XT, pre, hid, fn, kind, Wg, biases, affine=None, again=False):
        hp = hid // 128
        o = S0 + 6250
        L, cw = at(o, T, 8), at(o + 200, T, 8)
        small = o + 400
        b1a = at(o + 1400, 8, hp, p=128)
        b2a = at(o + 1464, D, p=8)
        o += 1720
        lg = lb = None
        if affine:
            lg, lb = at(o, 8, 2, p=128), at(o + 16, 8, 2, p=128)
            o += 32
            XE = [at(o + i * 1000, 2, 500, p=128) for i in range(2)]
            o += 2000
        cT = [at(o + i * 125, P, p=8) for i in range(2)]
        o += 250
        wsz = 2 * hid + hp * D
        W1 = [at(o + i * wsz, 2, hid, p=128) for i in range(2)]
        W2 = [at(o + i * wsz + 2 * hid, hp, D, p=128) for i in range(2)]
        o += 2 * wsz
        Hb = [at(o + i * hp * 500, hp, 500, p=128) for i in range(2)]
        o += 2 * hp * 500
        assert o <= K0, o
        used = [None, None]

        def get(e8):
            i = e8 % 2
            load(W1[i], inp[pre + "_W1"][e8].rearrange("(k p) f -> p k f", p=128), "w%d" % i, used[i])
            return load(W2[i], inp[pre + "_W2"][e8].rearrange("(k p) f -> p k f", p=128), "w%d" % i)

        tw = [get(0), get(1)]
        dma(sp, None, None, None, make=lambda e: e.dma_start(
            b1a, inp[pre + "_b1"].rearrange("e (k p) -> p e k", p=128), allow_slow_non_contiguous=True))
        if affine:
            for v, nme in ((lg, affine[0]), (lb, affine[1])):
                dma(sp, None, None, None, make=lambda e, v=v, nme=nme: e.dma_start(
                    v, inp[nme].rearrange("e (k p) -> p e k", p=128), allow_slow_non_contiguous=True))
        tb = load(b2a, inp[pre + "_b2"], None)
        g = gate(XT, Wg, biases, kind, small, L, cw)
        tt = to_T(XN, XT, norm_tiles(XN, XN, g)) if again else None
        cu = [None, None]
        for t in range(T):
            i = t % 2
            b = bank()
            a = pe(lambda e, t=t, b=b: e.transpose(banks[b][0:8, 0:P], cw[:, t, :], ident[0:P, 0:P]), g, free[b])
            free[b] = c = act(lambda e, b=b, i=i: e.activation(cT[i], banks[b][0:8, 0:P], ACT.Copy), a, cu[i])
            b = bank()
            a = pe(lambda e, b=b, i=i: e.matmul(banks[b][0:P, 0:D], cT[i], b2a, start=True, stop=True), c, tb, free[b])
            cu[i] = a
            free[b] = dve(lambda e, b=b, t=t: e.tensor_tensor(X[:, t, :], banks[b][0:P, 0:D], X[:, t, :], ALU.add), a)
        xt_done = {}
        hu = [None, None]
        xu = [None, None]
        it = 0
        for e8 in range(8):
            w1, w2 = W1[e8 % 2], W2[e8 % 2]
            for ci, (n0, w) in enumerate(CH):
                i = it % 2
                it += 1
                if affine:
                    xl = []
                    for k in range(2):
                        xl.append(dve(lambda e, k=k, i=i, e8=e8, n0=n0, w=w: e.tensor_scalar(
                            XE[i][:, k, 0:w], XT[:, k, n0:n0 + w], lg[:, e8, k:k + 1], lb[:, e8, k:k + 1],
                            ALU.mult, ALU.add), tb, tt, xu[i]))
                    src, off = XE[i], 0
                else:
                    xl, src, off = None, XT, n0
                hl = []
                for oo in range(hp):
                    b = bank()
                    for kk in range(2):
                        a = pe(lambda e, b=b, oo=oo, kk=kk, w1=w1, src=src, off=off, w=w: e.matmul(
                            banks[b][:, 0:w], w1[:, kk, oo * 128:(oo + 1) * 128], src[:, kk, off:off + w],
                            start=(kk == 0), stop=(kk == 1)), free[b], tw[e8], xl, inc=(kk == 1))
                    free[b] = act(lambda e, b=b, oo=oo, i=i, e8=e8, w=w: e.activation(
                        Hb[i][:, oo, 0:w], banks[b][:, 0:w], fn, bias=b1a[:, e8, oo:oo + 1]), a, tb, hu[i])
                    hl.append(free[b])
                xu[i] = a
                for j in range(w // P):
                    t = n0 // P + j
                    b = bank()
                    for kk in range(hp):
                        a = pe(lambda e, b=b, kk=kk, i=i, j=j, w2=w2: e.matmul(
                            banks[b][0:P, 0:D], Hb[i][:, kk, j * P:(j + 1) * P], w2[:, kk, :],
                            start=(kk == 0), stop=(kk == hp - 1)), free[b], hl, inc=(kk == hp - 1))
                    free[b] = xt_done[t] = dve(lambda e, b=b, t=t, e8=e8: e.scalar_tensor_tensor(
                        out=X[:, t, :], in0=banks[b][0:P, 0:D], scalar=cw[:, t, e8:e8 + 1], in1=X[:, t, :],
                        op0=ALU.mult, op1=ALU.add), a, xt_done.get(t), dve.last if e8 == 0 else None)
                hu[i] = a
            used[e8 % 2] = a
            if e8 + 2 < 8:
                tw.append(get(e8 + 2))
        barrier()

    def l2_ffn(XT):
        hid, hp = 1024, 8
        o = S0 + 6250
        wr = at(o, 2, p=128)
        dma(sp, None, None, None, make=lambda e: e.dma_start(
            wr, inp["L2_ffn_wr"].rearrange("(k p) o -> p (k o)", p=128), allow_slow_non_contiguous=True))
        br, t0 = param_n("L2_ffn_br", o + 2, 1)
        b1, t0 = param_t("L2_ffn_b1", o + 4, 8)
        b2, t0 = param_n("L2_ffn_b2", o + 12)
        o += 268
        wN, r_, cf = at(o, T), at(o + 25, 4, T), at(o + 125, T)
        o += 150
        tmp = o
        o += 125
        wrow = at(o, N)
        o += 3125
        jk = at(o, N)
        o += 3125
        W1 = at(o, 2, hid, p=128)
        t1 = load(W1, inp["L2_ffn_w1"].rearrange("(k p) f -> p k f", p=128), "w0")
        o += 2048
        W2 = at(o, hp, D, p=128)
        t1 = load(W2, inp["L2_ffn_w2"].rearrange("(k p) f -> p k f", p=128), "w0")
        o += 2048
        Hb = [at(o + i * hp * 500, hp, 500, p=128) for i in range(2)]
        o += 8000
        Y = [at(o + i * D, D) for i in range(2)]
        o += 2 * D
        assert o <= K0
        b = bank()
        for t in range(T):
            for k in range(2):
                a = pe(lambda e, t=t, k=k: e.matmul(banks[b][0:P, t:t + 1], XT[:, k, t * P:(t + 1) * P],
                                                    wr[:, k:k + 1], start=(k == 0), stop=(k == 1)), t0, free[b],
                       inc=(k == 1 and t == T - 1))
        free[b] = a = dve(lambda e: e.tensor_scalar(wN, banks[b][0:P, 0:T], br[:, 0:1], None, ALU.add), a)
        ro = rows_out(wN, T, 0, tmp, "ro", a)
        lw = row_bcast(wrow, 0, 0, N, "asr", ro)
        z = dve(lambda e: e.memset(r_, 0.0), lw)
        dve.wait(z)
        j0 = None
        for t in range(T):
            sc = wN[:, t:t + 1]
            lo, hi = t * P, (t + 1) * P
            if t:
                j0 = dve(lambda e, sc=sc, lo=lo, t=t: e.tensor_scalar(
                    jk[:, 0:lo], wrow[:, 0:lo], sc, None, ALU.is_ge, ALU.add, accum_out=r_[:, 0, t:t + 1]), j0)
            j0 = dve(lambda e, sc=sc, lo=lo, t=t: e.tensor_scalar(
                jk[:, lo:N], wrow[:, lo:N], sc, None, ALU.is_gt, ALU.add, accum_out=r_[:, 1, t:t + 1]), j0)
            j0 = dve(lambda e, sc=sc, lo=lo, hi=hi, t=t: e.scalar_tensor_tensor(
                out=jk[:, lo:hi], in0=wrow[:, lo:hi], scalar=sc, in1=tri, op0=ALU.is_equal, op1=ALU.mult,
                accum_out=r_[:, 2, t:t + 1]), j0)
        a = dve(lambda e: e.tensor_tensor(r_[:, 0, :], r_[:, 0, :], r_[:, 1, :], ALU.add), j0)
        a = dve(lambda e: e.tensor_tensor(r_[:, 0, :], r_[:, 0, :], r_[:, 2, :], ALU.add), a)
        a = dve(lambda e: e.tensor_scalar(r_[:, 0, :], r_[:, 0, :], 1560.5, None, ALU.is_lt), a)
        a = dve(lambda e: e.tensor_tensor(cf, r_[:, 0, :], wN, ALU.mult), a)
        a = dve(lambda e: e.tensor_tensor(X, X, XN, ALU.add), a)
        dve.wait(a)
        hu, yu = [None, None], [None, None]
        n = 0
        for ci, (n0, w) in enumerate(CH):
            i = ci % 2
            hl = []
            for oo in range(hp):
                b = bank()
                for kk in range(2):
                    a = pe(lambda e, b=b, oo=oo, kk=kk, n0=n0, w=w: e.matmul(
                        banks[b][:, 0:w], W1[:, kk, oo * 128:(oo + 1) * 128], XT[:, kk, n0:n0 + w],
                        start=(kk == 0), stop=(kk == 1)), free[b], t1, inc=(kk == 1))
                free[b] = act(lambda e, b=b, oo=oo, i=i, w=w: e.activation(
                    Hb[i][:, oo, 0:w], banks[b][:, 0:w], ACT.Gelu_apprx_tanh, bias=b1[:, oo:oo + 1]), a, t0, hu[i])
                hl.append(free[b])
            for j in range(w // P):
                t = n0 // P + j
                b = bank()
                for kk in range(hp):
                    a = pe(lambda e, b=b, kk=kk, i=i, j=j: e.matmul(
                        banks[b][0:P, 0:D], Hb[i][:, kk, j * P:(j + 1) * P], W2[:, kk, :],
                        start=(kk == 0), stop=(kk == hp - 1)), free[b], hl, inc=(kk == hp - 1))
                y = n % 2
                n += 1
                free[b] = d = dve(lambda e, b=b, y=y: e.tensor_tensor(Y[y], banks[b][0:P, 0:D], b2, ALU.add), a, yu[y])
                yu[y] = dve(lambda e, y=y, t=t: e.scalar_tensor_tensor(
                    out=X[:, t, :], in0=Y[y], scalar=cf[:, t:t + 1], in1=X[:, t, :], op0=ALU.mult, op1=ALU.add), d)
            hu[i] = a
        barrier()

    wtv = WT.rearrange("(s p) d -> p s d", p=P)
    c16v = C16.rearrange("(s p) d -> p s d", p=P)

    def aggregate(src, k, ro, counts, sink, *tokens):
        if counts:
            Lb = [at(ro + i * 1250, 5, 500, dt=U16) for i in range(2)]
            Vb = [at(ro + 2500 + i * 2500, 5, 500) for i in range(2)]
        else:
            Vb = [at(ro + i * 2500, 5, 500) for i in range(3)]
        nb = len(Vb)
        used = [None] * nb
        lu = [None, None]
        it = 0
        for ci, (n0, w) in enumerate(CH):
            bs = [(ci % 2) * k + kk for kk in range(k)]
            for s5 in range(5):
                i = it % nb
                if counts:
                    l = load(Lb[i][:, :, 0:w], c16v[:, s5 * 5:s5 * 5 + 5, n0:n0 + w], "lb%d" % i, lu[i])
                    l = copy_out(it, Vb[i][:, :, 0:w], Lb[i][:, :, 0:w], l, used[i])
                    lu[i] = l
                else:
                    l = load(Vb[i][:, :, 0:w], wtv[:, s5 * 5:s5 * 5 + 5, n0:n0 + w], "lb%d" % i, used[i])
                it += 1
                for s in range(5):
                    for kk in range(k):
                        a = pe(lambda e, i=i, s=s, s5=s5, kk=kk, b=bs[kk], w=w: e.matmul(
                            banks[b][:, 0:w], src[:, s5 * 5 + s, kk * 128:(kk + 1) * 128], Vb[i][:, s, 0:w],
                            start=(s5 == 0 and s == 0), stop=(s5 == 4 and s == 4)), l, free[bs[kk]], *tokens)
                used[i] = a
            ends = sink(ci, n0, w, bs, a)
            for kk in range(k):
                free[bs[kk]] = ends[kk]

    def bn(v, g, bb, o, relu, *tokens):
        s = at(o, 2 * T, 6, p=128)
        m = at(o + 300, 2, 2, p=128)
        sc, sh, tm = at(o + 304, 2, p=128), at(o + 306, 2, p=128), at(o + 308, 2, p=128)
        dve.wait(*tokens)
        for k in range(2):
            for c in range(T):
                a = dve(lambda e, k=k, c=c: e.bn_stats(s[:, k * T + c, :], v[:, k, c * P:(c + 1) * P]))
        dve.wait(a)
        for k in range(2):
            a = dve(lambda e, k=k: e.bn_aggr(m[:, k, :], s[:, k * T:(k + 1) * T, :].rearrange("p a b -> p (a b)")))
        a = rstd(m[:, :, 1], sc, tm, a)
        a = dve(lambda e: e.tensor_tensor(sc, sc, g, ALU.mult), a)
        for k in range(2):
            a = dve(lambda e, k=k: e.tensor_scalar(v[:, k, :], v[:, k, :], m[:, k, 0:1], sc[:, k:k + 1],
                                                   ALU.subtract, ALU.mult), a)
        for k in range(2):
            a = act(lambda e, k=k: e.activation(v[:, k, :], v[:, k, :], ACT.Relu if relu else ACT.Identity,
                                                bias=bb[:, k:k + 1]), a)
        return a

    def l1_gnn(XT):
        hN = at(S0 + 6250, T, D)
        ro = S0 + 12650
        ag = [at(S0 + 20150 + i * 1000, 2, 500, p=128) for i in range(2)]
        h2 = at(S0 + 22150, 2, N, p=128)
        o = S0 + 28400
        w1, t1 = weight("L1_gnn_c1_w1", o, 2, D)
        w2, t1 = weight("L1_gnn_c1_w2", o + 512, 2, D)
        w3, t1 = weight("L1_gnn_c2_w1", o + 1024, 2, D)
        w4, t1 = weight("L1_gnn_c2_w2", o + 1536, 2, D)
        o += 2048
        b1, t0 = param_n("L1_gnn_c1_b1", o)
        b3, t0 = param_n("L1_gnn_c2_b1", o + 256)
        o += 512
        pt = {}
        for nme in ("c1_b2", "c1_g", "c1_b", "bn1_g", "bn1_b", "c2_b2", "c2_g", "c2_b", "bn2_g", "bn2_b"):
            pt[nme], t0 = param_t("L1_gnn_" + nme, o)
            o += 2
        bo = o
        assert o + 310 <= K0

        def conv(srcT, wa, ba, wb, bb, ready):
            def sink(t, ps, a):
                a = dve(lambda e: e.tensor_tensor(hN[:, t, :], ps, ba, ALU.add), a, t0)
                relu.append(dve(lambda e: e.tensor_scalar(hN[:, t, :], hN[:, t, :], 0.0, None, ALU.max), a))
                return a
            relu = []
            lin_N(srcT, 2, wa, D, sink, t1, ready)
            agu = [None, None]
            fin = []

            def sink2(ci, n0, w, bs, a):
                i = ci % 2
                ends = [copy_out(kk, ag[i][:, kk, 0:w], banks[bs[kk]][:, 0:w], a, agu[i]) for kk in range(2)]
                for oo in range(2):
                    b = bank((4, 8))
                    for kk in range(2):
                        m = pe(lambda e, b=b, kk=kk, oo=oo, i=i, w=w: e.matmul(
                            banks[b][:, 0:w], wb[:, kk, oo * 128:(oo + 1) * 128], ag[i][:, kk, 0:w],
                            start=(kk == 0), stop=(kk == 1)), free[b], ends, inc=(kk == 1))
                    free[b] = act(lambda e, b=b, oo=oo, n0=n0, w=w: e.activation(
                        h2[:, oo, n0:n0 + w], banks[b][:, 0:w], ACT.Identity, bias=bb[:, oo:oo + 1]), m)
                    fin.append(free[b])
                agu[i] = m
                return ends

            aggregate(hN, 2, ro, False, sink2, relu)
            return fin

        f = conv(XT, w1, b1, w2, pt["c1_b2"], None)
        a = bn(h2, pt["c1_g"], pt["c1_b"], bo, True, f)
        a = bn(h2, pt["bn1_g"], pt["bn1_b"], bo, True, a)
        barrier()
        f = conv(h2, w3, b3, w4, pt["c2_b2"], None)
        a = bn(h2, pt["c2_g"], pt["c2_b"], bo, True, f)
        a = bn(h2, pt["bn2_g"], pt["bn2_b"], bo, False, a)
        a = dve(lambda e: e.tensor_tensor(h2, h2, XT, ALU.add), a)
        a = dve(lambda e: e.tensor_scalar(h2, h2, 0.0, None, ALU.max), a)
        add_from_T(h2, 2, 0, N, a)
        barrier()

    def l3_gnn():
        u = at(XN0, T, D)
        z2 = at(XN0, T, 512)
        hT = at(19200, 4, N, p=128)
        o = 31700
        ro = o
        o += 7500
        wt = at(o, 2048, p=128)
        o += 2048
        dvB = at(o, N, p=128)
        o += 3125
        ag = [at(o + i * 2000, 4, 500, p=128) for i in range(2)]
        o += 4000
        dvN = at(o, T)
        o += 25
        b1, t0 = param_t("L3_gnn_b1", o, 4)
        b2, t0 = param_t("L3_gnn_b2", o + 4, 4)
        b3, t0 = param_t("L3_gnn_b3", o + 8, 2)
        o += 10
        assert o <= K0
        l = load(dvB, DEG[0, :].partition_broadcast(128), "dg")
        l = dma(sp, None, None, "dg", make=lambda e: e.dma_start(
            dvN, DEG.rearrange("o (t p) -> p (o t)", p=P), allow_slow_non_contiguous=True))
        a = act(lambda e: e.activation(dvB, dvB, ACT.Sqrt), l)
        a = act(lambda e: e.activation(dvN, dvN, ACT.Sqrt), l)
        a = dve(lambda e: e.reciprocal(dvB, dvB), a)
        a = dve(lambda e: e.reciprocal(dvN, dvN), a)
        us = [dve(lambda e, t=t: e.tensor_scalar(u[:, t, :], u[:, t, :], dvN[:, t:t + 1], None, ALU.mult), a)
              for t in range(T)]
        W1 = wt[:, 0:1024].rearrange("p (k f) -> p k f", k=2)
        t1 = load(W1, inp["L3_gnn_W1"].rearrange("(k p) f -> p k f", p=128), None)
        agu = [None, None]

        def sink1(ci, n0, w, bs, a):
            i = ci % 2
            ends = [dve(lambda e, kk=kk, i=i: e.tensor_tensor(ag[i][:, kk, 0:w], banks[bs[kk]][:, 0:w],
                                                              dvB[:, n0:n0 + w], ALU.mult), a, agu[i])
                    for kk in range(2)]
            for oo in range(4):
                b = bank((4, 8))
                for kk in range(2):
                    m = pe(lambda e, b=b, kk=kk, oo=oo: e.matmul(
                        banks[b][:, 0:w], W1[:, kk, oo * 128:(oo + 1) * 128], ag[i][:, kk, 0:w],
                        start=(kk == 0), stop=(kk == 1)), free[b], ends, t1, inc=(kk == 1))
                free[b] = act(lambda e, b=b, oo=oo: e.activation(
                    hT[:, oo, n0:n0 + w], banks[b][:, 0:w], ACT.Tanh, bias=b1[:, oo:oo + 1]), m, t0)
            agu[i] = m
            return ends

        aggregate(u, 2, ro, True, sink1, us)
        barrier()
        W2 = wt.rearrange("p (k f) -> p k f", k=4)
        t1 = load(W2, inp["L3_gnn_W2"].rearrange("(k p) f -> p k f", p=128), None)

        def sinkz(t, ps, a):
            return evac(t, lambda e: e.activation(z2[:, t, :], ps, ACT.Copy, scale=dvN[:, t:t + 1]),
                        lambda e: e.tensor_scalar(z2[:, t, :], ps, dvN[:, t:t + 1], None, ALU.mult), a)

        lin_N(hT, 4, W2, 512, sinkz, t1)
        barrier()

        def sink2(ci, n0, w, bs, a):
            i = ci % 2
            ends = []
            for kk in range(4):
                m = dve(lambda e, kk=kk: e.tensor_tensor(ag[i][:, kk, 0:w], banks[bs[kk]][:, 0:w],
                                                         dvB[:, n0:n0 + w], ALU.mult), a, agu[i])
                ends.append(m)
                m = act(lambda e, kk=kk: e.activation(hT[:, kk, n0:n0 + w], ag[i][:, kk, 0:w], ACT.Tanh,
                                                      bias=b2[:, kk:kk + 1]), m)
            agu[i] = m
            return ends

        agu = [None, None]
        aggregate(z2, 4, ro, True, sink2)
        barrier()
        W3 = wt[:, 0:1024].rearrange("p (k f) -> p k f", k=4)
        t1 = load(W3, inp["L3_gnn_W3"].rearrange("(k p) f -> p k f", p=128), None)

        def sinkz3(t, ps, a):
            return evac(t, lambda e: e.activation(u[:, t, :], ps, ACT.Copy, scale=dvN[:, t:t + 1]),
                        lambda e: e.tensor_scalar(u[:, t, :], ps, dvN[:, t:t + 1], None, ALU.mult), a)

        z3 = lin_N(hT, 4, W3, D, sinkz3, t1)
        agu = [None, None]

        def sink3(ci, n0, w, bs, a):
            i = ci % 2
            ends = []
            for kk in range(2):
                m = dve(lambda e, kk=kk: e.tensor_tensor(ag[i][:, kk, 0:w], banks[bs[kk]][:, 0:w],
                                                         dvB[:, n0:n0 + w], ALU.mult), a, agu[i])
                ends.append(m)
                m = act(lambda e, kk=kk: e.activation(ag[i][:, kk, 0:w], ag[i][:, kk, 0:w], ACT.Identity,
                                                      bias=b3[:, kk:kk + 1]), m)
            for j in range(w // P):
                t = n0 // P + j
                b = bank((4, 8))
                for kk in range(2):
                    x = pe(lambda e, kk=kk, j=j, b=b: e.transpose(
                        banks[b][0:P, kk * 128:(kk + 1) * 128], ag[i][:, kk, j * P:(j + 1) * P], ident[:, :]),
                        free[b], m, inc=(kk == 1))
                free[b] = dve(lambda e, t=t, b=b: e.tensor_tensor(X[:, t, :], banks[b][0:P, 0:D], X[:, t, :],
                                                                  ALU.add), x)
            agu[i] = x
            return ends

        aggregate(u, 2, ro, True, sink3, z3)
        barrier()

    XT = at(S0, 2, N, p=128)

    def norm_turn():
        nt = norm_tiles(X, XN)
        to_T(XN, XT, nt)
        barrier()

    def run():
        graph()
        if stop == "graph":
            return
        norm_turn()
        l0_mix(XT)
        if stop == "m0":
            return
        gat("L0_gnn", 4, 64, 1e-16, XT)
        if stop == "g0":
            return
        norm_turn()
        ffn(XT, "L0_ffn", 512, ACT.Gelu, "all", "L0_ffn_gate_w", ["L0_ffn_gate_b"])
        if stop == "f0":
            return
        norm_turn()
        l1_mix(XT)
        if stop == "m1":
            return
        l1_gnn(XT)
        if stop == "g1":
            return
        norm_turn()
        ffn(XT, "L1_ffn", 512, ACT.Relu, "two", "L1_ffn_Wg", ["L1_ffn_bg", "L1_ffn_bias"])
        if stop == "f1":
            return
        norm_turn()
        l2_mix(XT)
        if stop == "m2":
            return
        gat("L2_gnn", 8, 32, 0.0, XT)
        if stop == "g2":
            return
        norm_turn()
        l2_ffn(XT)
        if stop == "f2":
            return
        norm_turn()
        l3_mix(XT)
        if stop == "m3":
            return
        l3_gnn()
        if stop == "g3":
            return
        norm_turn()
        ffn(XT, "L3_ffn", 1024, ACT.Gelu, "share", "L3_ffn_Wr", ["L3_ffn_br"],
            affine=("L3_ffn_ln_g", "L3_ffn_ln_b"), again=True)

    run()
    t = load(rows(out, P), X, "out", dve.last)
    sp.wait(t)
    with ctx:
        block = ctx.enter_context(nc.Block())

        @block.tensor
        def _(eng):
            pe.emit(eng)

        @block.scalar
        def _(eng):
            act.emit(eng)

        @block.vector
        def _(eng):
            dve.emit(eng)

        @block.gpsimd
        def _(eng):
            pool.emit(eng)

        @block.sync
        def _(eng):
            sp.emit(eng)


_DERIVED = {"L0_mix_w_qkv": "w", "L0_mix_b_qkv": "b", "L3_mix_wq": "wqT", "L3_mix_wk": "wkT", "L3_mix_wv": "wvT",
            "L3_mix_wo": "woT"}
_UNUSED = {"L2_ffn_attention_mask"}


def _layout(inputs):
    arrays = {}
    for name, value in inputs.items():
        a = np.asarray(value)
        if name in _UNUSED:
            continue
        if name == "L0_mix_w_qkv":
            v = a.reshape(D, 8, 3, 32)
            for i, c in enumerate("qkv"):
                arrays[f"w{c}0"] = np.ascontiguousarray(v[:, :, i, :].reshape(D, D))
        elif name == "L0_mix_b_qkv":
            v = a.reshape(8, 3, 32)
            for i, c in enumerate("qkv"):
                arrays[f"b{c}0"] = np.ascontiguousarray(v[:, i, :].reshape(D))
        elif name in _DERIVED:
            arrays[_DERIVED[name]] = np.ascontiguousarray(a.T)
        else:
            arrays[name] = np.ascontiguousarray(a)
    return arrays


STOP = None


def kernel(**inputs):
    import concourse.bacc as bacc
    from concourse.bass_utils import run_bass_kernel_spmd

    nc = bacc.Bacc("TRN2", target_bir_lowering=False, num_devices=1)
    arrays = _layout(inputs)
    aps = {n: nc.dram_tensor(n, a.shape, mybir.dt.from_np(a.dtype), kind="ExternalInput").ap()
           for n, a in arrays.items()}
    out = nc.dram_tensor("out", (N, D), F32, kind="ExternalOutput").ap()
    program(nc, aps, out, STOP)
    r = run_bass_kernel_spmd(nc, [arrays], core_ids=[0])
    return r.results[0]["out"]
```

```python
import numpy as np
import concourse.bass as bass
from concourse import mybir
from contextlib import ExitStack

F32 = mybir.dt.float32
BF16 = mybir.dt.bfloat16
U16 = mybir.dt.uint16
I32 = mybir.dt.int32
ALU = mybir.AluOpType
ACT = mybir.ActivationFunctionType
AX = mybir.AxisListType.X

N, D, E = 3125, 256, 50000
P, T = 125, 25
CH = [(c * 500, 500 if c < 6 else 125) for c in range(7)]
NB, NQ = 100, 4
BIG = 1e30
WORDS = 51200


class Queue:

    def __init__(self, new_sem, name):
        self.new_sem, self.name = new_sem, name
        self.items, self.seen = [], {}
        self.turn()

    def turn(self):
        self.sem, self.count, self.last = self.new_sem(), 0, None

    def wait(self, *tokens):
        for t in tokens:
            if t is None:
                continue
            if isinstance(t, list):
                self.wait(*t)
                continue
            sem, value = t
            if self.seen.get(id(sem), 0) < value:
                self.seen[id(sem)] = value
                self.items.append((None, sem, value))

    def __call__(self, fn, *tokens, inc=True):
        self.wait(*tokens)
        if not inc:
            self.items.append((fn, None, 0))
            return None
        if self.count >= 30000:
            self.turn()
        self.count += 1
        self.items.append((fn, self.sem, 1))
        self.last = (self.sem, self.count)
        return self.last

    def emit(self, eng):
        for fn, sem, value in self.items:
            if fn is None:
                eng.wait_ge(sem, value)
            else:
                ins = fn(eng)
                if sem is not None:
                    ins.then_inc(sem, value)


def program(nc, inp, out, stop=None):
    dram = {}
    ctx = ExitStack()
    nsem = [0]

    def new_sem():
        nsem[0] += 1
        return ctx.enter_context(nc.semaphore(f"s{nsem[0]}"))

    pe, act, dve, pool, sp = (Queue(new_sem, n) for n in ("pe", "act", "dve", "pool", "sp"))
    engines = [pe, act, dve, pool, sp]
    channels = {}
    once = []

    def dma(eng, dst, src, ch, *tokens, make=None):
        if ch is None:
            once.append(dma(eng, dst, src, "once%d" % len(once), *tokens, make=make))
            return list(once)
        if ch not in channels:
            channels[ch] = [new_sem(), 0]
        c = channels[ch]
        if c[1] >= 30000:
            c[0], c[1] = new_sem(), 0
        eng.wait(*tokens)
        c[1] += 16
        eng.items.append((make or (lambda e: e.dma_start(dst, src)), c[0], 16))
        return (c[0], c[1])

    def load(dst, src, ch, *tokens):
        return dma(sp, dst, src, ch, *tokens)

    def barrier():
        marks = [e.last for e in engines] + [(c[0], c[1]) for c in channels.values() if c[1]]
        for e in engines:
            e.wait(*marks)
        for i in range(8):
            free[i] = None
        once.clear()

    arena = ctx.enter_context(nc.sbuf_tensor("arena", [128, WORDS], F32))
    banks = [ctx.enter_context(nc.psum_tensor(f"bank{i}", [128, 512], F32)) for i in range(8)]
    free = [None] * 8

    def at(off, *dims, p=P, dt=F32):
        n = int(np.prod(dims))
        words = n if dt in (F32, I32) else (n + 1) // 2
        assert off + words <= WORDS, (off, words)
        v = arena[0:p, off:off + words]
        if dt != F32:
            v = v.bitcast(dt)
            v = v[:, 0:n]
        if len(dims) == 2:
            v = v.rearrange("p (a b) -> p a b", a=dims[0])
        elif len(dims) == 3:
            v = v.rearrange("p (a b c) -> p a b c", a=dims[0], b=dims[1])
        return v

    def rows(v, n):
        return v.rearrange("(t p) f -> p t f", p=n)

    ring = [0]

    def bank(pool_of=(0, 8)):
        ring[0] += 1
        i = pool_of[0] + ring[0] % (pool_of[1] - pool_of[0])
        return i

    X0, XN0, S0 = 0, 6400, 12800
    K0 = 49700
    X = at(X0, T, D)
    XN = at(XN0, T, D)
    ident = at(K0, 128, p=128)
    ones = at(K0 + 128, 128, p=128)
    iota8 = at(K0 + 256, 8)
    bmask32 = at(K0 + 264, 128, p=128)
    bmask64 = at(K0 + 392, 128, p=128)
    tri = at(K0 + 520, 125)
    SM = K0 + 645
    st6 = at(SM, T, 6)
    mv = at(SM + 150, T, 2)
    rs = at(SM + 200, T)
    rs2 = at(SM + 225, T)
    PV = SM + 250

    def dd(name, shape, dt=F32):
        return nc.dram_tensor(name, shape, dt, kind="Internal").ap()

    G = dd("G", [N * N + 500, 2])
    C16 = dd("C16", [N, N], U16)
    WT = dd("WT", [N, N])
    MK = dd("MK", [N, N], BF16)
    KEY = dd("KEY", [1, E])
    DEG = dd("DEG", [1, N])
    ROW = dd("ROW", [24 * T, P])

    pm = pool(lambda e: e.memset(ident, 0.0))
    pm1 = pool(lambda e: e.memset(ones, 1.0))
    t_id = pool(lambda e: e.affine_select(out=ident, in_=ident, compare_op=ALU.not_equal, fill=1.0, base=0,
                                          pattern=[[-1, 128]], channel_multiplier=1), pm)
    t_tri = pool(lambda e: e.affine_select(out=tri, in_=ones[0:P, 0:P], compare_op=ALU.is_gt, fill=0.0, base=0,
                                           pattern=[[-1, P]], channel_multiplier=1), pm1)
    for e8 in range(8):
        pool(lambda e, e8=e8: e.memset(iota8[:, e8:e8 + 1], float(8 - e8)))

    def block_mask(m, c):
        a = pool(lambda e: e.memset(m, 1.0))
        v = m.rearrange("p (b c) -> p b c", c=c)
        a = pool(lambda e: e.affine_select(out=v, in_=v, compare_op=ALU.is_ge, fill=0.0, base=0,
                                           pattern=[[-c, 128 // c], [0, c]], channel_multiplier=1), a)
        return pool(lambda e: e.affine_select(out=v, in_=v, compare_op=ALU.is_ge, fill=0.0, base=c - 1,
                                              pattern=[[c, 128 // c], [0, c]], channel_multiplier=-1), a)

    block_mask(bmask32, 32)
    block_mask(bmask64, 64)
    load(X, rows(inp["x"], P), "x")
    barrier()

    def evac(i, fn_act, fn_dve, *tokens):
        return act(fn_act, *tokens) if i % 2 else dve(fn_dve, *tokens)

    def copy_out(i, dst, src, *tokens):
        return evac(i, lambda e: e.activation(dst, src, ACT.Copy), lambda e: e.tensor_copy(dst, src), *tokens)

    def bcast(v, n, k=1):
        s = list(v.shape)
        return v.unsqueeze(k).broadcast_to(s[:k] + [n] + s[k:])

    def param_n(name, off, w=D):
        dst = at(off, w)
        src = inp[name] if len(inp[name].shape) == 1 else inp[name].rearrange("a b -> (a b)")
        return dst, load(dst, src.partition_broadcast(P), None)

    def param_t(name, off, k=2, src=None):
        dst = at(off, k, p=128)
        src = inp[name] if src is None else src
        return dst, dma(sp, dst, None, None, make=lambda e: e.dma_start(
            dst, src.rearrange("(k p) -> p k", p=128), allow_slow_non_contiguous=True))

    def weight(name, off, k, f, src=None, ch=None, tokens=()):
        dst = at(off, k, f, p=128)
        src = inp[name] if src is None else src
        return dst, load(dst, src.rearrange("(k p) f -> p k f", p=128), ch, *tokens)

    def rstd(var, dst, tmp, *tokens, eps=1e-5):
        a = dve(lambda e: e.tensor_scalar(tmp, var, eps, None, ALU.add), *tokens)
        b = act(lambda e: e.activation(dst, tmp, ACT.Sqrt), a)
        return dve(lambda e: e.reciprocal(dst, dst), b)

    def norm_tiles(src, dst, *tokens):
        dve.wait(*tokens)
        for t in range(T):
            a = dve(lambda e, t=t: e.bn_stats(st6[:, t, :], src[:, t, :]))
        dve.wait(a)
        for t in range(T):
            a = dve(lambda e, t=t: e.bn_aggr(mv[:, t, :], st6[:, t, :]))
        r = rstd(mv[:, :, 1], rs, rs2, a)
        dve.wait(r)
        return [dve(lambda e, t=t: e.tensor_scalar(dst[:, t, :], src[:, t, :], mv[:, t, 0:1], rs[:, t:t + 1],
                                                   ALU.subtract, ALU.mult)) for t in range(T)]

    def to_T(src, dst, ready, k=2):
        last = []
        n = 0
        for c, (n0, w) in enumerate(CH):
            for kk in range(k):
                b = bank()
                m = w // P
                for i in range(m):
                    t = n0 // P + i
                    a = pe(lambda e, t=t, i=i, b=b, kk=kk: e.transpose(
                        banks[b][:, i * P:(i + 1) * P], src[:, t, kk * 128:(kk + 1) * 128], ident[0:P, 0:P]),
                        free[b], ready[t] if isinstance(ready, list) else ready, inc=(i == m - 1))
                free[b] = copy_out(n, dst[:, kk, n0:n0 + w], banks[b][:, 0:w], a)
                last.append(free[b])
                n += 1
        return last[-2:]

    def add_from_T(src, k, n0, w, *tokens):
        for i in range(w // P):
            t = n0 // P + i
            b = bank()
            for kk in range(k):
                a = pe(lambda e, kk=kk, i=i, b=b: e.transpose(
                    banks[b][0:P, kk * 128:(kk + 1) * 128], src[:, kk, i * P:(i + 1) * P], ident[:, :]),
                    free[b], *tokens, inc=(kk == k - 1))
            free[b] = dve(lambda e, t=t, b=b: e.tensor_tensor(X[:, t, :], banks[b][0:P, 0:D], X[:, t, :], ALU.add), a)
        return a

    def lin_N(srcT, k, W, f, sink, *tokens, f0=0):
        out_t = []
        for t in range(T):
            b = bank()
            for kk in range(k):
                a = pe(lambda e, t=t, kk=kk, b=b: e.matmul(
                    banks[b][0:P, 0:f], srcT[:, kk, t * P:(t + 1) * P], W[:, kk, f0:f0 + f],
                    start=(kk == 0), stop=(kk == k - 1)), free[b], *tokens, inc=(kk == k - 1))
            free[b] = sink(t, banks[b][0:P, 0:f], a)
            out_t.append(free[b])
        return out_t

    def lin_T(W, srcT, k, o, sink, *tokens, chunks=CH, base=0):
        last = []
        for n0, w in chunks:
            for oo in range(o):
                b = bank()
                for kk in range(k):
                    a = pe(lambda e, kk=kk, b=b, oo=oo, n0=n0, w=w: e.matmul(
                        banks[b][:, 0:w], W[:, kk, oo * 128:(oo + 1) * 128], srcT[:, kk, n0 - base:n0 - base + w],
                        start=(kk == 0), stop=(kk == k - 1)), free[b], *tokens, inc=(kk == k - 1))
                free[b] = sink(oo, n0, w, banks[b][:, 0:w], a)
                last.append(free[b])
        return last[-4:]

    def head_norm(v, tmp, sm, heads, g, bb, *tokens):
        c = D // heads
        n = T * heads
        s1, s2, s3 = (at(sm + i * n, n) for i in range(3))
        vv = v.rearrange("p t (h c) -> p (t h) c", c=c)
        tt = tmp.rearrange("p t (h c) -> p (t h) c", c=c)
        a = dve(lambda e: e.tensor_reduce(s1, vv, AX, ALU.add), *tokens)
        a = dve(lambda e: e.tensor_scalar(s1, s1, 1.0 / c, None, ALU.mult), a)
        a = dve(lambda e: e.tensor_tensor(vv, vv, bcast(s1, c, 2), ALU.subtract), a)
        a = act(lambda e: e.activation(tmp, v, ACT.Square), a)
        a = dve(lambda e: e.tensor_reduce(s2, tt, AX, ALU.add), a)
        a = dve(lambda e: e.tensor_scalar(s2, s2, 1.0 / c, 1e-5, ALU.mult, ALU.add), a)
        a = act(lambda e: e.activation(s3, s2, ACT.Sqrt), a)
        a = dve(lambda e: e.reciprocal(s3, s3), a)
        a = dve(lambda e: e.tensor_tensor(vv, vv, bcast(s3, c, 2), ALU.mult), a)
        a = dve(lambda e: e.tensor_tensor(vv, vv, bcast(g, n), ALU.mult), a)
        return dve(lambda e: e.tensor_tensor(vv, vv, bcast(bb, n), ALU.add), a)

    def rows_out(src, m, row0, tmp_off, ch, *tokens):
        b = bank()
        tmp = at(tmp_off, P, p=m)
        a = pe(lambda e: e.transpose(banks[b][0:m, 0:P], src, ident[0:P, 0:P]), free[b], *tokens)
        free[b] = dve(lambda e: e.tensor_copy(tmp, banks[b][0:m, 0:P]), a)
        return load(ROW[row0:row0 + m, :], tmp, ch, free[b])

    def row_bcast(dst, row0, n0, w, ch, *tokens):
        src = ROW[row0:row0 + T, :].rearrange("t p -> (t p)")[n0:n0 + w]
        return load(dst, src.partition_broadcast(P), ch, *tokens)

    def graph():
        b0 = S0 + 6250
        si, di, sf, df = (at(b0 + i * 500, 500, p=NB, dt=I32 if i < 2 else F32) for i in range(4))
        a = load(si, inp["src"].rearrange("(b j) -> b j", b=NB), "ed")
        le = load(di, inp["dst"].rearrange("(b j) -> b j", b=NB), "ed")
        zero = at(S0, 6250)
        z = dve(lambda e: e.memset(zero, 0.0))
        gz = G[0:N * N, :].rearrange("(s p n) c -> s p (n c)", p=P, n=N)
        for s in range(T):
            zt = dma(sp if s % 2 else act, gz[s], zero, "gz%d" % (s % 2), z)
        load(G[N * N:N * N + 500, :].rearrange("(p n) c -> p (n c)", p=P), zero[:, 0:8], "gz1", z)
        a = le
        c1 = dve(lambda e: e.tensor_copy(sf, si), a)
        c2 = dve(lambda e: e.tensor_copy(df, di))
        c3 = dve(lambda e: e.scalar_tensor_tensor(out=sf, in0=sf, scalar=float(N), in1=df, op0=ALU.mult,
                                                  op1=ALU.add), c2)
        kd = load(KEY.rearrange("o (b j) -> (o b) j", b=NB), sf, "key", c3)
        b1 = b0 + 2000
        K = at(b1, NQ, NB)
        CT = at(b1 + 400, NQ, NB)
        IDF = at(b1 + 800, NQ, NB)
        IDX = at(b1 + 1200, NQ, NB, dt=I32)
        LD = at(b1 + 1600, NQ, NB)
        DM = at(b1 + 2000, NQ)
        DMI = at(b1 + 2004, NQ, dt=I32)
        VAL = at(b1 + 2010, NQ * NB * 2)
        val = VAL.rearrange("p (q b c) -> p q b c", q=NQ, c=2)
        TR = at(b1 + 2810, NQ, 500)
        b2 = b1 + 4810
        KR = [at(b2 + i * 2500, 5, 500) for i in range(2)]
        WR = [at(b2 + 5000 + i * 2500, 5, 500) for i in range(2)]
        JK = [at(b2 + 10000 + i * 500, 500) for i in range(2)]
        p1 = pool(lambda e: e.iota(DMI, pattern=[[P, NQ]], base=N * N, channel_multiplier=1))
        dm = dve(lambda e: e.tensor_copy(DM, DMI), p1)
        p2 = pool(lambda e: e.memset(TR, 1025.0))
        trt = pool(lambda e: e.affine_select(out=TR, in_=TR, compare_op=ALU.is_gt, fill=1.0, base=0,
                                             pattern=[[P, NQ], [-1, 500]], channel_multiplier=1), p2)
        kt = None
        for q in range(NQ):
            b = bank()
            a = pe(lambda e, q=q, b=b: e.transpose(banks[b][0:P, 0:NB], sf[:, q * P:(q + 1) * P],
                                                   ident[0:NB, 0:NB]), c3)
            kt = dve(lambda e, q=q, b=b: e.tensor_copy(K[:, q, :], banks[b][0:P, 0:NB]), a)
        dve.wait(kt, trt, dm)
        used = [None, None]
        chain = [channels["gz0"], channels["gz1"]]
        chain = [(c[0], c[1]) for c in chain]
        jt = [None, None]
        for g in range(NB // 5):
            i = g % 2
            l1 = load(KR[i], KEY[0, g * 2500:(g + 1) * 2500].rearrange("(b j) -> b j", b=5).partition_broadcast(P),
                      "kr%d" % i, kd, used[i])
            l2 = load(WR[i], inp["edge_weight"][g * 2500:(g + 1) * 2500].rearrange("(b j) -> b j", b=5)
                      .partition_broadcast(P), "kr%d" % i)
            dve.wait(l2)
            for bb in range(5):
                b = g * 5 + bb
                for q in range(NQ):
                    a1 = dve(lambda e, i=i, bb=bb, b=b, q=q: e.scalar_tensor_tensor(
                        out=JK[0], in0=KR[i][:, bb, :], scalar=K[:, q, b:b + 1], in1=TR[:, q, :],
                        op0=ALU.is_equal, op1=ALU.mult, accum_out=CT[:, q, b:b + 1]), jt[0])
                    jt[0] = a1
                    a2 = dve(lambda e, i=i, bb=bb, b=b, q=q: e.scalar_tensor_tensor(
                        out=JK[1], in0=KR[i][:, bb, :], scalar=K[:, q, b:b + 1], in1=WR[i][:, bb, :],
                        op0=ALU.is_equal, op1=ALU.mult, accum_out=val[:, q, b, 1:2]), jt[1])
                    jt[1] = a2
            used[i] = a2
            bs = slice(g * 5, g * 5 + 5)
            a = dve(lambda e, bs=bs: e.tensor_scalar(LD[:, :, bs], CT[:, :, bs], 1024.0, None, ALU.is_lt), a2)
            a = dve(lambda e, bs=bs: e.tensor_copy(val[:, :, bs, 0], CT[:, :, bs]))
            a = dve(lambda e, bs=bs: e.tensor_tensor(IDF[:, :, bs], K[:, :, bs], bcast(DM, 5, 2), ALU.subtract))
            a = dve(lambda e, bs=bs: e.tensor_tensor(IDF[:, :, bs], IDF[:, :, bs], LD[:, :, bs], ALU.mult), a)
            a = dve(lambda e, bs=bs: e.tensor_tensor(IDF[:, :, bs], IDF[:, :, bs], bcast(DM, 5, 2), ALU.add), a)
            a = dve(lambda e, bs=bs: e.tensor_copy(IDX[:, :, bs], IDF[:, :, bs]), a)
            for bb in range(5):
                b = g * 5 + bb
                for q in range(NQ):
                    t = dma(pool, None, None, "sc", a, chain, make=lambda e, q=q, b=b: e.indirect_dma_start(
                        out=G[:, :], out_offset=bass.IndirectOffsetOnAxis(ap=IDX[:, q, b:b + 1], axis=0),
                        in_=val[:, q, b, :], in_offset=None, compute_op=ALU.add))
                chain = t
        barrier()
        o = S0
        GT = [at(o + i * 6250, N, 2) for i in range(2)]
        o += 12500
        CO = [at(o + i * 1563, N, dt=U16) for i in range(2)]
        o += 3126
        WO = [at(o + i * 3125, N) for i in range(2)]
        o += 6250
        MB = [at(o + i * 1563, N, dt=BF16) for i in range(2)]
        o += 3126
        idb = at(o, 126, dt=BF16)
        o += 63
        MS = at(o, T, 625, dt=BF16)
        o += 7813
        assert o <= K0
        ib = dve(lambda e: e.tensor_copy(idb[:, 0:P], ident[0:P, 0:P]))
        gt = G[0:N * N, :].rearrange("(s p n) c -> s p n c", p=P, n=N)
        gfree = [None, None]
        cw = [None, None]
        ww = [None, None]
        mused = [None, None]
        msw = None
        tb = banks[7]
        tbv = tb[0:P, :].bitcast(BF16)
        for s in range(T):
            i = s % 2
            l = load(GT[i], gt[s], "gt%d" % i, gfree[i])
            d = dve(lambda e, i=i, s=s: e.tensor_tensor(GT[i][:, s * P:(s + 1) * P, 0], GT[i][:, s * P:(s + 1) * P, 0],
                                                        ident[0:P, 0:P], ALU.add), l)
            c = act(lambda e, i=i: e.activation(CO[i], GT[i][:, :, 0], ACT.Copy), d, cw[i])
            w = act(lambda e, i=i: e.activation(WO[i], GT[i][:, :, 1], ACT.Copy), ww[i])
            m = dve(lambda e, i=i: e.tensor_scalar(MB[i], GT[i][:, :, 0], 1.0, None, ALU.min), d, mused[i])
            cw[i] = load(C16[s * P:(s + 1) * P, :], CO[i], "co%d" % i, c)
            ww[i] = load(WT[s * P:(s + 1) * P, :], WO[i], "wo%d" % i, w)
            for cc, (n0, wd) in enumerate(CH):
                a = pe(lambda e, cc=cc, n0=n0, wd=wd, i=i, s=s: e.matmul(
                    banks[cc][:, 0:wd], ones[0:P, :], GT[i][:, n0:n0 + wd, 0], start=(s == 0), stop=(s == T - 1)),
                    d)
            gfree[i] = [a, m, w, c]
            for j0 in range(0, T, 8):
                nj = min(8, T - j0)
                for j in range(nj):
                    a = pe(lambda e, j=j, j0=j0, i=i: e.transpose(
                        tbv[:, j * 128:j * 128 + P], MB[i][:, (j0 + j) * P:(j0 + j + 1) * P], idb[:, 0:P]),
                        m, ib, free[7], inc=(j == nj - 1))
                sl = s % 5
                free[7] = dve(lambda e, j0=j0, nj=nj, sl=sl: e.tensor_scalar(
                    MS[:, j0:j0 + nj, sl * P:(sl + 1) * P],
                    tbv[:, 0:nj * 128].rearrange("p (j c) -> p j c", c=128)[:, :, 0:P],
                    -1.0, BIG, ALU.add, ALU.mult), a, msw if sl == 0 else None)
            mused[i] = a
            if s % 5 == 4:
                msw = load(MK[:, (s - 4) * P:(s + 1) * P].rearrange("(j p) c -> p j c", p=P), MS, "ms", free[7])
        dr = WO[0]
        for cc, (n0, wd) in enumerate(CH):
            a = dve(lambda e, cc=cc, n0=n0, wd=wd: e.tensor_copy(dr[0:1, n0:n0 + wd], banks[cc][0:1, 0:wd]),
                    pe.last, ww[0])
        load(DEG, dr[0:1, :], "deg", a)
        barrier()

    def gat(pre, H, C, eps, XT):
        R0 = S0
        H1o, OUTo = S0 + 8000, S0 + 14600
        B0 = S0 + 21000
        S1 = S0 + 33500
        CW = C + 1
        h1 = at(H1o, T, H, CW) if True else None
        outN = at(OUTo, T, D)
        W, tw = weight(pre + "_W", B0, 2, D)
        ats, ta = param_n(pre + "_att_src", B0 + 512)
        atd, ta = param_n(pre + "_att_dst", B0 + 768)
        asN, as2, adN, mx, u, m, r1, r2 = (at(S1 + i * 200, H, T) for i in range(8))
        one = pool(lambda e: e.memset(h1[:, :, :, C], 1.0))

        def sink(t, ps, a):
            return evac(t, lambda e: e.activation(h1[:, t, :, 0:C], ps.rearrange("p (h c) -> p h c", c=C), ACT.Copy),
                        lambda e: e.tensor_copy(h1[:, t, :, 0:C], ps.rearrange("p (h c) -> p h c", c=C)), a)

        ts = lin_N(XT, 2, W, D, sink, tw)
        tmp = outN.rearrange("p t (h c) -> p t h c", c=C)
        a = None
        for att, dst in ((ats, asN), (atd, adN)):
            for h in range(H):
                a = dve(lambda e, att=att, h=h: e.tensor_tensor(
                    tmp[:, :, h, :], h1[:, :, h, 0:C], bcast(att[:, h * C:(h + 1) * C], T), ALU.mult), ts, ta, a)
            a = dve(lambda e, dst=dst: e.tensor_reduce(dst.rearrange("p h t -> p t h"), tmp, AX, ALU.add), a)
        a = dve(lambda e: e.tensor_scalar(as2, asN, 0.2, None, ALU.mult), a)
        for g in range(H // 4):
            fl = asN[:, 4 * g:4 * g + 4, :].rearrange("p h t -> p (h t)")
            ro = rows_out(fl, 100, 100 * g, B0 + 1024 + 125 * g, "ro", a)
        barrier()
        asr = at(B0, 4, N)
        jk = at(R0, N)
        ml = [at(R0 + 3125 + i * 1563, N, dt=BF16) for i in range(2)]
        for g in range(H // 4):
            for h in range(4):
                l = row_bcast(asr[:, h, :], 100 * g + 25 * h, 0, N, "asr", a if g else None)
            mu = [None, None]
            for j in range(T):
                i = j % 2
                lm = load(ml[i], MK[j * P:(j + 1) * P, :], "mk%d" % i, mu[i])
                for h in range(4):
                    a = dve(lambda e, i=i, h=h, g=g, j=j: e.tensor_tensor_reduce(
                        out=jk, in0=ml[i], in1=asr[:, h, :], scale=1.0, scalar=-3e38, op0=ALU.add, op1=ALU.max,
                        accum_out=mx[:, 4 * g + h, j:j + 1]), lm, l, a)
                mu[i] = a
        a = dve(lambda e: e.tensor_tensor(u, mx, adN, ALU.add), a)
        a = dve(lambda e: e.scalar_tensor_tensor(out=m, in0=u, scalar=0.2, in1=u, op0=ALU.mult, op1=ALU.max), a)
        a = dve(lambda e: e.tensor_tensor(r1, adN, m, ALU.subtract), a)
        a = dve(lambda e: e.scalar_tensor_tensor(out=r2, in0=adN, scalar=0.2, in1=m, op0=ALU.mult, op1=ALU.subtract), a)
        for g in range(H // 4):
            for k, r in enumerate((r1, r2)):
                fl = r[:, 4 * g:4 * g + 4, :].rearrange("p h t -> p (h t)")
                rows_out(fl, 100, 200 * g + 100 * k, B0 + 125 * (2 * g + k), "ro", a)
        barrier()
        Rb = [at(R0 + i * 4000, 2, 4, 500) for i in range(2)]
        Cb = [at(B0 + i * 1250, 5, 500, dt=U16) for i in range(2)]
        Tb = [at(B0 + 2500 + i * 2000, 4, 500) for i in range(2)]
        Xb = [at(B0 + 6500, 4, 500), at(B0 + 8500, 4, 500), at(XN0, 4, 500)]
        AC = [at(B0 + 10500, 4, 500, p=128), at(XN0 + 2000, 4, 500, p=128)]
        rused = [None, None]
        cused = [None, None]
        xused = [None] * 3
        tused = [None, None]
        acused = [None, None]
        it = 0
        rcp = at(S1 + 1600, 4)
        c16v = C16.rearrange("(s p) d -> p s d", p=P)
        steps = [(g, n0, w, s) for g in range(H // 4) for n0, w in CH for s in range(T)]
        lr, lc = {}, {}

        def fetch(n):
            if n >= len(steps):
                return
            g, n0, w, s = steps[n]
            r = n // T
            if s == 0:
                for k in range(2):
                    for h in range(4):
                        lr[r] = row_bcast(Rb[r % 2][:, k, h, 0:w], 200 * g + 100 * k + 25 * h, n0, w,
                                          "rb%d" % (r % 2), rused[r % 2])
            if s % 5 == 0:
                c = n // 5
                lc[c] = load(Cb[c % 2][:, :, 0:w], c16v[:, s:s + 5, n0:n0 + w], "cb%d" % (c % 2), cused[c % 2])

        def exponents(n):
            g, n0, w, s = steps[n]
            r, i, j, jx = n // T, n // T % 2, n % 2, n % 3
            for h in range(4):
                tt = act(lambda e, h=h: e.activation(Tb[j][:, h, 0:w], Rb[i][:, 1, h, 0:w], ACT.Identity,
                                                     bias=as2[:, 4 * g + h, s:s + 1]), lr[r], tused[j])
            for h in range(4):
                x = dve(lambda e, h=h: e.scalar_tensor_tensor(
                    out=Xb[jx][:, h, 0:w], in0=Rb[i][:, 0, h, 0:w], scalar=asN[:, 4 * g + h, s:s + 1],
                    in1=Tb[j][:, h, 0:w], op0=ALU.add, op1=ALU.max), tt, lr[r], xused[jx])
            tused[j] = x
            if s == T - 1:
                rused[i] = [x, tt]
            return x

        def weigh(n, x):
            g, n0, w, s = steps[n]
            r, jx, c = n // T, n % 3, n // 5
            ex = act(lambda e: e.activation(Xb[jx][:, :, 0:w], Xb[jx][:, :, 0:w], ACT.Exp), x)
            pr = dve(lambda e: e.scalar_tensor_tensor(
                out=Xb[jx][:, :, 0:w], in0=Xb[jx][:, :, 0:w], scalar=1.0, in1=bcast(Cb[c % 2][:, s % 5, 0:w], 4),
                op0=ALU.min, op1=ALU.mult), ex, lc[c])
            b0 = 4 * (r % 2)
            for h in range(4):
                a = pe(lambda e, h=h: e.matmul(
                    banks[b0 + h][0:CW, 0:w], h1[:, s, 4 * g + h, :], Xb[jx][:, h, 0:w],
                    start=(s == 0), stop=(s == T - 1)), pr, free[b0 + h])
            xused[jx] = a
            cused[c % 2] = pr
            if s == T - 1:
                divide(g, n0, w, r, a)

        def divide(g, n0, w, r, a):
            b0 = 4 * (r % 2)
            ac = AC[r % 2]
            cp = [act(lambda e, h=h: e.activation(ac[0:CW, h, 0:w], banks[b0 + h][0:CW, 0:w], ACT.Copy),
                      a, acused[r % 2]) for h in range(4)]
            for k in range(w // P):
                t = n0 // P + k
                b = b0 + k
                for h in range(4):
                    a = pe(lambda e, h=h, k=k, b=b: e.transpose(
                        banks[b][0:P, h * CW:(h + 1) * CW], ac[0:CW, h, k * P:(k + 1) * P],
                        ident[0:CW, 0:CW]), cp, inc=(h == 3))
                v = banks[b][0:P, 0:4 * CW].rearrange("p (h c) -> p h c", c=CW)
                z = dve(lambda e, v=v: e.tensor_scalar(rcp, v[:, :, C], eps, None, ALU.add), a, dve.last)
                z = dve(lambda e: e.reciprocal(rcp, rcp), z)
                o = outN[:, t, 4 * g * C:4 * (g + 1) * C].rearrange("p (h c) -> p h c", c=C)
                free[b] = dve(lambda e, v=v, o=o: e.tensor_tensor(o, v[:, :, 0:C], bcast(rcp, C, 2), ALU.mult), z)
            for k in range(w // P, 4):
                free[b0 + k] = cp
            acused[r % 2] = a

        fetch(0)
        xs = {}
        for n in range(len(steps) + 1):
            if n < len(steps):
                xs[n] = exponents(n)
            if n:
                weigh(n - 1, xs[n - 1])
            if n + 1 < len(steps):
                fetch(n + 1)
        barrier()
        bi, t1 = param_n(pre + "_bias", B0)
        ga, t1 = param_n(pre + "_gamma", B0 + 256)
        be, t1 = param_n(pre + "_beta", B0 + 512)
        a = dve(lambda e: e.tensor_tensor(outN, outN, bcast(bi, T), ALU.add), t1)
        nt = norm_tiles(outN, outN, a)
        a = dve(lambda e: e.tensor_tensor(outN, outN, bcast(ga, T), ALU.mult), nt)
        a = dve(lambda e: e.tensor_tensor(outN, outN, bcast(be, T), ALU.add), a)
        dve(lambda e: e.tensor_tensor(X, X, outN, ALU.add), a)
        barrier()

    def mix_ln(XT, Wq, bq, Wk, bk, Wv, bv, gk, bk2, gv, bv2, heads, tail):
        A0 = S0 + 6250
        kN, vN, tm = (at(A0 + i * 6400, T, D) for i in range(3))
        o = A0 + 19200
        c = D // heads
        mask = bmask32 if c == 32 else bmask64
        wq, tq = weight(Wq, o, 2, D)
        wk, tk = weight(Wk, o + 512, 2, D)
        wv, tv = weight(Wv, o + 1024, 2, D)
        o += 1536
        small = o
        o += 600
        prm = []
        for nme in (gk, bk2, gv, bv2):
            v, t1 = param_n(nme, o, c)
            prm.append(v)
            o += c
        bkn = bvn = bqt = None
        if bq is not None:
            bkn, t1 = param_n(bk, o)
            bvn, t1 = param_n(bv, o + 256)
            bqt, t1 = param_t(bq, o + 512)
        o += 520
        kvs = at(o, 2, 128, p=128)
        o += 256

        def sink_for(dst, bn):
            def sink(t, ps, a):
                if bn is not None:
                    return dve(lambda e: e.tensor_tensor(dst[:, t, :], ps, bn, ALU.add), a, t1)
                return copy_out(t, dst[:, t, :], ps, a)
            return sink

        tk2 = lin_N(XT, 2, wk, D, sink_for(kN, bkn), tk, tv)
        tv2 = lin_N(XT, 2, wv, D, sink_for(vN, bvn), tv)
        a = head_norm(kN, tm, small, heads, prm[0], prm[1], tk2, t1)
        a = head_norm(vN, tm, small, heads, prm[2], prm[3], tv2, a)
        bk_ = [bank(), bank()]
        for k in range(2):
            b = bk_[k]
            for t in range(T):
                m = pe(lambda e, b=b, k=k, t=t: e.matmul(
                    banks[b][:, 0:128], kN[:, t, k * 128:(k + 1) * 128], vN[:, t, k * 128:(k + 1) * 128],
                    start=(t == 0), stop=(t == T - 1)), a, free[b], inc=(t == T - 1))
            free[b] = dve(lambda e, b=b, k=k: e.scalar_tensor_tensor(
                out=kvs[:, k, :], in0=banks[b][:, 0:128], scalar=1.0 / N, in1=mask, op0=ALU.mult, op1=ALU.mult), m)
        kt = free[bk_[1]]
        qc = [at(A0 + i * 1000, 2, 500, p=128) for i in range(2)]
        qused = [None, None]
        for ci, (n0, w) in enumerate(CH):
            i = ci % 2
            ql = []
            for oo in range(2):
                b = bank()
                for kk in range(2):
                    a = pe(lambda e, b=b, oo=oo, kk=kk, n0=n0, w=w: e.matmul(
                        banks[b][:, 0:w], wq[:, kk, oo * 128:(oo + 1) * 128], XT[:, kk, n0:n0 + w],
                        start=(kk == 0), stop=(kk == 1)), free[b], tq, inc=(kk == 1))
                if bqt is not None:
                    free[b] = act(lambda e, b=b, oo=oo, i=i, w=w: e.activation(
                        qc[i][:, oo, 0:w], banks[b][:, 0:w], ACT.Identity, bias=bqt[:, oo:oo + 1]), a, kt, qused[i])
                else:
                    free[b] = act(lambda e, b=b, oo=oo, i=i, w=w: e.activation(
                        qc[i][:, oo, 0:w], banks[b][:, 0:w], ACT.Copy), a, kt, qused[i])
                ql.append(free[b])
            qused[i] = tail(ci, n0, w, qc[i], kvs, ql, o)
        barrier()

    def l0_mix(XT):
        w1, t1 = weight("L0_mix_w1", S0 + 30000, 2, D)
        w2, t1 = weight("L0_mix_w2", S0 + 30512, 2, D)
        b1, t1 = param_t("L0_mix_b1", S0 + 31024)
        b2, t2 = param_n("L0_mix_b2", S0 + 31040)
        rc = [at(S0 + 31300 + i * 1000, 2, 500, p=128) for i in range(2)]
        hc = [at(S0 + 33300 + i * 1000, 2, 500, p=128) for i in range(2)]
        rused = [None, None]
        hused = [None, None]

        def tail(ci, n0, w, q, kvs, ql, o):
            assert o <= S0 + 30000
            i = ci % 2
            rl = []
            for k in range(2):
                b = bank()
                a = pe(lambda e, b=b, k=k: e.matmul(banks[b][:, 0:w], kvs[:, k, :], q[:, k, 0:w], start=True,
                                                    stop=True), free[b], ql)
                free[b] = dve(lambda e, b=b, k=k: e.tensor_tensor(rc[i][:, k, 0:w], banks[b][:, 0:w],
                                                                  XT[:, k, n0:n0 + w], ALU.add), a, rused[i])
                rl.append(free[b])
            done = a
            hl = []
            for oo in range(2):
                b = bank()
                for k in range(2):
                    a = pe(lambda e, b=b, k=k, oo=oo: e.matmul(
                        banks[b][:, 0:w], w1[:, k, oo * 128:(oo + 1) * 128], rc[i][:, k, 0:w],
                        start=(k == 0), stop=(k == 1)), free[b], rl, t1, inc=(k == 1))
                free[b] = act(lambda e, b=b, oo=oo: e.activation(
                    hc[i][:, oo, 0:w], banks[b][:, 0:w], ACT.Gelu, bias=b1[:, oo:oo + 1]), a, t2, hused[i])
                hl.append(free[b])
            rused[i] = a
            for j in range(w // P):
                t = n0 // P + j
                b = bank()
                for k in range(2):
                    a = pe(lambda e, b=b, k=k, j=j: e.matmul(
                        banks[b][0:P, 0:D], hc[i][:, k, j * P:(j + 1) * P], w2[:, k, :],
                        start=(k == 0), stop=(k == 1)), free[b], hl, inc=(k == 1))
                free[b] = dve(lambda e, b=b, t=t: e.tensor_tensor(X[:, t, :], banks[b][0:P, 0:D], X[:, t, :],
                                                                  ALU.add), a)
            hused[i] = a
            return done

        a = dve(lambda e: e.tensor_tensor(X, X, XN, ALU.add))
        a = dve(lambda e: e.tensor_tensor(X, X, bcast(b2, T), ALU.add), a, t2)
        dve.wait(a)
        mix_ln(XT, "wq0", "bq0", "wk0", "bk0", "wv0", "bv0", "L0_mix_kln_g", "L0_mix_kln_b",
               "L0_mix_vln_g", "L0_mix_vln_b", 8, tail)

    def l3_mix(XT):
        wo, t1 = weight("woT", S0 + 30000, 2, D)
        bo, t2 = param_n("L3_mix_bo", S0 + 31040)
        rc = [at(S0 + 31300 + i * 1000, 2, 500, p=128) for i in range(2)]
        rused = [None, None]

        def tail(ci, n0, w, q, kvs, ql, o):
            assert o <= S0 + 30000
            i = ci % 2
            rl = []
            for k in range(2):
                b = bank()
                a = pe(lambda e, b=b, k=k: e.matmul(banks[b][:, 0:w], kvs[:, k, :], q[:, k, 0:w], start=True,
                                                    stop=True), free[b], ql)
                free[b] = dve(lambda e, b=b, k=k: e.tensor_copy(rc[i][:, k, 0:w], banks[b][:, 0:w]), a, rused[i])
                rl.append(free[b])
            done = a
            for j in range(w // P):
                t = n0 // P + j
                b = bank()
                for k in range(2):
                    a = pe(lambda e, b=b, k=k, j=j: e.matmul(
                        banks[b][0:P, 0:D], rc[i][:, k, j * P:(j + 1) * P], wo[:, k, :],
                        start=(k == 0), stop=(k == 1)), free[b], rl, t1, inc=(k == 1))
                free[b] = dve(lambda e, b=b, t=t: e.tensor_tensor(X[:, t, :], banks[b][0:P, 0:D], X[:, t, :],
                                                                  ALU.add), a)
            rused[i] = a
            return done

        a = dve(lambda e: e.tensor_tensor(X, X, bcast(bo, T), ALU.add), t2)
        dve.wait(a)
        mix_ln(XT, "wqT", None, "wkT", None, "wvT", None, "L3_mix_ln_k_g", "L3_mix_ln_k_b",
               "L3_mix_ln_v_g", "L3_mix_ln_v_b", 4, tail)

    def l1_mix(XT):
        o = S0 + 6250
        W, tw = weight("L1_mix_W_qkv", o, 2, 384)
        o += 768
        Wo = at(o, D, p=128)
        tw = load(Wo, inp["L1_mix_W_out"], None)
        o += 256
        bo, tb = param_n("L1_mix_b_out", o)
        o += 256
        kT = at(o, N, p=128)
        o += 3125
        kN = at(o, T, 128)
        o += 3200
        vN = at(o, T, 128)
        o += 3200
        ctx_ = at(o, 128, p=128)
        o += 128
        sm = at(o, 8, p=128)
        o += 8
        qc = [at(o + i * 500, 500, p=128) for i in range(2)]
        o += 1000
        oc = [at(o + i * 500, 500, p=128) for i in range(2)]
        o += 1000
        assert o <= K0
        a = dve(lambda e: e.tensor_tensor(X, X, bcast(bo, T), ALU.add), tb)
        dve.wait(a)
        last = []
        for ci, (n0, w) in enumerate(CH):
            b = bank()
            for kk in range(2):
                a = pe(lambda e, b=b, kk=kk, n0=n0, w=w: e.matmul(
                    banks[b][:, 0:w], W[:, kk, 128:256], XT[:, kk, n0:n0 + w], start=(kk == 0), stop=(kk == 1)),
                    free[b], tw, inc=(kk == 1))
            free[b] = copy_out(ci, kT[:, n0:n0 + w], banks[b][:, 0:w], a)
            last.append(free[b])
        a = dve(lambda e: e.tensor_reduce(sm[:, 0:1], kT, AX, ALU.max, negate=True), last)
        ek = act(lambda e: e.activation(kT, kT, ACT.Exp, bias=sm[:, 0:1], accum_out=sm[:, 1:2]), a)
        rr = dve(lambda e: e.reciprocal(sm[:, 2:3], sm[:, 1:2]), ek)
        rr = dve(lambda e: e.tensor_scalar(sm[:, 2:3], sm[:, 2:3], 32.0 ** -0.5, None, ALU.mult), rr)

        def sinkv(t, ps, a):
            return copy_out(t, vN[:, t, :], ps, a)

        tv = lin_N(XT, 2, W, 128, sinkv, tw, f0=256)
        tk = []
        for t in range(T):
            b = bank()
            a = pe(lambda e, t=t, b=b: e.transpose(banks[b][0:P, 0:128], kT[:, t * P:(t + 1) * P], ident[:, :]),
                   ek, free[b])
            free[b] = copy_out(t, kN[:, t, :], banks[b][0:P, 0:128], a)
            tk.append(free[b])
        b = bank()
        for t in range(T):
            a = pe(lambda e, t=t, b=b: e.matmul(banks[b][:, 0:128], kN[:, t, :], vN[:, t, :], start=(t == 0),
                                                stop=(t == T - 1)), free[b], tk, tv, inc=(t == T - 1))
        free[b] = dve(lambda e, b=b: e.scalar_tensor_tensor(
            out=ctx_, in0=banks[b][:, 0:128], scalar=sm[:, 2:3], in1=bmask32, op0=ALU.mult, op1=ALU.mult), a, rr)
        ct = free[b]
        qu, ou = [None, None], [None, None]
        for ci, (n0, w) in enumerate(CH):
            i = ci % 2
            b = bank()
            for kk in range(2):
                a = pe(lambda e, b=b, kk=kk, n0=n0, w=w: e.matmul(
                    banks[b][:, 0:w], W[:, kk, 0:128], XT[:, kk, n0:n0 + w], start=(kk == 0), stop=(kk == 1)),
                    free[b], inc=(kk == 1))
            free[b] = q1 = act(lambda e, b=b, i=i, w=w: e.activation(qc[i][:, 0:w], banks[b][:, 0:w], ACT.Copy), a, qu[i])
            b = bank()
            a = pe(lambda e, b=b, i=i, w=w: e.matmul(banks[b][:, 0:w], ctx_, qc[i][:, 0:w], start=True, stop=True),
                   q1, ct, free[b])
            qu[i] = a
            free[b] = o1 = act(lambda e, b=b, i=i, w=w: e.activation(oc[i][:, 0:w], banks[b][:, 0:w], ACT.Copy), a, ou[i])
            for j in range(w // P):
                t = n0 // P + j
                b = bank()
                a = pe(lambda e, b=b, i=i, j=j: e.matmul(banks[b][0:P, 0:D], oc[i][:, j * P:(j + 1) * P], Wo,
                                                         start=True, stop=True), o1, free[b])
                free[b] = dve(lambda e, b=b, t=t: e.tensor_tensor(X[:, t, :], banks[b][0:P, 0:D], X[:, t, :],
                                                                  ALU.add), a)
            ou[i] = a
        barrier()

    def l2_mix(XT):
        o = S0 + 6250
        W, tw = weight("L2_mix_W_qkv", o, 2, 768)
        o += 1536
        Wo, tw = weight("L2_mix_W_out", o, 2, D)
        o += 512
        bqkv = at(o, 768)
        load(bqkv, inp["L2_mix_b_qkv"].partition_broadcast(P), None)
        o += 768
        bo, tb = param_n("L2_mix_b_out", o)
        o += 256
        bvt, tb = param_t("L2_mix_b_qkv", o, src=inp["L2_mix_b_qkv"][512:768])
        o += 2
        kN, vN = (at(o + i * 6400, T, D) for i in range(2))
        o += 12800
        q2T = at(o, 2, N, p=128)
        o += 6250
        kv = at(o, 2, D, p=128)
        o += 512
        cn = at(o, 8, p=128)
        o += 8
        sm = [at(o + i * 25, T) for i in range(6)]
        o += 150
        sq = at(o, 2, D)
        o += 512
        assert o <= K0 - 2000, o
        vc = [at(o + i * 1000, 2, 500, p=128) for i in range(2)]
        a = dve(lambda e: e.tensor_tensor(X, X, bcast(bo, T), ALU.add), tb)
        dve.wait(a)

        def sink_for(dst, f):
            def sink(t, ps, a):
                return dve(lambda e: e.tensor_tensor(dst[:, t, :], ps, bqkv[:, f:f + D], ALU.add), a, tb)
            return sink

        def squares(v, ready):
            vf = v
            a = dve(lambda e: e.tensor_reduce(sm[0], vf, AX, ALU.add), ready)
            a = dve(lambda e: e.tensor_scalar(sm[0], sm[0], 1.0 / D, None, ALU.mult), a)
            a = dve(lambda e: e.tensor_tensor(vf, vf, bcast(sm[0], D, 2), ALU.subtract), a)
            a = act(lambda e: e.activation(vf, vf, ACT.Square), a)
            a = dve(lambda e: e.tensor_reduce(sm[1], vf, AX, ALU.add), a)
            a = dve(lambda e: e.tensor_scalar(sm[1], sm[1], 1e-7, None, ALU.add), a)
            a = dve(lambda e: e.reciprocal(sm[1], sm[1]), a)
            return dve(lambda e: e.tensor_tensor(vf, vf, bcast(sm[1], D, 2), ALU.mult), a)

        tq = lin_N(XT, 2, W, D, sink_for(vN, 0), tw, f0=0)
        a = squares(vN, tq)
        for t in range(T):
            a = dve(lambda e, t=t: e.scalar_tensor_tensor(out=sq[:, 0, :], in0=vN[:, t, :], scalar=1.0,
                                                          in1=vN[:, t, :], op0=ALU.mult, op1=ALU.mult,
                                                          accum_out=sm[2][:, t:t + 1]), a)
        a = act(lambda e: e.activation(sm[3], sm[2], ACT.Sqrt), a)
        a = dve(lambda e: e.tensor_scalar(sm[3], sm[3], 1e-12, None, ALU.max), a)
        a = dve(lambda e: e.reciprocal(sm[3], sm[3]), a)
        a = dve(lambda e: e.tensor_tensor(vN, vN, bcast(sm[3], D, 2), ALU.mult), a)
        qt = to_T(vN, q2T, a)
        tk = lin_N(XT, 2, W, D, sink_for(kN, D), f0=D)
        ka = squares(kN, [tk, a])
        dve.wait(qt, pe.last)
        tv = lin_N(XT, 2, W, D, sink_for(vN, 2 * D), f0=2 * D)
        b0, b1, b2 = bank(), bank(), bank()
        su = [None, None]
        for t in range(T):
            i = t % 2
            s_ = dve(lambda e, t=t, i=i: e.tensor_tensor(sq[:, i, :], kN[:, t, :], kN[:, t, :], ALU.mult), ka, su[i])
            for k in range(2):
                a = pe(lambda e, k=k, t=t, b=(b0, b1)[k]: e.matmul(banks[b][:, 0:D], kN[:, t, k * 128:(k + 1) * 128],
                                                                 vN[:, t, :], start=(t == 0), stop=(t == T - 1)),
                       ka, tv, free[(b0, b1)[k]])
            a = pe(lambda e, t=t, i=i: e.matmul(banks[b2][0:1, 0:D], ones[0:P, 0:1], sq[:, i, :], start=(t == 0),
                                                stop=(t == T - 1)), s_, free[b2])
            su[i] = a
        rowt = sq[0:1, 0, :]
        r = dve(lambda e: e.tensor_copy(rowt, banks[b2][0:1, 0:D]), a)
        free[b2] = r
        b3 = bank()
        for k in range(2):
            a = pe(lambda e, k=k: e.matmul(banks[b3][:, k:k + 1], sq[0:1, 0, k * 128:(k + 1) * 128], ones[0:1, 0:1],
                                           start=True, stop=True), r, free[b3])
        r = dve(lambda e: e.tensor_copy(cn[:, 0:2], banks[b3][:, 0:2]), a)
        free[b3] = r
        r = act(lambda e: e.activation(cn[:, 0:2], cn[:, 0:2], ACT.Sqrt), r)
        r = dve(lambda e: e.tensor_scalar(cn[:, 0:2], cn[:, 0:2], 1e-12, None, ALU.max), r)
        r = dve(lambda e: e.reciprocal(cn[:, 2:4], cn[:, 0:2]), r)
        r = dve(lambda e: e.tensor_scalar(cn[:, 4:6], cn[:, 2:4], float(N) ** -0.5, None, ALU.mult), r)
        for k, b in enumerate((b0, b1)):
            free[b] = r = dve(lambda e, k=k, b=b: e.tensor_scalar(kv[:, k, :], banks[b][:, 0:D], cn[:, 4 + k:5 + k],
                                                                  None, ALU.mult), r, a)
        vu = [None, None]
        for ci, (n0, w) in enumerate(CH):
            i = ci % 2
            al = []
            for oo in range(2):
                b = bank()
                for kk in range(4):
                    lhs = (kv[:, kk, oo * 128:(oo + 1) * 128] if kk < 2
                           else W[:, kk - 2, 512 + oo * 128:512 + (oo + 1) * 128])
                    rhs = q2T[:, kk, n0:n0 + w] if kk < 2 else XT[:, kk - 2, n0:n0 + w]
                    a = pe(lambda e, b=b, lhs=lhs, rhs=rhs, kk=kk, w=w: e.matmul(
                        banks[b][:, 0:w], lhs, rhs, start=(kk == 0), stop=(kk == 3)), free[b], r, qt, inc=(kk == 3))
                free[b] = act(lambda e, b=b, oo=oo, i=i, w=w: e.activation(
                    vc[i][:, oo, 0:w], banks[b][:, 0:w], ACT.Identity, bias=bvt[:, oo:oo + 1]), a, vu[i])
                al.append(free[b])
            for j in range(w // P):
                t = n0 // P + j
                b = bank()
                for k in range(2):
                    a = pe(lambda e, b=b, k=k, j=j, i=i: e.matmul(
                        banks[b][0:P, 0:D], vc[i][:, k, j * P:(j + 1) * P], Wo[:, k, :],
                        start=(k == 0), stop=(k == 1)), free[b], al, inc=(k == 1))
                free[b] = dve(lambda e, b=b, t=t: e.tensor_tensor(X[:, t, :], banks[b][0:P, 0:D], X[:, t, :],
                                                                  ALU.add), a)
            vu[i] = a
        barrier()

    picks = []
    SLOTS, NT = 250, 32
    XS = dd("XS", [SLOTS * NT, D])
    YS = dd("YS", [SLOTS * NT, D])
    upper = at(PV, P)
    k250 = at(PV + 125, T)
    kj = at(PV + 150, NT)
    kti = at(PV + 182, NT, dt=I32)

    def expert_consts():
        a = pool(lambda e: e.memset(upper, 1.0))
        pool(lambda e: e.affine_select(out=upper, in_=upper, compare_op=ALU.is_gt, fill=0.0, base=0,
                                       pattern=[[1, P]], channel_multiplier=-1), a)
        a = pool(lambda e: e.iota(kti, pattern=[[1, NT]], base=0, channel_multiplier=0))
        a = dve(lambda e: e.tensor_copy(kj, kti), a)
        dve(lambda e: e.tensor_scalar(k250, kj[:, 0:T], 250.0, None, ALU.mult), a)
        z = at(S0, 16384, p=P)
        a = dve(lambda e: e.memset(z, 0.0))
        load(XS.rearrange("(a p) f -> p a f", p=P)[:, 0:NT, :], z[:, 0:NT * D].rearrange("p (a f) -> p a f", f=D),
             "xz", a)
        load(XS.rearrange("(a p) f -> p a f", p=P)[:, NT:2 * NT, :],
             z[:, 0:NT * D].rearrange("p (a f) -> p a f", f=D), "xz", a)
        barrier()
    def top2(V, o):
        m1, eq, x1, o1, V2, sel = at(o, T), at(o + 25, T, 8), at(o + 225, T), at(o + 250, T, 8), at(o + 450, T, 8), \
            at(o + 650, T, 8)
        w8 = bcast(iota8, T)
        a = dve.last
        src = V
        for r in range(2):
            dst = sel if r == 0 else o1
            mm_ = m1 if r == 0 else x1
            a = dve(lambda e, src=src, mm_=mm_: e.tensor_reduce(mm_, src, AX, ALU.max), a)
            a = dve(lambda e, src=src, mm_=mm_: e.tensor_tensor(eq, src, bcast(mm_, 8, 2), ALU.is_equal), a)
            a = dve(lambda e: e.tensor_tensor(eq, eq, w8, ALU.mult), a)
            a = dve(lambda e: e.tensor_reduce(x1, eq, AX, ALU.max), a)
            a = dve(lambda e, dst=dst: e.tensor_tensor(dst, eq, bcast(x1, 8, 2), ALU.is_equal), a)
            if r == 0:
                a = dve(lambda e: e.scalar_tensor_tensor(out=V2, in0=sel, scalar=-3e38, in1=V, op0=ALU.mult,
                                                         op1=ALU.add), a)
                src = V2
        a = dve(lambda e: e.tensor_tensor(V2, sel, o1, ALU.add), a)
        picks[:] = [sel, o1, V2]
        return V2, m1, a

    def gate(XT, Wg, biases, kind, o, L, cw):
        W = at(o, 2, 8, p=128)
        t0 = dma(sp, None, None, None, make=lambda e: e.dma_start(
            W, inp[Wg].rearrange("(k p) f -> p k f", p=128)))
        bs = []
        for i, nme in enumerate(biases):
            v, t0 = param_n(nme, o + 16 + 8 * i, 8)
            bs.append(v)
        b = bank()
        for t in range(T):
            for k in range(2):
                a = pe(lambda e, t=t, k=k: e.matmul(banks[b][0:P, t * 8:t * 8 + 8], XT[:, k, t * P:(t + 1) * P],
                                                    W[:, k, :], start=(k == 0), stop=(k == 1)), t0, free[b],
                       inc=(k == 1 and t == T - 1))
        ps = banks[b][0:P, 0:200].rearrange("p (t e) -> p t e", e=8)
        for i, v in enumerate(bs):
            a = dve(lambda e, i=i, v=v: e.tensor_tensor(L, ps if i == 0 else L, bcast(v, T), ALU.add), a)
            if i == 0:
                free[b] = a
        w0 = o + 64
        mx, s = at(w0, T), at(w0 + 25, T)
        if kind != "two":
            a = dve(lambda e: e.tensor_reduce(mx, L, AX, ALU.max), a)
            a = dve(lambda e: e.tensor_tensor(L, L, bcast(mx, 8, 2), ALU.subtract), a)
            a = act(lambda e: e.activation(L, L, ACT.Exp), a)
            a = dve(lambda e: e.tensor_reduce(s, L, AX, ALU.add), a)
            a = dve(lambda e: e.reciprocal(s, s), a)
            a = dve(lambda e: e.tensor_tensor(L, L, bcast(s, 8, 2), ALU.mult), a)
            sel, m1, a = top2(L, w0 + 50)
            a = dve(lambda e: e.tensor_tensor(cw, L, sel, ALU.mult), a)
        else:
            sel, m1, a = top2(L, w0 + 50)
            a = dve(lambda e: e.tensor_tensor(L, L, bcast(m1, 8, 2), ALU.subtract), a)
            a = act(lambda e: e.activation(L, L, ACT.Exp), a)
            a = dve(lambda e: e.tensor_tensor(cw, L, sel, ALU.mult), a)
        if kind != "all":
            a = dve(lambda e: e.tensor_reduce(s, cw, AX, ALU.add), a)
            a = dve(lambda e: e.reciprocal(s, s), a)
            a = dve(lambda e: e.tensor_tensor(cw, cw, bcast(s, 8, 2), ALU.mult), a)
        return a

    def ffn(XT, pre, hid, fn, kind, Wg, biases, affine=False, again=False):
        hp = hid // 128
        WCn = 2 * hid + hp * D + hp + (4 if affine else 0)
        pack = inp[pre + "_pack"]
        o = S0 + 6250
        L, cw = at(o, T, 8), at(o + 200, T, 8)
        small = o + 400
        b2a = at(o + 1500, D, p=8)
        o += 1756
        cT = [at(o + i * 125, P, p=8) for i in range(2)]
        o += 250
        R, TO, OF, TM = (at(o + i * 200, T, 8) for i in range(4))
        o += 800
        cnt, tl, st = at(o, 8), at(o + 8, 8), at(o + 16, 8)
        CM = at(o + 24, 8, T)
        o += 224
        sl = [at(o + i * 25, T) for i in range(2)]
        sli = [at(o + 50 + i * 25, T, dt=I32) for i in range(2)]
        wi = [at(o + 100 + i * 25, T) for i in range(2)]
        o += 150
        ei, eii = at(o, NT), at(o + NT, NT, dt=I32)
        o += 2 * NT
        W = [at(o + i * WCn, WCn, p=128) for i in range(3)]
        o += 3 * WCn
        XR = [at(o + i * 512, 2, D) for i in range(3)]
        o += 1536
        XE = [at(o + i * 500, 2, SLOTS, p=128) for i in range(2)]
        o += 1000
        Hb = [at(o + i * hp * SLOTS, hp, SLOTS, p=128) for i in range(2)]
        o += 2 * hp * SLOTS
        Y = [at(o + i * 512, 2, D) for i in range(2)]
        o += 1024
        GB = [at(o + i * D, D) for i in range(8)]
        o += 8 * D
        assert o <= K0, o
        tb = load(b2a, inp[pre + "_b2"], None)
        g = gate(XT, Wg, biases, kind, small, L, cw)
        one, two, both = picks
        ready = norm_tiles(XN, XN, g) if again else None
        bu, b_ = bank(), bank()
        a = pe(lambda e: e.matmul(banks[bu][0:P, 0:200], upper, both.rearrange("p t e -> p (t e)"), start=True,
                                  stop=True), g, free[bu])
        c = pe(lambda e: e.matmul(banks[b_][0:P, 0:200], ones[0:P, 0:P], both.rearrange("p t e -> p (t e)"),
                                  start=True, stop=True), g, free[b_])
        free[bu] = dve(lambda e: e.tensor_copy(R.rearrange("p t e -> p (t e)"), banks[bu][0:P, 0:200]), a)
        free[b_] = dve(lambda e: e.tensor_copy(TO.rearrange("p t e -> p (t e)"), banks[b_][0:P, 0:200]), c)
        a = dve(lambda e: e.memset(OF[:, 0, :], 0.0), free[b_])
        for t in range(1, T):
            a = dve(lambda e, t=t: e.tensor_tensor(OF[:, t, :], OF[:, t - 1, :], TO[:, t - 1, :], ALU.add), a)
        a = dve(lambda e: e.tensor_tensor(cnt, OF[:, T - 1, :], TO[:, T - 1, :], ALU.add), a)
        a = dve(lambda e: e.tensor_tensor(CM, bcast(cnt, T, 2), bcast(k250, 8), ALU.is_gt), a)
        a = dve(lambda e: e.tensor_reduce(tl, CM, AX, ALU.add), a)
        a = dve(lambda e: e.memset(st[:, 0:1], 0.0), a)
        for e8 in range(1, 8):
            a = dve(lambda e, i=e8: e.tensor_tensor(st[:, i:i + 1], st[:, i - 1:i], tl[:, i - 1:i], ALU.add), a)
        a = dve(lambda e: e.memset(ei, 0.0), a)
        for e8 in range(1, 8):
            a = dve(lambda e, i=e8: e.scalar_tensor_tensor(out=ei, in0=kj, scalar=st[:, i:i + 1], in1=ei,
                                                           op0=ALU.is_ge, op1=ALU.add), a)
        te = dve(lambda e: e.tensor_copy(eii, ei), a)
        a = dve(lambda e: e.tensor_tensor(R, R, OF, ALU.add), te)
        a = dve(lambda e: e.scalar_tensor_tensor(out=R, in0=bcast(st, T), scalar=float(SLOTS), in1=R, op0=ALU.mult,
                                                 op1=ALU.add), a)
        for i, pick in enumerate((one, two)):
            a = dve(lambda e, pick=pick: e.tensor_tensor(TM, pick, R, ALU.mult), a)
            a = dve(lambda e, i=i: e.tensor_reduce(sl[i], TM, AX, ALU.add), a)
            a = dve(lambda e, i=i: e.tensor_copy(sli[i], sl[i]), a)
        ts = a
        for i, pick in enumerate((one, two)):
            a = dve(lambda e, pick=pick: e.tensor_tensor(TM, pick, cw, ALU.mult), a)
            a = dve(lambda e, i=i: e.tensor_reduce(wi[i], TM, AX, ALU.add), a)
        tw = a
        for t in range(T):
            for i in range(2):
                xs = dma(pool, None, None, "xs", ts, ready[t] if ready else None,
                         make=lambda e, t=t, i=i: e.indirect_dma_start(
                             out=XS[:, :], out_offset=bass.IndirectOffsetOnAxis(ap=sli[i][:, t:t + 1], axis=0),
                             in_=XN[:, t, :], in_offset=None))
        wused, xused, lw, lx = [None] * 3, [None] * 3, {}, {}

        def weights(k):
            i = k % 3

            def make(e):
                v = e.value_load(eii[0:1, k:k + 1], min_val=0, max_val=7)
                return e.dma_start(W[i], pack[bass.ds(v, 1), :, :].rearrange("o p f -> p (o f)"))
            lw[k] = dma(sp, None, None, "w%d" % i, te, wused[i], make=make)

        def nodes(k):
            i = k % 3
            lx[k] = load(XR[i], XS[k * SLOTS:(k + 1) * SLOTS, :].rearrange("(j p) f -> p j f", p=P), "xr%d" % i,
                         xs, xused[i])

        for k in range(3):
            weights(k)
        cu = [None, None]
        for t in range(T):
            i = t % 2
            b = bank()
            a = pe(lambda e, t=t, b=b: e.transpose(banks[b][0:8, 0:P], cw[:, t, :], ident[0:P, 0:P]), g, free[b])
            free[b] = c = act(lambda e, b=b, i=i: e.activation(cT[i], banks[b][0:8, 0:P], ACT.Copy), a, cu[i])
            b = bank()
            a = pe(lambda e, b=b, i=i: e.matmul(banks[b][0:P, 0:D], cT[i], b2a, start=True, stop=True), c, tb, free[b])
            cu[i] = a
            free[b] = xd = dve(lambda e, b=b, t=t: e.tensor_tensor(X[:, t, :], banks[b][0:P, 0:D], X[:, t, :],
                                                                  ALU.add), a)
        for k in range(3):
            nodes(k)
        eu, hu, yu, hd = [None, None], [None, None], [None, None], {}

        def hidden(k):
            i, j3 = k % 2, k % 3
            w = W[j3]
            w1 = w[:, 0:2 * hid].rearrange("p (k f) -> p k f", k=2)
            b1 = w[:, 2 * hid + hp * D:2 * hid + hp * D + hp]
            bt = bank()
            for kk in range(2):
                for j in range(2):
                    a = pe(lambda e, kk=kk, j=j: e.transpose(
                        banks[bt][:, kk * SLOTS + j * P:kk * SLOTS + (j + 1) * P], XR[j3][:, j, kk * 128:(kk + 1) * 128],
                        ident[0:P, 0:P]), lx[k], free[bt], inc=(kk == 1 and j == 1))
            xused[j3] = a
            if affine:
                gb = w[:, WCn - 4:WCn]
                xl = [dve(lambda e, kk=kk: e.tensor_scalar(
                    XE[i][:, kk, :], banks[bt][:, kk * SLOTS:(kk + 1) * SLOTS], gb[:, kk:kk + 1], gb[:, 2 + kk:3 + kk],
                    ALU.mult, ALU.add), a, lw[k], eu[i]) for kk in range(2)]
            else:
                xl = [dve(lambda e: e.tensor_copy(XE[i].rearrange("p k f -> p (k f)"), banks[bt][:, 0:500]), a, eu[i])]
            free[bt] = xl
            if k + 3 < NT:
                nodes(k + 3)
            hl = []
            for oo in range(hp):
                b = bank()
                for kk in range(2):
                    a = pe(lambda e, b=b, oo=oo, kk=kk: e.matmul(
                        banks[b][:, 0:SLOTS], w1[:, kk, oo * 128:(oo + 1) * 128], XE[i][:, kk, :],
                        start=(kk == 0), stop=(kk == 1)), free[b], lw[k], xl, inc=(kk == 1))
                free[b] = act(lambda e, b=b, oo=oo: e.activation(
                    Hb[i][:, oo, :], banks[b][:, 0:SLOTS], fn, bias=b1[:, oo:oo + 1]), a, lw[k], hu[i])
                hl.append(free[b])
            eu[i] = a
            hd[k] = hl

        def outputs(k):
            i = k % 2
            w2 = W[k % 3][:, 2 * hid:2 * hid + hp * D].rearrange("p (k f) -> p k f", k=hp)
            b = bank()
            for j in range(2):
                for kk in range(hp):
                    a = pe(lambda e, b=b, kk=kk, j=j: e.matmul(
                        banks[b][0:P, j * D:(j + 1) * D], Hb[i][:, kk, j * P:(j + 1) * P], w2[:, kk, :],
                        start=(kk == 0), stop=(kk == hp - 1)), free[b], hd[k], inc=(kk == hp - 1 and j == 1))
            hu[i] = wused[k % 3] = a
            free[b] = c = dve(lambda e, b=b: e.tensor_copy(Y[i].rearrange("p j f -> p (j f)"), banks[b][0:P, 0:512]),
                              a, yu[i])
            yu[i] = dma(pool, YS[k * SLOTS:(k + 1) * SLOTS, :].rearrange("(j p) f -> p j f", p=P), Y[i],
                        "ys%d" % i, c)
            if k + 3 < NT:
                weights(k + 3)

        for k in range(NT + 1):
            if k < NT:
                hidden(k)
            if k:
                outputs(k - 1)
        gu = [None] * 8
        n = 0
        for t in range(T):
            for i in range(2):
                q = n % 8
                n += 1
                gt_ = dma(pool, None, None, "gb%d" % q, yu, gu[q], make=lambda e, t=t, i=i, q=q: e.indirect_dma_start(
                    out=GB[q], out_offset=None, in_=YS[:, :],
                    in_offset=bass.IndirectOffsetOnAxis(ap=sli[i][:, t:t + 1], axis=0)))
                gu[q] = xd = dve(lambda e, t=t, i=i, q=q: e.scalar_tensor_tensor(
                    out=X[:, t, :], in0=GB[q], scalar=wi[i][:, t:t + 1], in1=X[:, t, :], op0=ALU.mult, op1=ALU.add),
                    gt_, xd, tw)
        barrier()

    def l2_ffn(XT):
        hid, hp = 1024, 8
        o = S0 + 6250
        wr = at(o, 2, p=128)
        dma(sp, None, None, None, make=lambda e: e.dma_start(
            wr, inp["L2_ffn_wr"].rearrange("(k p) o -> p (k o)", p=128), allow_slow_non_contiguous=True))
        br, t0 = param_n("L2_ffn_br", o + 2, 1)
        b1, t0 = param_t("L2_ffn_b1", o + 4, 8)
        b2, t0 = param_n("L2_ffn_b2", o + 12)
        o += 268
        wN, r_, cf = at(o, T), at(o + 25, 4, T), at(o + 125, T)
        o += 150
        tmp = o
        o += 125
        wrow = at(o, N)
        o += 3125
        jk = at(o, N)
        o += 3125
        W1 = at(o, 2, hid, p=128)
        t1 = load(W1, inp["L2_ffn_w1"].rearrange("(k p) f -> p k f", p=128), "w0")
        o += 2048
        W2 = at(o, hp, D, p=128)
        t1 = load(W2, inp["L2_ffn_w2"].rearrange("(k p) f -> p k f", p=128), "w0")
        o += 2048
        Hb = [at(o + i * hp * 500, hp, 500, p=128) for i in range(2)]
        o += 8000
        Y = [at(o + i * D, D) for i in range(2)]
        o += 2 * D
        assert o <= K0
        bt = bank()
        for t in range(T):
            for k in range(2):
                a = pe(lambda e, t=t, k=k: e.matmul(banks[bt][0:P, t:t + 1], XT[:, k, t * P:(t + 1) * P],
                                                    wr[:, k:k + 1], start=(k == 0), stop=(k == 1)), t0, free[bt],
                       inc=(k == 1 and t == T - 1))
        free[bt] = a = dve(lambda e: e.tensor_scalar(wN, banks[bt][0:P, 0:T], br[:, 0:1], None, ALU.add), a)
        ro = rows_out(wN, T, 0, tmp, "ro", a)
        lw = row_bcast(wrow, 0, 0, N, "asr", ro)
        z = dve(lambda e: e.memset(r_, 0.0), lw)
        dve.wait(z)
        j0 = None
        for t in range(T):
            sc = wN[:, t:t + 1]
            lo, hi = t * P, (t + 1) * P
            if t:
                j0 = dve(lambda e, sc=sc, lo=lo, t=t: e.tensor_scalar(
                    jk[:, 0:lo], wrow[:, 0:lo], sc, None, ALU.is_ge, ALU.add, accum_out=r_[:, 0, t:t + 1]), j0)
            j0 = dve(lambda e, sc=sc, lo=lo, t=t: e.tensor_scalar(
                jk[:, lo:N], wrow[:, lo:N], sc, None, ALU.is_gt, ALU.add, accum_out=r_[:, 1, t:t + 1]), j0)
            j0 = dve(lambda e, sc=sc, lo=lo, hi=hi, t=t: e.scalar_tensor_tensor(
                out=jk[:, lo:hi], in0=wrow[:, lo:hi], scalar=sc, in1=tri, op0=ALU.is_equal, op1=ALU.mult,
                accum_out=r_[:, 2, t:t + 1]), j0)
        a = dve(lambda e: e.tensor_tensor(r_[:, 0, :], r_[:, 0, :], r_[:, 1, :], ALU.add), j0)
        a = dve(lambda e: e.tensor_tensor(r_[:, 0, :], r_[:, 0, :], r_[:, 2, :], ALU.add), a)
        a = dve(lambda e: e.tensor_scalar(r_[:, 0, :], r_[:, 0, :], 1560.5, None, ALU.is_lt), a)
        a = dve(lambda e: e.tensor_tensor(cf, r_[:, 0, :], wN, ALU.mult), a)
        a = dve(lambda e: e.tensor_tensor(X, X, XN, ALU.add), a)
        dve.wait(a)
        hu, yu = [None, None], [None, None]
        n = 0
        for ci, (n0, w) in enumerate(CH):
            i = ci % 2
            hl = []
            for oo in range(hp):
                b = bank()
                for kk in range(2):
                    a = pe(lambda e, b=b, oo=oo, kk=kk, n0=n0, w=w: e.matmul(
                        banks[b][:, 0:w], W1[:, kk, oo * 128:(oo + 1) * 128], XT[:, kk, n0:n0 + w],
                        start=(kk == 0), stop=(kk == 1)), free[b], t1, inc=(kk == 1))
                free[b] = act(lambda e, b=b, oo=oo, i=i, w=w: e.activation(
                    Hb[i][:, oo, 0:w], banks[b][:, 0:w], ACT.Gelu_apprx_tanh, bias=b1[:, oo:oo + 1]), a, t0, hu[i])
                hl.append(free[b])
            for j in range(w // P):
                t = n0 // P + j
                b = bank()
                for kk in range(hp):
                    a = pe(lambda e, b=b, kk=kk, i=i, j=j: e.matmul(
                        banks[b][0:P, 0:D], Hb[i][:, kk, j * P:(j + 1) * P], W2[:, kk, :],
                        start=(kk == 0), stop=(kk == hp - 1)), free[b], hl, inc=(kk == hp - 1))
                y = n % 2
                n += 1
                free[b] = d = dve(lambda e, b=b, y=y: e.tensor_tensor(Y[y], banks[b][0:P, 0:D], b2, ALU.add), a, yu[y])
                yu[y] = dve(lambda e, y=y, t=t: e.scalar_tensor_tensor(
                    out=X[:, t, :], in0=Y[y], scalar=cf[:, t:t + 1], in1=X[:, t, :], op0=ALU.mult, op1=ALU.add), d)
            hu[i] = a
        barrier()

    wtv = WT.rearrange("(s p) d -> p s d", p=P)
    c16v = C16.rearrange("(s p) d -> p s d", p=P)

    def aggregate(src, k, ro, counts, sink, *tokens):
        if counts:
            Lb = [at(ro + i * 1250, 5, 500, dt=U16) for i in range(2)]
            Vb = [at(ro + 2500 + i * 2500, 5, 500) for i in range(2)]
        else:
            Vb = [at(ro + i * 2500, 5, 500) for i in range(3)]
        nb = len(Vb)
        used = [None] * nb
        lu = [None, None]
        it = 0
        for ci, (n0, w) in enumerate(CH):
            bs = [(ci % 2) * k + kk for kk in range(k)]
            for s5 in range(5):
                i = it % nb
                if counts:
                    l = load(Lb[i][:, :, 0:w], c16v[:, s5 * 5:s5 * 5 + 5, n0:n0 + w], "lb%d" % i, lu[i])
                    l = copy_out(it, Vb[i][:, :, 0:w], Lb[i][:, :, 0:w], l, used[i])
                    lu[i] = l
                else:
                    l = load(Vb[i][:, :, 0:w], wtv[:, s5 * 5:s5 * 5 + 5, n0:n0 + w], "lb%d" % i, used[i])
                it += 1
                for s in range(5):
                    for kk in range(k):
                        a = pe(lambda e, i=i, s=s, s5=s5, kk=kk, b=bs[kk], w=w: e.matmul(
                            banks[b][:, 0:w], src[:, s5 * 5 + s, kk * 128:(kk + 1) * 128], Vb[i][:, s, 0:w],
                            start=(s5 == 0 and s == 0), stop=(s5 == 4 and s == 4)), l, free[bs[kk]], *tokens)
                used[i] = a
            ends = sink(ci, n0, w, bs, a)
            for kk in range(k):
                free[bs[kk]] = ends[kk]

    def bn(v, g, bb, o, relu, *tokens):
        s = at(o, 2 * T, 6, p=128)
        m = at(o + 300, 2, 2, p=128)
        sc, sh, tm = at(o + 304, 2, p=128), at(o + 306, 2, p=128), at(o + 308, 2, p=128)
        dve.wait(*tokens)
        for k in range(2):
            for c in range(T):
                a = dve(lambda e, k=k, c=c: e.bn_stats(s[:, k * T + c, :], v[:, k, c * P:(c + 1) * P]))
        dve.wait(a)
        for k in range(2):
            a = dve(lambda e, k=k: e.bn_aggr(m[:, k, :], s[:, k * T:(k + 1) * T, :].rearrange("p a b -> p (a b)")))
        a = rstd(m[:, :, 1], sc, tm, a)
        a = dve(lambda e: e.tensor_tensor(sc, sc, g, ALU.mult), a)
        for k in range(2):
            a = dve(lambda e, k=k: e.tensor_scalar(v[:, k, :], v[:, k, :], m[:, k, 0:1], sc[:, k:k + 1],
                                                   ALU.subtract, ALU.mult), a)
        for k in range(2):
            a = act(lambda e, k=k: e.activation(v[:, k, :], v[:, k, :], ACT.Relu if relu else ACT.Identity,
                                                bias=bb[:, k:k + 1]), a)
        return a

    def l1_gnn(XT):
        hN = at(S0 + 6250, T, D)
        ro = S0 + 12650
        ag = [at(S0 + 20150 + i * 1000, 2, 500, p=128) for i in range(2)]
        h2 = at(S0 + 22150, 2, N, p=128)
        o = S0 + 28400
        w1, t1 = weight("L1_gnn_c1_w1", o, 2, D)
        w2, t1 = weight("L1_gnn_c1_w2", o + 512, 2, D)
        w3, t1 = weight("L1_gnn_c2_w1", o + 1024, 2, D)
        w4, t1 = weight("L1_gnn_c2_w2", o + 1536, 2, D)
        o += 2048
        b1, t0 = param_n("L1_gnn_c1_b1", o)
        b3, t0 = param_n("L1_gnn_c2_b1", o + 256)
        o += 512
        pt = {}
        for nme in ("c1_b2", "c1_g", "c1_b", "bn1_g", "bn1_b", "c2_b2", "c2_g", "c2_b", "bn2_g", "bn2_b"):
            pt[nme], t0 = param_t("L1_gnn_" + nme, o)
            o += 2
        bo = o
        assert o + 310 <= K0

        def conv(srcT, wa, ba, wb, bb, ready):
            def sink(t, ps, a):
                a = dve(lambda e: e.tensor_tensor(hN[:, t, :], ps, ba, ALU.add), a, t0)
                relu.append(dve(lambda e: e.tensor_scalar(hN[:, t, :], hN[:, t, :], 0.0, None, ALU.max), a))
                return a
            relu = []
            lin_N(srcT, 2, wa, D, sink, t1, ready)
            agu = [None, None]
            fin = []

            def sink2(ci, n0, w, bs, a):
                i = ci % 2
                ends = [copy_out(kk, ag[i][:, kk, 0:w], banks[bs[kk]][:, 0:w], a, agu[i]) for kk in range(2)]
                for oo in range(2):
                    b = bank((4, 8))
                    for kk in range(2):
                        m = pe(lambda e, b=b, kk=kk, oo=oo, i=i, w=w: e.matmul(
                            banks[b][:, 0:w], wb[:, kk, oo * 128:(oo + 1) * 128], ag[i][:, kk, 0:w],
                            start=(kk == 0), stop=(kk == 1)), free[b], ends, inc=(kk == 1))
                    free[b] = act(lambda e, b=b, oo=oo, n0=n0, w=w: e.activation(
                        h2[:, oo, n0:n0 + w], banks[b][:, 0:w], ACT.Identity, bias=bb[:, oo:oo + 1]), m)
                    fin.append(free[b])
                agu[i] = m
                return ends

            aggregate(hN, 2, ro, False, sink2, relu)
            return fin

        f = conv(XT, w1, b1, w2, pt["c1_b2"], None)
        a = bn(h2, pt["c1_g"], pt["c1_b"], bo, True, f)
        a = bn(h2, pt["bn1_g"], pt["bn1_b"], bo, True, a)
        barrier()
        f = conv(h2, w3, b3, w4, pt["c2_b2"], None)
        a = bn(h2, pt["c2_g"], pt["c2_b"], bo, True, f)
        a = bn(h2, pt["bn2_g"], pt["bn2_b"], bo, False, a)
        a = dve(lambda e: e.tensor_tensor(h2, h2, XT, ALU.add), a)
        a = dve(lambda e: e.tensor_scalar(h2, h2, 0.0, None, ALU.max), a)
        add_from_T(h2, 2, 0, N, a)
        barrier()

    def l3_gnn():
        u = at(XN0, T, D)
        z2 = at(XN0, T, 512)
        hT = at(19200, 4, N, p=128)
        o = 31700
        ro = o
        o += 7500
        wt = at(o, 2048, p=128)
        o += 2048
        dvB = at(o, N, p=128)
        o += 3125
        ag = [at(o + i * 2000, 4, 500, p=128) for i in range(2)]
        o += 4000
        dvN = at(o, T)
        o += 25
        b1, t0 = param_t("L3_gnn_b1", o, 4)
        b2, t0 = param_t("L3_gnn_b2", o + 4, 4)
        b3, t0 = param_t("L3_gnn_b3", o + 8, 2)
        o += 10
        assert o <= K0
        l = load(dvB, DEG[0, :].partition_broadcast(128), "dg")
        l = dma(sp, None, None, "dg", make=lambda e: e.dma_start(
            dvN, DEG.rearrange("o (t p) -> p (o t)", p=P), allow_slow_non_contiguous=True))
        a = act(lambda e: e.activation(dvB, dvB, ACT.Sqrt), l)
        a = act(lambda e: e.activation(dvN, dvN, ACT.Sqrt), l)
        a = dve(lambda e: e.reciprocal(dvB, dvB), a)
        a = dve(lambda e: e.reciprocal(dvN, dvN), a)
        us = [dve(lambda e, t=t: e.tensor_scalar(u[:, t, :], u[:, t, :], dvN[:, t:t + 1], None, ALU.mult), a)
              for t in range(T)]
        W1 = wt[:, 0:1024].rearrange("p (k f) -> p k f", k=2)
        t1 = load(W1, inp["L3_gnn_W1"].rearrange("(k p) f -> p k f", p=128), None)
        agu = [None, None]

        def sink1(ci, n0, w, bs, a):
            i = ci % 2
            ends = [dve(lambda e, kk=kk, i=i: e.tensor_tensor(ag[i][:, kk, 0:w], banks[bs[kk]][:, 0:w],
                                                              dvB[:, n0:n0 + w], ALU.mult), a, agu[i])
                    for kk in range(2)]
            for oo in range(4):
                b = bank((4, 8))
                for kk in range(2):
                    m = pe(lambda e, b=b, kk=kk, oo=oo: e.matmul(
                        banks[b][:, 0:w], W1[:, kk, oo * 128:(oo + 1) * 128], ag[i][:, kk, 0:w],
                        start=(kk == 0), stop=(kk == 1)), free[b], ends, t1, inc=(kk == 1))
                free[b] = act(lambda e, b=b, oo=oo: e.activation(
                    hT[:, oo, n0:n0 + w], banks[b][:, 0:w], ACT.Tanh, bias=b1[:, oo:oo + 1]), m, t0)
            agu[i] = m
            return ends

        aggregate(u, 2, ro, True, sink1, us)
        barrier()
        W2 = wt.rearrange("p (k f) -> p k f", k=4)
        t1 = load(W2, inp["L3_gnn_W2"].rearrange("(k p) f -> p k f", p=128), None)

        def sinkz(t, ps, a):
            return evac(t, lambda e: e.activation(z2[:, t, :], ps, ACT.Copy, scale=dvN[:, t:t + 1]),
                        lambda e: e.tensor_scalar(z2[:, t, :], ps, dvN[:, t:t + 1], None, ALU.mult), a)

        lin_N(hT, 4, W2, 512, sinkz, t1)
        barrier()

        def sink2(ci, n0, w, bs, a):
            i = ci % 2
            ends = []
            for kk in range(4):
                m = dve(lambda e, kk=kk: e.tensor_tensor(ag[i][:, kk, 0:w], banks[bs[kk]][:, 0:w],
                                                         dvB[:, n0:n0 + w], ALU.mult), a, agu[i])
                ends.append(m)
                m = act(lambda e, kk=kk: e.activation(hT[:, kk, n0:n0 + w], ag[i][:, kk, 0:w], ACT.Tanh,
                                                      bias=b2[:, kk:kk + 1]), m)
            agu[i] = m
            return ends

        agu = [None, None]
        aggregate(z2, 4, ro, True, sink2)
        barrier()
        W3 = wt[:, 0:1024].rearrange("p (k f) -> p k f", k=4)
        t1 = load(W3, inp["L3_gnn_W3"].rearrange("(k p) f -> p k f", p=128), None)

        def sinkz3(t, ps, a):
            return evac(t, lambda e: e.activation(u[:, t, :], ps, ACT.Copy, scale=dvN[:, t:t + 1]),
                        lambda e: e.tensor_scalar(u[:, t, :], ps, dvN[:, t:t + 1], None, ALU.mult), a)

        z3 = lin_N(hT, 4, W3, D, sinkz3, t1)
        agu = [None, None]

        def sink3(ci, n0, w, bs, a):
            i = ci % 2
            ends = []
            for kk in range(2):
                m = dve(lambda e, kk=kk: e.tensor_tensor(ag[i][:, kk, 0:w], banks[bs[kk]][:, 0:w],
                                                         dvB[:, n0:n0 + w], ALU.mult), a, agu[i])
                ends.append(m)
                m = act(lambda e, kk=kk: e.activation(ag[i][:, kk, 0:w], ag[i][:, kk, 0:w], ACT.Identity,
                                                      bias=b3[:, kk:kk + 1]), m)
            for j in range(w // P):
                t = n0 // P + j
                b = bank((4, 8))
                for kk in range(2):
                    x = pe(lambda e, kk=kk, j=j, b=b: e.transpose(
                        banks[b][0:P, kk * 128:(kk + 1) * 128], ag[i][:, kk, j * P:(j + 1) * P], ident[:, :]),
                        free[b], m, inc=(kk == 1))
                free[b] = dve(lambda e, t=t, b=b: e.tensor_tensor(X[:, t, :], banks[b][0:P, 0:D], X[:, t, :],
                                                                  ALU.add), x)
            agu[i] = x
            return ends

        aggregate(u, 2, ro, True, sink3, z3)
        barrier()

    XT = at(S0, 2, N, p=128)

    def norm_turn():
        nt = norm_tiles(X, XN)
        to_T(XN, XT, nt)
        barrier()

    def run():
        expert_consts()
        graph()
        if stop == "graph":
            return
        norm_turn()
        l0_mix(XT)
        if stop == "m0":
            return
        gat("L0_gnn", 4, 64, 1e-16, XT)
        if stop == "g0":
            return
        norm_turn()
        ffn(XT, "L0_ffn", 512, ACT.Gelu, "all", "L0_ffn_gate_w", ["L0_ffn_gate_b"])
        if stop == "f0":
            return
        norm_turn()
        l1_mix(XT)
        if stop == "m1":
            return
        l1_gnn(XT)
        if stop == "g1":
            return
        norm_turn()
        ffn(XT, "L1_ffn", 512, ACT.Relu, "two", "L1_ffn_Wg", ["L1_ffn_bg", "L1_ffn_bias"])
        if stop == "f1":
            return
        norm_turn()
        l2_mix(XT)
        if stop == "m2":
            return
        gat("L2_gnn", 8, 32, 0.0, XT)
        if stop == "g2":
            return
        norm_turn()
        l2_ffn(XT)
        if stop == "f2":
            return
        norm_turn()
        l3_mix(XT)
        if stop == "m3":
            return
        l3_gnn()
        if stop == "g3":
            return
        norm_turn()
        ffn(XT, "L3_ffn", 1024, ACT.Gelu, "share", "L3_ffn_Wr", ["L3_ffn_br"],
            affine=True, again=True)

    run()
    t = load(rows(out, P), X, "out", dve.last)
    sp.wait(t)
    with ctx:
        block = ctx.enter_context(nc.Block())

        @block.tensor
        def _(eng):
            pe.emit(eng)

        @block.scalar
        def _(eng):
            act.emit(eng)

        @block.vector
        def _(eng):
            dve.emit(eng)

        @block.gpsimd
        def _(eng):
            pool.emit(eng)

        @block.sync
        def _(eng):
            sp.emit(eng)


_DERIVED = {"L0_mix_w_qkv": "w", "L0_mix_b_qkv": "b", "L3_mix_wq": "wqT", "L3_mix_wk": "wkT", "L3_mix_wv": "wvT",
            "L3_mix_wo": "woT"}
_UNUSED = {"L2_ffn_attention_mask"}


def _layout(inputs):
    arrays = {}
    for name, value in inputs.items():
        a = np.asarray(value)
        if name in _UNUSED:
            continue
        if name == "L0_mix_w_qkv":
            v = a.reshape(D, 8, 3, 32)
            for i, c in enumerate("qkv"):
                arrays[f"w{c}0"] = np.ascontiguousarray(v[:, :, i, :].reshape(D, D))
        elif name == "L0_mix_b_qkv":
            v = a.reshape(8, 3, 32)
            for i, c in enumerate("qkv"):
                arrays[f"b{c}0"] = np.ascontiguousarray(v[:, i, :].reshape(D))
        elif name in _DERIVED:
            arrays[_DERIVED[name]] = np.ascontiguousarray(a.T)
        else:
            arrays[name] = np.ascontiguousarray(a)
    for pre, hid in (("L0_ffn", 512), ("L1_ffn", 512), ("L3_ffn", 1024)):
        def lanes(a, k):
            return a.reshape(8, k, 128, -1).transpose(0, 2, 1, 3).reshape(8, 128, -1)
        parts = [lanes(arrays.pop(pre + "_W1"), 2), lanes(arrays.pop(pre + "_W2"), hid // 128),
                 lanes(arrays.pop(pre + "_b1"), hid // 128)]
        if pre == "L3_ffn":
            parts += [lanes(arrays.pop(pre + "_ln_g"), 2), lanes(arrays.pop(pre + "_ln_b"), 2)]
        arrays[pre + "_pack"] = np.ascontiguousarray(np.concatenate(parts, axis=2))
    return arrays


STOP = None


def kernel(**inputs):
    import concourse.bacc as bacc
    from concourse.bass_utils import run_bass_kernel_spmd

    nc = bacc.Bacc("TRN2", target_bir_lowering=False, num_devices=1)
    arrays = _layout(inputs)
    aps = {n: nc.dram_tensor(n, a.shape, mybir.dt.from_np(a.dtype), kind="ExternalInput").ap()
           for n, a in arrays.items()}
    out = nc.dram_tensor("out", (N, D), F32, kind="ExternalOutput").ap()
    program(nc, aps, out, STOP)
    r = run_bass_kernel_spmd(nc, [arrays], core_ids=[0])
    return r.results[0]["out"]
```

```python
import numpy as np
import concourse.bass as bass
from concourse import mybir
from contextlib import ExitStack

F32 = mybir.dt.float32
BF16 = mybir.dt.bfloat16
U16 = mybir.dt.uint16
I32 = mybir.dt.int32
ALU = mybir.AluOpType
ACT = mybir.ActivationFunctionType
AX = mybir.AxisListType.X

N, D, E = 3125, 256, 50000
P, T = 125, 25
CH = [(c * 500, 500) for c in range(4)] + [(2000 + c * 375, 375) for c in range(3)]
NB, NQ = 100, 4
BIG = 1e30
WORDS = 51200


class Queue:

    def __init__(self, new_sem, name):
        self.new_sem, self.name = new_sem, name
        self.items, self.seen = [], {}
        self.beside, self.every, self.due = None, 1, 0
        self.turn()

    def turn(self):
        self.sem, self.count, self.last = self.new_sem(), 0, None

    def wait(self, *tokens):
        for t in tokens:
            if t is None:
                continue
            if isinstance(t, list):
                self.wait(*t)
                continue
            sem, value = t
            if self.seen.get(id(sem), 0) < value:
                self.seen[id(sem)] = value
                self.items.append((None, sem, value))

    def __call__(self, fn, *tokens, inc=True):
        self.wait(*tokens)
        if not inc:
            self.items.append((fn, None, 0))
            return None
        if self.count >= 30000:
            self.turn()
        self.count += 1
        self.items.append((fn, self.sem, 1))
        self.last = last = (self.sem, self.count)
        if self.beside is not None:
            self.due += 1
            if self.due % self.every == 0:
                work, self.beside = self.beside, None
                if next(work, "end") != "end":
                    self.beside = work
        return last

    def emit(self, eng):
        for fn, sem, value in self.items:
            if fn is None:
                eng.wait_ge(sem, value)
            else:
                ins = fn(eng)
                if sem is not None:
                    ins.then_inc(sem, value)


def program(nc, inp, out, stop=None):
    dram = {}
    ctx = ExitStack()
    nsem = [0]

    def new_sem():
        nsem[0] += 1
        return ctx.enter_context(nc.semaphore(f"s{nsem[0]}"))

    pe, act, dve, pool, sp = (Queue(new_sem, n) for n in ("pe", "act", "dve", "pool", "sp"))
    engines = [pe, act, dve, pool, sp]
    channels = {}
    once = []

    def dma(eng, dst, src, ch, *tokens, make=None):
        if ch is None:
            once.append(dma(eng, dst, src, "once%d" % len(once), *tokens, make=make))
            return list(once)
        if ch not in channels:
            channels[ch] = [new_sem(), 0]
        c = channels[ch]
        if c[1] >= 30000:
            c[0], c[1] = new_sem(), 0
        eng.wait(*tokens)
        c[1] += 16
        eng.items.append((make or (lambda e: e.dma_start(dst, src)), c[0], 16))
        return (c[0], c[1])

    def load(dst, src, ch, *tokens):
        return dma(sp, dst, src, ch, *tokens)

    def barrier():
        marks = [e.last for e in engines] + [(c[0], c[1]) for c in channels.values() if c[1]]
        for e in engines:
            e.wait(*marks)
        for i in range(8):
            free[i] = None
        once.clear()

    def fence(*but):
        marks = [e.last for e in (pe, act, dve)]
        marks += [(c[0], c[1]) for n, c in channels.items() if c[1] and not n.startswith(but)]
        for e in (pe, act, dve, sp):
            e.wait(*marks)
        for i in range(8):
            free[i] = None
        once.clear()

    arena = ctx.enter_context(nc.sbuf_tensor("arena", [128, WORDS], F32))
    banks = [ctx.enter_context(nc.psum_tensor(f"bank{i}", [128, 512], F32)) for i in range(8)]
    free = [None] * 8

    def at(off, *dims, p=P, dt=F32):
        n = int(np.prod(dims))
        words = n if dt in (F32, I32) else (n + 1) // 2
        assert off + words <= WORDS, (off, words)
        v = arena[0:p, off:off + words]
        if dt != F32:
            v = v.bitcast(dt)
            v = v[:, 0:n]
        if len(dims) == 2:
            v = v.rearrange("p (a b) -> p a b", a=dims[0])
        elif len(dims) == 3:
            v = v.rearrange("p (a b c) -> p a b c", a=dims[0], b=dims[1])
        return v

    def rows(v, n):
        return v.rearrange("(t p) f -> p t f", p=n)

    ring = [0]

    def bank(pool_of=(0, 8)):
        ring[0] += 1
        i = pool_of[0] + ring[0] % (pool_of[1] - pool_of[0])
        return i

    X0, XN0, S0 = 0, 6400, 12800
    K0 = 49700
    X = at(X0, T, D)
    XN = at(XN0, T, D)
    ident = at(K0, 128, p=128)
    ones = at(K0 + 128, 128, p=128)
    iota8 = at(K0 + 256, 8)
    bmask32 = at(K0 + 264, 128, p=128)
    bmask64 = at(K0 + 392, 128, p=128)
    tri = at(K0 + 520, 125)
    SM = K0 + 645
    st6 = at(SM, T, 6)
    mv = at(SM + 150, T, 2)
    rs = at(SM + 200, T)
    rs2 = at(SM + 225, T)
    PV = SM + 250

    def dd(name, shape, dt=F32):
        return nc.dram_tensor(name, shape, dt, kind="Internal").ap()

    G = dd("G", [N * N + 500, 2])
    C16 = dd("C16", [N, N], U16)
    WT = dd("WT", [N, N])
    MK = dd("MK", [N, N], BF16)
    KEY = dd("KEY", [1, E])
    DEG = dd("DEG", [1, N])
    ROW = dd("ROW", [24 * T, P])

    pm = pool(lambda e: e.memset(ident, 0.0))
    pm1 = pool(lambda e: e.memset(ones, 1.0))
    t_id = pool(lambda e: e.affine_select(out=ident, in_=ident, compare_op=ALU.not_equal, fill=1.0, base=0,
                                          pattern=[[-1, 128]], channel_multiplier=1), pm)
    t_tri = pool(lambda e: e.affine_select(out=tri, in_=ones[0:P, 0:P], compare_op=ALU.is_gt, fill=0.0, base=0,
                                           pattern=[[-1, P]], channel_multiplier=1), pm1)
    for e8 in range(8):
        pool(lambda e, e8=e8: e.memset(iota8[:, e8:e8 + 1], float(8 - e8)))

    def block_mask(m, c):
        a = pool(lambda e: e.memset(m, 1.0))
        v = m.rearrange("p (b c) -> p b c", c=c)
        a = pool(lambda e: e.affine_select(out=v, in_=v, compare_op=ALU.is_ge, fill=0.0, base=0,
                                           pattern=[[-c, 128 // c], [0, c]], channel_multiplier=1), a)
        return pool(lambda e: e.affine_select(out=v, in_=v, compare_op=ALU.is_ge, fill=0.0, base=c - 1,
                                              pattern=[[c, 128 // c], [0, c]], channel_multiplier=-1), a)

    block_mask(bmask32, 32)
    block_mask(bmask64, 64)
    load(X, rows(inp["x"], P), "x")
    barrier()

    def evac(i, fn_act, fn_dve, *tokens):
        return act(fn_act, *tokens) if i % 2 else dve(fn_dve, *tokens)

    def copy_out(i, dst, src, *tokens):
        return evac(i, lambda e: e.activation(dst, src, ACT.Copy), lambda e: e.tensor_copy(dst, src), *tokens)

    def bcast(v, n, k=1):
        s = list(v.shape)
        return v.unsqueeze(k).broadcast_to(s[:k] + [n] + s[k:])

    def param_n(name, off, w=D):
        dst = at(off, w)
        src = inp[name] if len(inp[name].shape) == 1 else inp[name].rearrange("a b -> (a b)")
        return dst, load(dst, src.partition_broadcast(P), None)

    def param_t(name, off, k=2, src=None):
        dst = at(off, k, p=128)
        src = inp[name] if src is None else src
        return dst, dma(sp, dst, None, None, make=lambda e: e.dma_start(
            dst, src.rearrange("(k p) -> p k", p=128), allow_slow_non_contiguous=True))

    def weight(name, off, k, f, src=None, ch=None, tokens=()):
        dst = at(off, k, f, p=128)
        src = inp[name] if src is None else src
        return dst, load(dst, src.rearrange("(k p) f -> p k f", p=128), ch, *tokens)

    def rstd(var, dst, tmp, *tokens, eps=1e-5):
        a = dve(lambda e: e.tensor_scalar(tmp, var, eps, None, ALU.add), *tokens)
        b = act(lambda e: e.activation(dst, tmp, ACT.Sqrt), a)
        return dve(lambda e: e.reciprocal(dst, dst), b)

    def norm_tiles(src, dst, *tokens):
        dve.wait(*tokens)
        for t in range(T):
            a = dve(lambda e, t=t: e.bn_stats(st6[:, t, :], src[:, t, :]))
        dve.wait(a)
        for t in range(T):
            a = dve(lambda e, t=t: e.bn_aggr(mv[:, t, :], st6[:, t, :]))
        r = rstd(mv[:, :, 1], rs, rs2, a)
        dve.wait(r)
        return [dve(lambda e, t=t: e.tensor_scalar(dst[:, t, :], src[:, t, :], mv[:, t, 0:1], rs[:, t:t + 1],
                                                   ALU.subtract, ALU.mult)) for t in range(T)]

    def to_T(src, dst, ready, k=2):
        last = []
        n = 0
        for c, (n0, w) in enumerate(CH):
            for kk in range(k):
                b = bank()
                m = w // P
                for i in range(m):
                    t = n0 // P + i
                    a = pe(lambda e, t=t, i=i, b=b, kk=kk: e.transpose(
                        banks[b][:, i * P:(i + 1) * P], src[:, t, kk * 128:(kk + 1) * 128], ident[0:P, 0:P]),
                        free[b], ready[t] if isinstance(ready, list) else ready, inc=(i == m - 1))
                free[b] = copy_out(n, dst[:, kk, n0:n0 + w], banks[b][:, 0:w], a)
                last.append(free[b])
                n += 1
        return last[-2:]

    def add_from_T(src, k, n0, w, *tokens):
        for i in range(w // P):
            t = n0 // P + i
            b = bank()
            for kk in range(k):
                a = pe(lambda e, kk=kk, i=i, b=b: e.transpose(
                    banks[b][0:P, kk * 128:(kk + 1) * 128], src[:, kk, i * P:(i + 1) * P], ident[:, :]),
                    free[b], *tokens, inc=(kk == k - 1))
            free[b] = dve(lambda e, t=t, b=b: e.tensor_tensor(X[:, t, :], banks[b][0:P, 0:D], X[:, t, :], ALU.add), a)
        return a

    def lin_N(srcT, k, W, f, sink, *tokens, f0=0):
        out_t = []
        for t in range(T):
            b = bank()
            for kk in range(k):
                a = pe(lambda e, t=t, kk=kk, b=b: e.matmul(
                    banks[b][0:P, 0:f], srcT[:, kk, t * P:(t + 1) * P], W[:, kk, f0:f0 + f],
                    start=(kk == 0), stop=(kk == k - 1)), free[b], *tokens, inc=(kk == k - 1))
            free[b] = sink(t, banks[b][0:P, 0:f], a)
            out_t.append(free[b])
        return out_t

    def lin_T(W, srcT, k, o, sink, *tokens, chunks=CH, base=0):
        last = []
        for n0, w in chunks:
            for oo in range(o):
                b = bank()
                for kk in range(k):
                    a = pe(lambda e, kk=kk, b=b, oo=oo, n0=n0, w=w: e.matmul(
                        banks[b][:, 0:w], W[:, kk, oo * 128:(oo + 1) * 128], srcT[:, kk, n0 - base:n0 - base + w],
                        start=(kk == 0), stop=(kk == k - 1)), free[b], *tokens, inc=(kk == k - 1))
                free[b] = sink(oo, n0, w, banks[b][:, 0:w], a)
                last.append(free[b])
        return last[-4:]

    def head_norm(v, tmp, sm, heads, g, bb, *tokens):
        c = D // heads
        n = T * heads
        s1, s2, s3 = (at(sm + i * n, n) for i in range(3))
        vv = v.rearrange("p t (h c) -> p (t h) c", c=c)
        tt = tmp.rearrange("p t (h c) -> p (t h) c", c=c)
        a = dve(lambda e: e.tensor_reduce(s1, vv, AX, ALU.add), *tokens)
        a = dve(lambda e: e.tensor_scalar(s1, s1, 1.0 / c, None, ALU.mult), a)
        a = dve(lambda e: e.tensor_tensor(vv, vv, bcast(s1, c, 2), ALU.subtract), a)
        a = act(lambda e: e.activation(tmp, v, ACT.Square), a)
        a = dve(lambda e: e.tensor_reduce(s2, tt, AX, ALU.add), a)
        a = dve(lambda e: e.tensor_scalar(s2, s2, 1.0 / c, 1e-5, ALU.mult, ALU.add), a)
        a = act(lambda e: e.activation(s3, s2, ACT.Sqrt), a)
        a = dve(lambda e: e.reciprocal(s3, s3), a)
        a = dve(lambda e: e.tensor_tensor(vv, vv, bcast(s3, c, 2), ALU.mult), a)
        a = dve(lambda e: e.tensor_tensor(vv, vv, bcast(g, n), ALU.mult), a)
        return dve(lambda e: e.tensor_tensor(vv, vv, bcast(bb, n), ALU.add), a)

    def rows_out(src, m, row0, tmp_off, ch, *tokens):
        b = bank()
        tmp = at(tmp_off, P, p=m)
        a = pe(lambda e: e.transpose(banks[b][0:m, 0:P], src, ident[0:P, 0:P]), free[b], *tokens)
        free[b] = dve(lambda e: e.tensor_copy(tmp, banks[b][0:m, 0:P]), a)
        return load(ROW[row0:row0 + m, :], tmp, ch, free[b])

    def row_bcast(dst, row0, n0, w, ch, *tokens):
        src = ROW[row0:row0 + T, :].rearrange("t p -> (t p)")[n0:n0 + w]
        return load(dst, src.partition_broadcast(P), ch, *tokens)

    GRAPH = ("sc", "gz", "kr", "key", "ed", "xz")
    G0 = S0 + 24500

    def graph_pairs(after):
        zero = at(G0, 1250)
        b1 = G0 + 1250
        K = at(b1, NQ, NB)
        CT = at(b1 + 400, NQ, NB)
        IDF = at(b1 + 800, NQ, NB)
        IDX = at(b1 + 1200, NQ, NB, dt=I32)
        LD = at(b1 + 1600, NQ, NB)
        DM = at(b1 + 2000, NQ)
        DMI = at(b1 + 2004, NQ, dt=I32)
        VAL = at(b1 + 2010, NQ * NB * 2)
        val = VAL.rearrange("p (q b c) -> p q b c", q=NQ, c=2)
        TR = at(b1 + 2810, NQ, 500)
        b2 = b1 + 4810
        KR = [at(b2 + i * 1000, 2, 500) for i in range(2)]
        WR = [at(b2 + 2000 + i * 1000, 2, 500) for i in range(2)]
        JK = [at(b2 + 4000 + i * 250, 500, dt=BF16) for i in range(2)]
        assert b2 + 4500 <= S0 + 35200
        si, di, sf, df = (at(b2 + i * 500, 500, p=NB, dt=I32 if i < 2 else F32) for i in range(4))
        a = load(si, inp["src"].rearrange("(b j) -> b j", b=NB), "ed")
        a = load(di, inp["dst"].rearrange("(b j) -> b j", b=NB), "ed")
        z = dve(lambda e: e.memset(zero, 0.0), after)
        c1 = dve(lambda e: e.tensor_copy(sf, si), a)
        c2 = dve(lambda e: e.tensor_copy(df, di))
        c3 = dve(lambda e: e.scalar_tensor_tensor(out=sf, in0=sf, scalar=float(N), in1=df, op0=ALU.mult,
                                                  op1=ALU.add), c2)
        kd = load(KEY.rearrange("o (b j) -> (o b) j", b=NB), sf, "key", c3)
        p1 = pool(lambda e: e.iota(DMI, pattern=[[P, NQ]], base=N * N, channel_multiplier=1))
        dm = dve(lambda e: e.tensor_copy(DM, DMI), p1)
        p2 = pool(lambda e: e.memset(TR, 1025.0))
        trt = pool(lambda e: e.affine_select(out=TR, in_=TR, compare_op=ALU.is_gt, fill=1.0, base=0,
                                             pattern=[[P, NQ], [-1, 500]], channel_multiplier=1), p2)
        kt = None
        for q in range(NQ):
            b = bank()
            a = pe(lambda e, q=q, b=b: e.transpose(banks[b][0:P, 0:NB], sf[:, q * P:(q + 1) * P],
                                                   ident[0:NB, 0:NB]), c3, free[b])
            free[b] = kt = dve(lambda e, q=q, b=b: e.tensor_copy(K[:, q, :], banks[b][0:P, 0:NB]), a)
        ready = [kt, trt, dm]
        gz = G[0:N * N, :].rearrange("(s p n) c -> s p (n c)", p=P, n=N)
        zt = {}

        def clear(s):
            zt[s] = dma(sp, gz[s].rearrange("p (a b) -> p a b", b=1250), bcast(zero, 5), "gz%d" % (s % 3), z,
                        zt.get(s - 3))

        load(G[N * N:N * N + 500, :].rearrange("(p n) c -> p (n c)", p=P), zero[:, 0:8], "gzt", z)
        used = [None, None]
        jt = [None, None]
        cleared = 0
        chain = None
        rows_ = {}

        def lot_rows(g):
            i = g % 2
            load(KR[i], KEY[0, g * 1000:(g + 1) * 1000].rearrange("(b j) -> b j", b=2).partition_broadcast(P),
                 "kr%d" % i, kd, kt, used[i])
            rows_[g] = load(WR[i], inp["edge_weight"][g * 1000:(g + 1) * 1000].rearrange("(b j) -> b j", b=2)
                            .partition_broadcast(P), "kr%d" % i)

        lot_rows(0)
        lot_rows(1)
        waiting = []
        for g in range(NB // 2):
            i = g % 2
            for bb in range(2):
                b = g * 2 + bb
                for q in range(NQ):
                    jt[0] = dve(lambda e, i=i, bb=bb, b=b, q=q: e.scalar_tensor_tensor(
                        out=JK[0], in0=KR[i][:, bb, :], scalar=K[:, q, b:b + 1], in1=TR[:, q, :],
                        op0=ALU.is_equal, op1=ALU.mult, accum_out=CT[:, q, b:b + 1]), jt[0], ready, rows_[g])
                    jt[1] = a2 = dve(lambda e, i=i, bb=bb, b=b, q=q: e.scalar_tensor_tensor(
                        out=JK[1], in0=KR[i][:, bb, :], scalar=K[:, q, b:b + 1], in1=WR[i][:, bb, :],
                        op0=ALU.is_equal, op1=ALU.mult, accum_out=val[:, q, b, 1:2]), jt[1])
            used[i] = a2
            bs = slice(g * 2, g * 2 + 2)
            a = dve(lambda e, bs=bs: e.tensor_scalar(LD[:, :, bs], CT[:, :, bs], 1024.0, None, ALU.is_lt), a2)
            a = dve(lambda e, bs=bs: e.tensor_copy(val[:, :, bs, 0], CT[:, :, bs]))
            a = dve(lambda e, bs=bs: e.tensor_tensor(IDF[:, :, bs], K[:, :, bs], bcast(DM, 2, 2), ALU.subtract))
            a = dve(lambda e, bs=bs: e.tensor_tensor(IDF[:, :, bs], IDF[:, :, bs], LD[:, :, bs], ALU.mult), a)
            a = dve(lambda e, bs=bs: e.tensor_tensor(IDF[:, :, bs], IDF[:, :, bs], bcast(DM, 2, 2), ALU.add), a)
            a = dve(lambda e, bs=bs: e.tensor_copy(IDX[:, :, bs], IDF[:, :, bs]), a)
            if g + 2 < NB // 2:
                lot_rows(g + 2)
            waiting.append((g, a))
            for _ in range(2):
                if cleared < T:
                    clear(cleared)
                    cleared += 1
                    if cleared == T:
                        chain = [(c[0], c[1]) for n, c in channels.items() if n.startswith("gz")]
            while cleared == T and waiting:
                gg, a = waiting.pop(0)
                for b in range(2 * gg, 2 * gg + 2):
                    for q in range(NQ):
                        t = dma(pool, None, None, "sc", a, chain, make=lambda e, q=q, b=b: e.indirect_dma_start(
                            out=G[:, :], out_offset=bass.IndirectOffsetOnAxis(ap=IDX[:, q, b:b + 1], axis=0),
                            in_=val[:, q, b, :], in_offset=None, compute_op=ALU.add))
                    chain = t
            yield
        clear_slots(zero, z)

    def graph_split(asN, mx):
        asr = at(XN0, 4, N)
        MB = [at(XN0 + 12500 + i * 813, 1625, dt=BF16) for i in range(2)]
        o = S0 + 14600
        GT = [at(o + i * 3250, 1625, 2) for i in range(3)]
        o += 9750
        CO = [at(o + i * 813, 1625, dt=U16) for i in range(2)]
        o += 1626
        WO = [at(o + i * 1625, 1625) for i in range(2)]
        o += 3250
        MS = at(o, 13, 625, dt=BF16)
        o += 4063
        jk = at(o, 625, dt=BF16)
        o += 313
        mxp = at(o, 100, 5)
        o += 500
        idb = at(o, 126, dt=BF16)
        o += 63
        assert o <= S0 + 35200
        la = None
        for h in range(4):
            la = row_bcast(asr[:, h, :], 25 * h, 0, N, "asr")
        ib = dve(lambda e: e.tensor_copy(idb[:, 0:P], ident[0:P, 0:P]))
        gt = G[0:N * N, :].rearrange("(s p n) c -> s p n c", p=P, n=N)
        gfree = [None] * 3
        cw = [None, None]
        ww = [None, None]
        mused = [None, None]
        msw = None
        mxt = None
        tbs = [4, 5, 6, 7]
        steps = [(j0, nj, s) for j0, nj in ((0, 13), (13, 12)) for s in range(T)]
        lg = {}

        def fetch(n):
            if n < len(steps):
                j0, nj, s = steps[n]
                lg[n] = load(GT[n % 3][:, 0:nj * P, :], gt[s][:, j0 * P:(j0 + nj) * P, :], "gt%d" % (n % 3),
                             gfree[n % 3])

        fetch(0)
        fetch(1)
        nb = 0
        for n, (jb, nj, s) in enumerate(steps):
            i, i3 = n % 2, n % 3
            wd_ = nj * P
            d = l = lg[n]
            if jb <= s < jb + nj:
                c0 = (s - jb) * P
                d = dve(lambda e, i3=i3, c0=c0: e.tensor_tensor(
                    GT[i3][:, c0:c0 + P, 0], GT[i3][:, c0:c0 + P, 0], ident[0:P, 0:P], ALU.add), l)
            m = dve(lambda e, i=i, i3=i3, w=wd_: e.tensor_scalar(MB[i][:, 0:w], GT[i3][:, 0:w, 0], 1.0, None, ALU.min),
                    d, mused[i])
            c = act(lambda e, i=i, i3=i3, w=wd_: e.activation(CO[i][:, 0:w], GT[i3][:, 0:w, 0], ACT.Copy), d, cw[i])
            w = act(lambda e, i=i, i3=i3, w=wd_: e.activation(WO[i][:, 0:w], GT[i3][:, 0:w, 1], ACT.Copy), ww[i])
            fetch(n + 2)
            cw[i] = load(C16[s * P:(s + 1) * P, jb * P:(jb + nj) * P], CO[i][:, 0:wd_], "co%d" % i, c)
            ww[i] = load(WT[s * P:(s + 1) * P, jb * P:(jb + nj) * P], WO[i][:, 0:wd_], "wo%d" % i, w)
            for cc in range(4):
                n0 = cc * 500
                wd = min(500, wd_ - n0)
                if wd <= 0:
                    continue
                a = pe(lambda e, cc=cc, n0=n0, wd=wd, i3=i3, s=s: e.matmul(
                    banks[cc][:, 0:wd], ones[0:P, :], GT[i3][:, n0:n0 + wd, 0], start=(s == 0), stop=(s == T - 1)),
                    d, free[cc])
            gfree[i3] = [a, m, w, c]
            if s == T - 1:
                for cc in range(4):
                    n0 = cc * 500
                    wd = min(500, wd_ - n0)
                    if wd > 0:
                        free[cc] = a = dve(lambda e, cc=cc, n0=n0, wd=wd, i=i: e.tensor_copy(
                            WO[i][0:1, n0:n0 + wd], banks[cc][0:1, 0:wd]), a, ww[i])
                ww[i] = load(DEG[:, jb * P:(jb + nj) * P], WO[i][0:1, 0:wd_], "deg", a)
            sl = s % 5
            for j0 in range(0, nj, 8):
                mj = min(8, nj - j0)
                tb_ = tbs[nb % 4]
                nb += 1
                tbv = banks[tb_][0:P, :].bitcast(BF16)
                for j in range(mj):
                    a = pe(lambda e, j=j, j0=j0, i=i, tbv=tbv: e.transpose(
                        tbv[:, j * 128:j * 128 + P], MB[i][:, (j0 + j) * P:(j0 + j + 1) * P], idb[:, 0:P]),
                        m, ib, free[tb_], inc=(j == mj - 1))
                free[tb_] = ms = dve(lambda e, j0=j0, mj=mj, sl=sl, tbv=tbv: e.tensor_scalar(
                    MS[:, j0:j0 + mj, sl * P:(sl + 1) * P],
                    tbv[:, 0:mj * 128].rearrange("p (j c) -> p j c", c=128)[:, :, 0:P],
                    -1.0, BIG, ALU.add, ALU.mult), a, msw if sl == 0 else None)
            mused[i] = a
            if sl == 4:
                g5 = s // 5
                msw = [load(MK[jb * P:(jb + nj) * P, (s - 4) * P:(s + 1) * P].rearrange("(j p) c -> p j c", p=P),
                            MS[:, 0:nj, :], "ms", ms)]
                for j in range(nj):
                    for h in range(4):
                        mxt = dve(lambda e, j=j, h=h, g5=g5, jb=jb: e.tensor_tensor_reduce(
                            out=jk, in0=MS[:, j, :], in1=asr[:, h, g5 * 625:(g5 + 1) * 625], scale=1.0,
                            scalar=-3e38, op0=ALU.add, op1=ALU.max,
                            accum_out=mxp[:, h * T + jb + j, g5:g5 + 1]), la, ms, mxt)
                msw.append(mxt)
        dve(lambda e: e.tensor_reduce(mx[:, 0:4, :].rearrange("p h t -> p (h t)"), mxp, AX, ALU.max), mxt)
        barrier()

    H1o, OUTo, B0, S1 = S0 + 8000, S0 + 14600, S0 + 21000, S0 + 35200

    def gat_names(H, C):
        return (at(H1o, T, H, C + 1), at(OUTo, T, D), *(at(S1 + i * 200, H, T) for i in range(8)))

    def gat_source(pre, H, C, XT):
        h1, outN, asN, as2, adN, mx, u, m, r1, r2 = gat_names(H, C)
        W, tw = weight(pre + "_W", B0, 2, D)
        ats, ta = param_n(pre + "_att_src", B0 + 512)
        atd, ta = param_n(pre + "_att_dst", B0 + 768)
        dve(lambda e: e.memset(h1[:, :, :, C], 1.0))

        def sink(t, ps, a):
            return evac(t, lambda e: e.activation(h1[:, t, :, 0:C], ps.rearrange("p (h c) -> p h c", c=C), ACT.Copy),
                        lambda e: e.tensor_copy(h1[:, t, :, 0:C], ps.rearrange("p (h c) -> p h c", c=C)), a)

        ts = lin_N(XT, 2, W, D, sink, tw)
        tmp = outN.rearrange("p t (h c) -> p t h c", c=C)
        a = None
        for att, dst in ((ats, asN), (atd, adN)):
            for h in range(H):
                a = dve(lambda e, att=att, h=h: e.tensor_tensor(
                    tmp[:, :, h, :], h1[:, :, h, 0:C], bcast(att[:, h * C:(h + 1) * C], T), ALU.mult), ts, ta, a)
            a = dve(lambda e, dst=dst: e.tensor_reduce(dst.rearrange("p h t -> p t h"), tmp, AX, ALU.add), a)
        a = dve(lambda e: e.tensor_scalar(as2, asN, 0.2, None, ALU.mult), a)
        for g in range(H // 4):
            fl = asN[:, 4 * g:4 * g + 4, :].rearrange("p h t -> p (h t)")
            ro = rows_out(fl, 100, 100 * g, B0 + 1024 + 125 * g, "ro", a)

    def gat_largest(H, asN, mx):
        R0 = S0
        asr = at(B0, 4, N)
        jk = at(R0, N)
        a = None
        ml = [at(R0 + 3125 + i * 1563, N, dt=BF16) for i in range(2)]
        for g in range(H // 4):
            for h in range(4):
                l = row_bcast(asr[:, h, :], 100 * g + 25 * h, 0, N, "asr", a if g else None)
            mu = [None, None]
            for j in range(T):
                i = j % 2
                lm = load(ml[i], MK[j * P:(j + 1) * P, :], "mk%d" % i, mu[i])
                for h in range(4):
                    a = dve(lambda e, i=i, h=h, g=g, j=j: e.tensor_tensor_reduce(
                        out=jk, in0=ml[i], in1=asr[:, h, :], scale=1.0, scalar=-3e38, op0=ALU.add, op1=ALU.max,
                        accum_out=mx[:, 4 * g + h, j:j + 1]), lm, l, a)
                mu[i] = a
        barrier()

    def gat_sum(pre, H, C, eps):
        h1, outN, asN, as2, adN, mx, u, m, r1, r2 = gat_names(H, C)
        R0, CW = S0, C + 1
        a = None
        a = dve(lambda e: e.tensor_tensor(u, mx, adN, ALU.add), a)
        a = dve(lambda e: e.scalar_tensor_tensor(out=m, in0=u, scalar=0.2, in1=u, op0=ALU.mult, op1=ALU.max), a)
        a = dve(lambda e: e.tensor_tensor(r1, adN, m, ALU.subtract), a)
        a = dve(lambda e: e.scalar_tensor_tensor(out=r2, in0=adN, scalar=0.2, in1=m, op0=ALU.mult, op1=ALU.subtract), a)
        for g in range(H // 4):
            for k, r in enumerate((r1, r2)):
                fl = r[:, 4 * g:4 * g + 4, :].rearrange("p h t -> p (h t)")
                rows_out(fl, 100, 200 * g + 100 * k, B0 + 125 * (2 * g + k), "ro", a)
        barrier()
        Rb = [at(R0 + i * 4000, 2, 4, 500) for i in range(2)]
        Cb = [at(B0 + i * 1250, 5, 500, dt=U16) for i in range(2)]
        Tb = [at(B0 + 2500 + i * 2000, 4, 500) for i in range(2)]
        Xb = [at(B0 + 6500, 4, 500), at(B0 + 8500, 4, 500), at(XN0, 4, 500)]
        AC = [at(B0 + 10500, 4, 500, p=128), at(XN0 + 2000, 4, 500, p=128)]
        rused = [None, None]
        cused = [None, None]
        xused = [None] * 3
        tused = [None, None]
        acused = [None, None]
        it = 0
        rcp = at(S1 + 1600, 4, 4)
        c16v = C16.rearrange("(s p) d -> p s d", p=P)
        steps = [(g, n0, w, s) for g in range(H // 4) for n0, w in CH for s in range(T)]
        lr, lc = {}, {}

        def fetch(n):
            if n >= len(steps):
                return
            g, n0, w, s = steps[n]
            r = n // T
            if s == 0:
                for k in range(2):
                    for h in range(4):
                        lr[r] = row_bcast(Rb[r % 2][:, k, h, 0:w], 200 * g + 100 * k + 25 * h, n0, w,
                                          "rb%d" % (r % 2), rused[r % 2])
            if s % 5 == 0:
                c = n // 5
                lc[c] = load(Cb[c % 2][:, :, 0:w], c16v[:, s:s + 5, n0:n0 + w], "cb%d" % (c % 2), cused[c % 2])

        def exponents(n):
            g, n0, w, s = steps[n]
            r, i, j, jx = n // T, n // T % 2, n % 2, n % 3
            for h in range(4):
                tt = act(lambda e, h=h: e.activation(Tb[j][:, h, 0:w], Rb[i][:, 1, h, 0:w], ACT.Identity,
                                                     bias=as2[:, 4 * g + h, s:s + 1]), lr[r], tused[j])
            for h in range(4):
                x = dve(lambda e, h=h: e.scalar_tensor_tensor(
                    out=Xb[jx][:, h, 0:w], in0=Rb[i][:, 0, h, 0:w], scalar=asN[:, 4 * g + h, s:s + 1],
                    in1=Tb[j][:, h, 0:w], op0=ALU.add, op1=ALU.max), tt, lr[r], xused[jx])
            tused[j] = x
            if s == T - 1:
                rused[i] = [x, tt]
            return x

        def weigh(n, x):
            g, n0, w, s = steps[n]
            r, jx, c = n // T, n % 3, n // 5
            ex = act(lambda e: e.activation(Xb[jx][:, :, 0:w], Xb[jx][:, :, 0:w], ACT.Exp), x)
            pr = dve(lambda e: e.scalar_tensor_tensor(
                out=Xb[jx][:, :, 0:w], in0=Xb[jx][:, :, 0:w], scalar=1.0, in1=bcast(Cb[c % 2][:, s % 5, 0:w], 4),
                op0=ALU.min, op1=ALU.mult), ex, lc[c])
            b0 = 4 * (r % 2)
            for h in range(4):
                a = pe(lambda e, h=h: e.matmul(
                    banks[b0 + h][0:CW, 0:w], h1[:, s, 4 * g + h, :], Xb[jx][:, h, 0:w],
                    start=(s == 0), stop=(s == T - 1)), pr, free[b0 + h])
            xused[jx] = a
            cused[c % 2] = pr
            if s == T - 1:
                later.extend(divide(g, n0, w, r, a))

        def divide(g, n0, w, r, a):
            b0 = 4 * (r % 2)
            ac = AC[r % 2]
            cp = [act(lambda e, h=h: e.activation(ac[0:CW, h, 0:w], banks[b0 + h][0:CW, 0:w], ACT.Copy),
                      a, acused[r % 2]) for h in range(4)]
            nt = w // P
            tp = []

            def turn():
                for k in range(nt):
                    for h in range(4):
                        x = pe(lambda e, h=h, k=k: e.transpose(
                            banks[b0 + k][0:P, h * CW:(h + 1) * CW], ac[0:CW, h, k * P:(k + 1) * P],
                            ident[0:CW, 0:CW]), cp, inc=(h == 3))
                    tp.append(x)
                acused[r % 2] = x

            def scale():
                vs = [banks[b0 + k][0:P, 0:4 * CW].rearrange("p (h c) -> p h c", c=CW) for k in range(nt)]
                zs = [dve(lambda e, k=k: e.tensor_scalar(rcp[:, k, :], vs[k][:, :, C], eps, None, ALU.add),
                          tp[k], rcu[0]) for k in range(nt)]
                zs = dve(lambda e: e.reciprocal(rcp[:, 0:nt, :], rcp[:, 0:nt, :]), zs)
                for k in range(nt):
                    o = outN[:, n0 // P + k, 4 * g * C:4 * (g + 1) * C].rearrange("p (h c) -> p h c", c=C)
                    free[b0 + k] = rcu[0] = dve(lambda e, k=k, o=o: e.tensor_tensor(
                        o, vs[k][:, :, 0:C], bcast(rcp[:, k, :], C, 2), ALU.mult), zs)
                for k in range(nt, 4):
                    free[b0 + k] = cp
            return [turn, None, scale]

        later, rcu = [], [None]
        fetch(0)
        xs = {}
        for n in range(len(steps) + 1):
            if n < len(steps):
                xs[n] = exponents(n)
            if later:
                piece = later.pop(0)
                if piece:
                    piece()
            if n:
                weigh(n - 1, xs[n - 1])
            if n + 1 < len(steps):
                fetch(n + 1)
        for piece in later:
            if piece:
                piece()
        barrier()
        bi, t1 = param_n(pre + "_bias", B0)
        ga, t1 = param_n(pre + "_gamma", B0 + 256)
        be, t1 = param_n(pre + "_beta", B0 + 512)
        a = dve(lambda e: e.tensor_tensor(outN, outN, bcast(bi, T), ALU.add), t1)
        nt = norm_tiles(outN, outN, a)
        a = dve(lambda e: e.tensor_tensor(outN, outN, bcast(ga, T), ALU.mult), nt)
        a = dve(lambda e: e.tensor_tensor(outN, outN, bcast(be, T), ALU.add), a)
        dve(lambda e: e.tensor_tensor(X, X, outN, ALU.add), a)
        barrier()

    def mix_ln(XT, Wq, bq, Wk, bk, Wv, bv, gk, bk2, gv, bv2, heads, tail, end, tmp_of=None):
        A0 = S0 + 6250
        kN, vN = (at(A0 + i * 6400, T, D) for i in range(2))
        tm = tmp_of or XN
        o = A0 + 12800
        c = D // heads
        mask = bmask32 if c == 32 else bmask64
        wq, tq = weight(Wq, o, 2, D)
        wk, tk = weight(Wk, o + 512, 2, D)
        wv, tv = weight(Wv, o + 1024, 2, D)
        o += 1536
        small = o
        o += 600
        prm = []
        for nme in (gk, bk2, gv, bv2):
            v, t1 = param_n(nme, o, c)
            prm.append(v)
            o += c
        bkn = bvn = bqt = None
        if bq is not None:
            bkn, t1 = param_n(bk, o)
            bvn, t1 = param_n(bv, o + 256)
            bqt, t1 = param_t(bq, o + 512)
        o += 520
        kvs = at(o, 2, 128, p=128)
        o += 256

        def sink_for(dst, bn):
            def sink(t, ps, a):
                if bn is not None:
                    return dve(lambda e: e.tensor_tensor(dst[:, t, :], ps, bn, ALU.add), a, t1)
                return copy_out(t, dst[:, t, :], ps, a)
            return sink

        tk2 = lin_N(XT, 2, wk, D, sink_for(kN, bkn), tk, tv)
        tv2 = lin_N(XT, 2, wv, D, sink_for(vN, bvn), tv)
        a = head_norm(kN, tm, small, heads, prm[0], prm[1], tk2, t1)
        a = head_norm(vN, tm, small, heads, prm[2], prm[3], tv2, a)
        bk_ = [bank(), bank()]
        for k in range(2):
            b = bk_[k]
            for t in range(T):
                m = pe(lambda e, b=b, k=k, t=t: e.matmul(
                    banks[b][:, 0:128], kN[:, t, k * 128:(k + 1) * 128], vN[:, t, k * 128:(k + 1) * 128],
                    start=(t == 0), stop=(t == T - 1)), a, free[b], inc=(t == T - 1))
            free[b] = dve(lambda e, b=b, k=k: e.scalar_tensor_tensor(
                out=kvs[:, k, :], in0=banks[b][:, 0:128], scalar=1.0 / N, in1=mask, op0=ALU.mult, op1=ALU.mult), m)
        kt = free[bk_[1]]
        qc = [at(A0 + i * 1000, 2, 500, p=128) for i in range(2)]
        qused = [None, None]
        for ci, (n0, w) in enumerate(CH):
            i = ci % 2
            ql = []
            for oo in range(2):
                b = bank()
                for kk in range(2):
                    a = pe(lambda e, b=b, oo=oo, kk=kk, n0=n0, w=w: e.matmul(
                        banks[b][:, 0:w], wq[:, kk, oo * 128:(oo + 1) * 128], XT[:, kk, n0:n0 + w],
                        start=(kk == 0), stop=(kk == 1)), free[b], tq, inc=(kk == 1))
                if bqt is not None:
                    free[b] = act(lambda e, b=b, oo=oo, i=i, w=w: e.activation(
                        qc[i][:, oo, 0:w], banks[b][:, 0:w], ACT.Identity, bias=bqt[:, oo:oo + 1]), a, kt, qused[i])
                else:
                    free[b] = act(lambda e, b=b, oo=oo, i=i, w=w: e.activation(
                        qc[i][:, oo, 0:w], banks[b][:, 0:w], ACT.Copy), a, kt, qused[i])
                ql.append(free[b])
            qused[i] = tail(ci, n0, w, qc[i], kvs, ql, o)
        end()

    def l0_mix(XT):
        M0 = S0 + 23000
        w1, t1 = weight("L0_mix_w1", M0, 2, D)
        w2, t1 = weight("L0_mix_w2", M0 + 512, 2, D)
        b1, t1 = param_t("L0_mix_b1", M0 + 1024)
        b2, t2 = param_n("L0_mix_b2", M0 + 1026)
        rc = [at(S0 + 6250 + 2000 + i * 1000, 2, 500, p=128) for i in range(2)]
        hc = [at(S0 + 6250 + 4000 + i * 1000, 2, 500, p=128) for i in range(2)]
        rused = [None, None]
        hused = [None, None]

        def tail(ci, n0, w, q, kvs, ql, o):
            assert o <= S0 + 23000, o
            i = ci % 2
            rl = []
            for k in range(2):
                b = bank()
                a = pe(lambda e, b=b, k=k: e.matmul(banks[b][:, 0:w], kvs[:, k, :], q[:, k, 0:w], start=True,
                                                    stop=True), free[b], ql)
                free[b] = dve(lambda e, b=b, k=k: e.tensor_tensor(rc[i][:, k, 0:w], banks[b][:, 0:w],
                                                                  XT[:, k, n0:n0 + w], ALU.add), a, rused[i])
                rl.append(free[b])
            done = a
            hl = []
            for oo in range(2):
                b = bank()
                for k in range(2):
                    a = pe(lambda e, b=b, k=k, oo=oo: e.matmul(
                        banks[b][:, 0:w], w1[:, k, oo * 128:(oo + 1) * 128], rc[i][:, k, 0:w],
                        start=(k == 0), stop=(k == 1)), free[b], rl, t1, inc=(k == 1))
                free[b] = act(lambda e, b=b, oo=oo: e.activation(
                    hc[i][:, oo, 0:w], banks[b][:, 0:w], ACT.Gelu, bias=b1[:, oo:oo + 1]), a, t2, hused[i])
                hl.append(free[b])
            rused[i] = a
            for j in range(w // P):
                t = n0 // P + j
                b = bank()
                for k in range(2):
                    a = pe(lambda e, b=b, k=k, j=j: e.matmul(
                        banks[b][0:P, 0:D], hc[i][:, k, j * P:(j + 1) * P], w2[:, k, :],
                        start=(k == 0), stop=(k == 1)), free[b], hl, inc=(k == 1))
                free[b] = dve(lambda e, b=b, t=t: e.tensor_tensor(X[:, t, :], banks[b][0:P, 0:D], X[:, t, :],
                                                                  ALU.add), a)
            hused[i] = a
            return done

        a = dve(lambda e: e.tensor_tensor(X, X, XN, ALU.add))
        a = dve(lambda e: e.tensor_tensor(X, X, bcast(b2, T), ALU.add), a, t2)
        dve.wait(a)
        mix_ln(XT, "wq0", "bq0", "wk0", "bk0", "wv0", "bv0", "L0_mix_kln_g", "L0_mix_kln_b",
               "L0_mix_vln_g", "L0_mix_vln_b", 8, tail, lambda: fence(*GRAPH))

    def l3_mix(XT):
        wo, t1 = weight("woT", S0 + 30000, 2, D)
        bo, t2 = param_n("L3_mix_bo", S0 + 31040)
        rc = [at(S0 + 31300 + i * 1000, 2, 500, p=128) for i in range(2)]
        rused = [None, None]

        def tail(ci, n0, w, q, kvs, ql, o):
            assert o <= S0 + 30000
            i = ci % 2
            rl = []
            for k in range(2):
                b = bank()
                a = pe(lambda e, b=b, k=k: e.matmul(banks[b][:, 0:w], kvs[:, k, :], q[:, k, 0:w], start=True,
                                                    stop=True), free[b], ql)
                free[b] = dve(lambda e, b=b, k=k: e.tensor_copy(rc[i][:, k, 0:w], banks[b][:, 0:w]), a, rused[i])
                rl.append(free[b])
            done = a
            for j in range(w // P):
                t = n0 // P + j
                b = bank()
                for k in range(2):
                    a = pe(lambda e, b=b, k=k, j=j: e.matmul(
                        banks[b][0:P, 0:D], rc[i][:, k, j * P:(j + 1) * P], wo[:, k, :],
                        start=(k == 0), stop=(k == 1)), free[b], rl, t1, inc=(k == 1))
                free[b] = dve(lambda e, b=b, t=t: e.tensor_tensor(X[:, t, :], banks[b][0:P, 0:D], X[:, t, :],
                                                                  ALU.add), a)
            rused[i] = a
            return done

        a = dve(lambda e: e.tensor_tensor(X, X, bcast(bo, T), ALU.add), t2)
        dve.wait(a)
        mix_ln(XT, "wqT", None, "wkT", None, "wvT", None, "L3_mix_ln_k_g", "L3_mix_ln_k_b",
               "L3_mix_ln_v_g", "L3_mix_ln_v_b", 4, tail, barrier, at(S0 + 22000, T, D))

    def l1_mix(XT):
        o = S0 + 6250
        W, tw = weight("L1_mix_W_qkv", o, 2, 384)
        o += 768
        Wo = at(o, D, p=128)
        tw = load(Wo, inp["L1_mix_W_out"], None)
        o += 256
        bo, tb = param_n("L1_mix_b_out", o)
        o += 256
        kT = at(o, N, p=128)
        o += 3125
        kN = at(o, T, 128)
        o += 3200
        vN = at(o, T, 128)
        o += 3200
        ctx_ = at(o, 128, p=128)
        o += 128
        sm = at(o, 8, p=128)
        o += 8
        qc = [at(o + i * 500, 500, p=128) for i in range(2)]
        o += 1000
        oc = [at(o + i * 500, 500, p=128) for i in range(2)]
        o += 1000
        assert o <= K0
        a = dve(lambda e: e.tensor_tensor(X, X, bcast(bo, T), ALU.add), tb)
        dve.wait(a)
        last = []
        for ci, (n0, w) in enumerate(CH):
            b = bank()
            for kk in range(2):
                a = pe(lambda e, b=b, kk=kk, n0=n0, w=w: e.matmul(
                    banks[b][:, 0:w], W[:, kk, 128:256], XT[:, kk, n0:n0 + w], start=(kk == 0), stop=(kk == 1)),
                    free[b], tw, inc=(kk == 1))
            free[b] = copy_out(ci, kT[:, n0:n0 + w], banks[b][:, 0:w], a)
            last.append(free[b])
        a = dve(lambda e: e.tensor_reduce(sm[:, 0:1], kT, AX, ALU.max, negate=True), last)
        ek = act(lambda e: e.activation(kT, kT, ACT.Exp, bias=sm[:, 0:1], accum_out=sm[:, 1:2]), a)
        rr = dve(lambda e: e.reciprocal(sm[:, 2:3], sm[:, 1:2]), ek)
        rr = dve(lambda e: e.tensor_scalar(sm[:, 2:3], sm[:, 2:3], 32.0 ** -0.5, None, ALU.mult), rr)

        def sinkv(t, ps, a):
            return copy_out(t, vN[:, t, :], ps, a)

        tv = lin_N(XT, 2, W, 128, sinkv, tw, f0=256)
        tk = []
        for t in range(T):
            b = bank()
            a = pe(lambda e, t=t, b=b: e.transpose(banks[b][0:P, 0:128], kT[:, t * P:(t + 1) * P], ident[:, :]),
                   ek, free[b])
            free[b] = copy_out(t, kN[:, t, :], banks[b][0:P, 0:128], a)
            tk.append(free[b])
        b = bank()
        for t in range(T):
            a = pe(lambda e, t=t, b=b: e.matmul(banks[b][:, 0:128], kN[:, t, :], vN[:, t, :], start=(t == 0),
                                                stop=(t == T - 1)), free[b], tk, tv, inc=(t == T - 1))
        free[b] = dve(lambda e, b=b: e.scalar_tensor_tensor(
            out=ctx_, in0=banks[b][:, 0:128], scalar=sm[:, 2:3], in1=bmask32, op0=ALU.mult, op1=ALU.mult), a, rr)
        ct = free[b]
        qu, ou = [None, None], [None, None]
        for ci, (n0, w) in enumerate(CH):
            i = ci % 2
            b = bank()
            for kk in range(2):
                a = pe(lambda e, b=b, kk=kk, n0=n0, w=w: e.matmul(
                    banks[b][:, 0:w], W[:, kk, 0:128], XT[:, kk, n0:n0 + w], start=(kk == 0), stop=(kk == 1)),
                    free[b], inc=(kk == 1))
            free[b] = q1 = act(lambda e, b=b, i=i, w=w: e.activation(qc[i][:, 0:w], banks[b][:, 0:w], ACT.Copy), a, qu[i])
            b = bank()
            a = pe(lambda e, b=b, i=i, w=w: e.matmul(banks[b][:, 0:w], ctx_, qc[i][:, 0:w], start=True, stop=True),
                   q1, ct, free[b])
            qu[i] = a
            free[b] = o1 = act(lambda e, b=b, i=i, w=w: e.activation(oc[i][:, 0:w], banks[b][:, 0:w], ACT.Copy), a, ou[i])
            for j in range(w // P):
                t = n0 // P + j
                b = bank()
                a = pe(lambda e, b=b, i=i, j=j: e.matmul(banks[b][0:P, 0:D], oc[i][:, j * P:(j + 1) * P], Wo,
                                                         start=True, stop=True), o1, free[b])
                free[b] = dve(lambda e, b=b, t=t: e.tensor_tensor(X[:, t, :], banks[b][0:P, 0:D], X[:, t, :],
                                                                  ALU.add), a)
            ou[i] = a
        barrier()

    def l2_mix(XT):
        o = S0 + 6250
        W, tw = weight("L2_mix_W_qkv", o, 2, 768)
        o += 1536
        Wo, tw = weight("L2_mix_W_out", o, 2, D)
        o += 512
        bqkv = at(o, 768)
        load(bqkv, inp["L2_mix_b_qkv"].partition_broadcast(P), None)
        o += 768
        bo, tb = param_n("L2_mix_b_out", o)
        o += 256
        bvt, tb = param_t("L2_mix_b_qkv", o, src=inp["L2_mix_b_qkv"][512:768])
        o += 2
        kN, vN = (at(o + i * 6400, T, D) for i in range(2))
        o += 12800
        q2T = at(o, 2, N, p=128)
        o += 6250
        kv = at(o, 2, D, p=128)
        o += 512
        cn = at(o, 8, p=128)
        o += 8
        sm = [at(o + i * 25, T) for i in range(6)]
        o += 150
        sq = at(o, 2, D)
        o += 512
        assert o <= K0 - 2000, o
        vc = [at(o + i * 1000, 2, 500, p=128) for i in range(2)]
        a = dve(lambda e: e.tensor_tensor(X, X, bcast(bo, T), ALU.add), tb)
        dve.wait(a)

        def sink_for(dst, f):
            def sink(t, ps, a):
                return dve(lambda e: e.tensor_tensor(dst[:, t, :], ps, bqkv[:, f:f + D], ALU.add), a, tb)
            return sink

        def squares(v, ready):
            vf = v
            a = dve(lambda e: e.tensor_reduce(sm[0], vf, AX, ALU.add), ready)
            a = dve(lambda e: e.tensor_scalar(sm[0], sm[0], 1.0 / D, None, ALU.mult), a)
            a = dve(lambda e: e.tensor_tensor(vf, vf, bcast(sm[0], D, 2), ALU.subtract), a)
            a = act(lambda e: e.activation(vf, vf, ACT.Square), a)
            a = dve(lambda e: e.tensor_reduce(sm[1], vf, AX, ALU.add), a)
            a = dve(lambda e: e.tensor_scalar(sm[1], sm[1], 1e-7, None, ALU.add), a)
            a = dve(lambda e: e.reciprocal(sm[1], sm[1]), a)
            return dve(lambda e: e.tensor_tensor(vf, vf, bcast(sm[1], D, 2), ALU.mult), a)

        tq = lin_N(XT, 2, W, D, sink_for(vN, 0), tw, f0=0)
        a = squares(vN, tq)
        for t in range(T):
            a = dve(lambda e, t=t: e.scalar_tensor_tensor(out=sq[:, 0, :], in0=vN[:, t, :], scalar=1.0,
                                                          in1=vN[:, t, :], op0=ALU.mult, op1=ALU.mult,
                                                          accum_out=sm[2][:, t:t + 1]), a)
        a = act(lambda e: e.activation(sm[3], sm[2], ACT.Sqrt), a)
        a = dve(lambda e: e.tensor_scalar(sm[3], sm[3], 1e-12, None, ALU.max), a)
        a = dve(lambda e: e.reciprocal(sm[3], sm[3]), a)
        a = dve(lambda e: e.tensor_tensor(vN, vN, bcast(sm[3], D, 2), ALU.mult), a)
        qt = to_T(vN, q2T, a)
        tk = lin_N(XT, 2, W, D, sink_for(kN, D), f0=D)
        ka = squares(kN, [tk, a])
        dve.wait(qt, pe.last)
        tv = lin_N(XT, 2, W, D, sink_for(vN, 2 * D), f0=2 * D)
        b0, b1, b2 = bank(), bank(), bank()
        su = [None, None]
        for t in range(T):
            i = t % 2
            s_ = dve(lambda e, t=t, i=i: e.tensor_tensor(sq[:, i, :], kN[:, t, :], kN[:, t, :], ALU.mult), ka, su[i])
            for k in range(2):
                a = pe(lambda e, k=k, t=t, b=(b0, b1)[k]: e.matmul(banks[b][:, 0:D], kN[:, t, k * 128:(k + 1) * 128],
                                                                 vN[:, t, :], start=(t == 0), stop=(t == T - 1)),
                       ka, tv, free[(b0, b1)[k]])
            a = pe(lambda e, t=t, i=i: e.matmul(banks[b2][0:1, 0:D], ones[0:P, 0:1], sq[:, i, :], start=(t == 0),
                                                stop=(t == T - 1)), s_, free[b2])
            su[i] = a
        rowt = sq[0:1, 0, :]
        r = dve(lambda e: e.tensor_copy(rowt, banks[b2][0:1, 0:D]), a)
        free[b2] = r
        b3 = bank()
        for k in range(2):
            a = pe(lambda e, k=k: e.matmul(banks[b3][:, k:k + 1], sq[0:1, 0, k * 128:(k + 1) * 128], ones[0:1, 0:1],
                                           start=True, stop=True), r, free[b3])
        r = dve(lambda e: e.tensor_copy(cn[:, 0:2], banks[b3][:, 0:2]), a)
        free[b3] = r
        r = act(lambda e: e.activation(cn[:, 0:2], cn[:, 0:2], ACT.Sqrt), r)
        r = dve(lambda e: e.tensor_scalar(cn[:, 0:2], cn[:, 0:2], 1e-12, None, ALU.max), r)
        r = dve(lambda e: e.reciprocal(cn[:, 2:4], cn[:, 0:2]), r)
        r = dve(lambda e: e.tensor_scalar(cn[:, 4:6], cn[:, 2:4], float(N) ** -0.5, None, ALU.mult), r)
        for k, b in enumerate((b0, b1)):
            free[b] = r = dve(lambda e, k=k, b=b: e.tensor_scalar(kv[:, k, :], banks[b][:, 0:D], cn[:, 4 + k:5 + k],
                                                                  None, ALU.mult), r, a)
        vu = [None, None]
        for ci, (n0, w) in enumerate(CH):
            i = ci % 2
            al = []
            for oo in range(2):
                b = bank()
                for kk in range(4):
                    lhs = (kv[:, kk, oo * 128:(oo + 1) * 128] if kk < 2
                           else W[:, kk - 2, 512 + oo * 128:512 + (oo + 1) * 128])
                    rhs = q2T[:, kk, n0:n0 + w] if kk < 2 else XT[:, kk - 2, n0:n0 + w]
                    a = pe(lambda e, b=b, lhs=lhs, rhs=rhs, kk=kk, w=w: e.matmul(
                        banks[b][:, 0:w], lhs, rhs, start=(kk == 0), stop=(kk == 3)), free[b], r, qt, inc=(kk == 3))
                free[b] = act(lambda e, b=b, oo=oo, i=i, w=w: e.activation(
                    vc[i][:, oo, 0:w], banks[b][:, 0:w], ACT.Identity, bias=bvt[:, oo:oo + 1]), a, vu[i])
                al.append(free[b])
            for j in range(w // P):
                t = n0 // P + j
                b = bank()
                for k in range(2):
                    a = pe(lambda e, b=b, k=k, j=j, i=i: e.matmul(
                        banks[b][0:P, 0:D], vc[i][:, k, j * P:(j + 1) * P], Wo[:, k, :],
                        start=(k == 0), stop=(k == 1)), free[b], al, inc=(k == 1))
                free[b] = dve(lambda e, b=b, t=t: e.tensor_tensor(X[:, t, :], banks[b][0:P, 0:D], X[:, t, :],
                                                                  ALU.add), a)
            vu[i] = a
        barrier()

    picks = []
    SLOTS, NT = 250, 32
    XS = dd("XS", [SLOTS * NT, D])
    YS = dd("YS", [SLOTS * NT, D])
    upper = at(PV, P)
    k250 = at(PV + 125, T)
    kj = at(PV + 150, NT)
    kti = at(PV + 182, NT, dt=I32)

    def expert_consts():
        a = pool(lambda e: e.memset(upper, 1.0))
        pool(lambda e: e.affine_select(out=upper, in_=upper, compare_op=ALU.is_gt, fill=0.0, base=0,
                                       pattern=[[1, P]], channel_multiplier=-1), a)
        a = pool(lambda e: e.iota(kti, pattern=[[1, NT]], base=0, channel_multiplier=0))
        a = dve(lambda e: e.tensor_copy(kj, kti), a)
        dve(lambda e: e.tensor_scalar(k250, kj[:, 0:T], 250.0, None, ALU.mult), a)

    def clear_slots(zero, z):
        load(XS.rearrange("(a p) f -> p a f", p=P), bcast(zero[:, 0:D], 2 * NT), "xz", z)

    def top2(V, o):
        m1, eq, x1, o1, V2, sel = at(o, T), at(o + 25, T, 8), at(o + 225, T), at(o + 250, T, 8), at(o + 450, T, 8), \
            at(o + 650, T, 8)
        w8 = bcast(iota8, T)
        a = dve.last
        src = V
        for r in range(2):
            dst = sel if r == 0 else o1
            mm_ = m1 if r == 0 else x1
            a = dve(lambda e, src=src, mm_=mm_: e.tensor_reduce(mm_, src, AX, ALU.max), a)
            a = dve(lambda e, src=src, mm_=mm_: e.tensor_tensor(eq, src, bcast(mm_, 8, 2), ALU.is_equal), a)
            a = dve(lambda e: e.tensor_tensor(eq, eq, w8, ALU.mult), a)
            a = dve(lambda e: e.tensor_reduce(x1, eq, AX, ALU.max), a)
            a = dve(lambda e, dst=dst: e.tensor_tensor(dst, eq, bcast(x1, 8, 2), ALU.is_equal), a)
            if r == 0:
                a = dve(lambda e: e.scalar_tensor_tensor(out=V2, in0=sel, scalar=-3e38, in1=V, op0=ALU.mult,
                                                         op1=ALU.add), a)
                src = V2
        a = dve(lambda e: e.tensor_tensor(V2, sel, o1, ALU.add), a)
        picks[:] = [sel, o1, V2]
        return V2, m1, a

    def gate(XT, Wg, biases, kind, o, L, cw):
        W = at(o, 2, 8, p=128)
        t0 = dma(sp, None, None, None, make=lambda e: e.dma_start(
            W, inp[Wg].rearrange("(k p) f -> p k f", p=128)))
        bs = []
        for i, nme in enumerate(biases):
            v, t0 = param_n(nme, o + 16 + 8 * i, 8)
            bs.append(v)
        b = bank()
        for t in range(T):
            for k in range(2):
                a = pe(lambda e, t=t, k=k: e.matmul(banks[b][0:P, t * 8:t * 8 + 8], XT[:, k, t * P:(t + 1) * P],
                                                    W[:, k, :], start=(k == 0), stop=(k == 1)), t0, free[b],
                       inc=(k == 1 and t == T - 1))
        ps = banks[b][0:P, 0:200].rearrange("p (t e) -> p t e", e=8)
        for i, v in enumerate(bs):
            a = dve(lambda e, i=i, v=v: e.tensor_tensor(L, ps if i == 0 else L, bcast(v, T), ALU.add), a)
            if i == 0:
                free[b] = a
        w0 = o + 64
        mx, s = at(w0, T), at(w0 + 25, T)
        if kind != "two":
            a = dve(lambda e: e.tensor_reduce(mx, L, AX, ALU.max), a)
            a = dve(lambda e: e.tensor_tensor(L, L, bcast(mx, 8, 2), ALU.subtract), a)
            a = act(lambda e: e.activation(L, L, ACT.Exp), a)
            a = dve(lambda e: e.tensor_reduce(s, L, AX, ALU.add), a)
            a = dve(lambda e: e.reciprocal(s, s), a)
            a = dve(lambda e: e.tensor_tensor(L, L, bcast(s, 8, 2), ALU.mult), a)
            sel, m1, a = top2(L, w0 + 50)
            a = dve(lambda e: e.tensor_tensor(cw, L, sel, ALU.mult), a)
        else:
            sel, m1, a = top2(L, w0 + 50)
            a = dve(lambda e: e.tensor_tensor(L, L, bcast(m1, 8, 2), ALU.subtract), a)
            a = act(lambda e: e.activation(L, L, ACT.Exp), a)
            a = dve(lambda e: e.tensor_tensor(cw, L, sel, ALU.mult), a)
        if kind != "all":
            a = dve(lambda e: e.tensor_reduce(s, cw, AX, ALU.add), a)
            a = dve(lambda e: e.reciprocal(s, s), a)
            a = dve(lambda e: e.tensor_tensor(cw, cw, bcast(s, 8, 2), ALU.mult), a)
        return a

    def ffn(XT, pre, hid, fn, kind, Wg, biases, affine=False, again=False):
        hp = hid // 128
        WCn = 2 * hid + hp * D + hp + (4 if affine else 0)
        pack = inp[pre + "_pack"]
        o = S0 + 6250
        L, cw = at(o, T, 8), at(o + 200, T, 8)
        small = o + 400
        b2a = at(o + 1500, D, p=8)
        o += 1756
        cT = [at(o + i * 125, P, p=8) for i in range(2)]
        o += 250
        R, TO, OF, TM = (at(o + i * 200, T, 8) for i in range(4))
        o += 800
        cnt, tl, st = at(o, 8), at(o + 8, 8), at(o + 16, 8)
        CM = at(o + 24, 8, T)
        o += 224
        sl = [at(o + i * 25, T) for i in range(2)]
        sli = [at(o + 50 + i * 25, T, dt=I32) for i in range(2)]
        wi = [at(o + 100 + i * 25, T) for i in range(2)]
        o += 150
        ei, eii = at(o, NT), at(o + NT, NT, dt=I32)
        o += 2 * NT
        W = [at(o + i * WCn, WCn, p=128) for i in range(3)]
        o += 3 * WCn
        XR = [at(o + i * 512, 2, D) for i in range(3)]
        o += 1536
        XE = [at(o + i * 500, 2, SLOTS, p=128) for i in range(2)]
        o += 1000
        Hb = [at(o + i * hp * SLOTS, hp, SLOTS, p=128) for i in range(2)]
        o += 2 * hp * SLOTS
        Y = [at(o + i * 512, 2, D) for i in range(2)]
        o += 1024
        GB = [at(o + i * D, D) for i in range(8)]
        o += 8 * D
        assert o <= K0, o
        tb = load(b2a, inp[pre + "_b2"], None)
        g = gate(XT, Wg, biases, kind, small, L, cw)
        one, two, both = picks
        ready = norm_tiles(XN, XN, g) if again else None
        bu, b_ = bank(), bank()
        a = pe(lambda e: e.matmul(banks[bu][0:P, 0:200], upper, both.rearrange("p t e -> p (t e)"), start=True,
                                  stop=True), g, free[bu])
        c = pe(lambda e: e.matmul(banks[b_][0:P, 0:200], ones[0:P, 0:P], both.rearrange("p t e -> p (t e)"),
                                  start=True, stop=True), g, free[b_])
        free[bu] = dve(lambda e: e.tensor_copy(R.rearrange("p t e -> p (t e)"), banks[bu][0:P, 0:200]), a)
        free[b_] = dve(lambda e: e.tensor_copy(TO.rearrange("p t e -> p (t e)"), banks[b_][0:P, 0:200]), c)
        a = dve(lambda e: e.memset(OF[:, 0, :], 0.0), free[b_])
        for t in range(1, T):
            a = dve(lambda e, t=t: e.tensor_tensor(OF[:, t, :], OF[:, t - 1, :], TO[:, t - 1, :], ALU.add), a)
        a = dve(lambda e: e.tensor_tensor(cnt, OF[:, T - 1, :], TO[:, T - 1, :], ALU.add), a)
        a = dve(lambda e: e.tensor_tensor(CM, bcast(cnt, T, 2), bcast(k250, 8), ALU.is_gt), a)
        a = dve(lambda e: e.tensor_reduce(tl, CM, AX, ALU.add), a)
        a = dve(lambda e: e.memset(st[:, 0:1], 0.0), a)
        for e8 in range(1, 8):
            a = dve(lambda e, i=e8: e.tensor_tensor(st[:, i:i + 1], st[:, i - 1:i], tl[:, i - 1:i], ALU.add), a)
        a = dve(lambda e: e.memset(ei, 0.0), a)
        for e8 in range(1, 8):
            a = dve(lambda e, i=e8: e.scalar_tensor_tensor(out=ei, in0=kj, scalar=st[:, i:i + 1], in1=ei,
                                                           op0=ALU.is_ge, op1=ALU.add), a)
        te = dve(lambda e: e.tensor_copy(eii, ei), a)
        a = dve(lambda e: e.tensor_tensor(R, R, OF, ALU.add), te)
        a = dve(lambda e: e.scalar_tensor_tensor(out=R, in0=bcast(st, T), scalar=float(SLOTS), in1=R, op0=ALU.mult,
                                                 op1=ALU.add), a)
        for i, pick in enumerate((one, two)):
            a = dve(lambda e, pick=pick: e.tensor_tensor(TM, pick, R, ALU.mult), a)
            a = dve(lambda e, i=i: e.tensor_reduce(sl[i], TM, AX, ALU.add), a)
            a = dve(lambda e, i=i: e.tensor_copy(sli[i], sl[i]), a)
        ts = a
        for i, pick in enumerate((one, two)):
            a = dve(lambda e, pick=pick: e.tensor_tensor(TM, pick, cw, ALU.mult), a)
            a = dve(lambda e, i=i: e.tensor_reduce(wi[i], TM, AX, ALU.add), a)
        tw = a
        for t in range(T):
            for i in range(2):
                xs = dma(pool, None, None, "xs", ts, ready[t] if ready else None,
                         make=lambda e, t=t, i=i: e.indirect_dma_start(
                             out=XS[:, :], out_offset=bass.IndirectOffsetOnAxis(ap=sli[i][:, t:t + 1], axis=0),
                             in_=XN[:, t, :], in_offset=None))
        wused, xused, lw, lx = [None] * 3, [None] * 3, {}, {}

        def weights(k):
            i = k % 3

            def make(e):
                v = e.value_load(eii[0:1, k:k + 1], min_val=0, max_val=7)
                return e.dma_start(W[i], pack[bass.ds(v, 1), :, :].rearrange("o p f -> p (o f)"))
            lw[k] = dma(sp, None, None, "w%d" % i, te, wused[i], make=make)

        def nodes(k):
            i = k % 3
            lx[k] = load(XR[i], XS[k * SLOTS:(k + 1) * SLOTS, :].rearrange("(j p) f -> p j f", p=P), "xr%d" % i,
                         xs, xused[i])

        for k in range(3):
            weights(k)
        cu = [None, None]
        for t in range(T):
            i = t % 2
            b = bank()
            a = pe(lambda e, t=t, b=b: e.transpose(banks[b][0:8, 0:P], cw[:, t, :], ident[0:P, 0:P]), g, free[b])
            free[b] = c = act(lambda e, b=b, i=i: e.activation(cT[i], banks[b][0:8, 0:P], ACT.Copy), a, cu[i])
            b = bank()
            a = pe(lambda e, b=b, i=i: e.matmul(banks[b][0:P, 0:D], cT[i], b2a, start=True, stop=True), c, tb, free[b])
            cu[i] = a
            free[b] = xd = dve(lambda e, b=b, t=t: e.tensor_tensor(X[:, t, :], banks[b][0:P, 0:D], X[:, t, :],
                                                                  ALU.add), a)
        for k in range(3):
            nodes(k)
        eu, hu, yu, hd = [None, None], [None, None], [None, None], {}

        def hidden(k):
            i, j3 = k % 2, k % 3
            w = W[j3]
            w1 = w[:, 0:2 * hid].rearrange("p (k f) -> p k f", k=2)
            b1 = w[:, 2 * hid + hp * D:2 * hid + hp * D + hp]
            bt = bank()
            for kk in range(2):
                for j in range(2):
                    a = pe(lambda e, kk=kk, j=j: e.transpose(
                        banks[bt][:, kk * SLOTS + j * P:kk * SLOTS + (j + 1) * P], XR[j3][:, j, kk * 128:(kk + 1) * 128],
                        ident[0:P, 0:P]), lx[k], free[bt], inc=(kk == 1 and j == 1))
            xused[j3] = a
            if affine:
                gb = w[:, WCn - 4:WCn]
                xl = [dve(lambda e, kk=kk: e.tensor_scalar(
                    XE[i][:, kk, :], banks[bt][:, kk * SLOTS:(kk + 1) * SLOTS], gb[:, kk:kk + 1], gb[:, 2 + kk:3 + kk],
                    ALU.mult, ALU.add), a, lw[k], eu[i]) for kk in range(2)]
            else:
                xl = [dve(lambda e: e.tensor_copy(XE[i].rearrange("p k f -> p (k f)"), banks[bt][:, 0:500]), a, eu[i])]
            free[bt] = xl
            if k + 3 < NT:
                nodes(k + 3)
            hl = []
            for oo in range(hp):
                b = bank()
                for kk in range(2):
                    a = pe(lambda e, b=b, oo=oo, kk=kk: e.matmul(
                        banks[b][:, 0:SLOTS], w1[:, kk, oo * 128:(oo + 1) * 128], XE[i][:, kk, :],
                        start=(kk == 0), stop=(kk == 1)), free[b], lw[k], xl, inc=(kk == 1))
                free[b] = act(lambda e, b=b, oo=oo: e.activation(
                    Hb[i][:, oo, :], banks[b][:, 0:SLOTS], fn, bias=b1[:, oo:oo + 1]), a, lw[k], hu[i])
                hl.append(free[b])
            eu[i] = a
            hd[k] = hl

        def outputs(k):
            i = k % 2
            w2 = W[k % 3][:, 2 * hid:2 * hid + hp * D].rearrange("p (k f) -> p k f", k=hp)
            b = bank()
            for j in range(2):
                for kk in range(hp):
                    a = pe(lambda e, b=b, kk=kk, j=j: e.matmul(
                        banks[b][0:P, j * D:(j + 1) * D], Hb[i][:, kk, j * P:(j + 1) * P], w2[:, kk, :],
                        start=(kk == 0), stop=(kk == hp - 1)), free[b], hd[k], inc=(kk == hp - 1 and j == 1))
            hu[i] = wused[k % 3] = a
            free[b] = c = dve(lambda e, b=b: e.tensor_copy(Y[i].rearrange("p j f -> p (j f)"), banks[b][0:P, 0:512]),
                              a, yu[i])
            yu[i] = dma(pool, YS[k * SLOTS:(k + 1) * SLOTS, :].rearrange("(j p) f -> p j f", p=P), Y[i],
                        "ys%d" % i, c)
            if k + 3 < NT:
                weights(k + 3)

        for k in range(NT + 1):
            if k < NT:
                hidden(k)
            if k:
                outputs(k - 1)
        gu = [None] * 8
        n = 0
        for t in range(T):
            for i in range(2):
                q = n % 8
                n += 1
                gt_ = dma(pool, None, None, "gb%d" % q, yu, gu[q], make=lambda e, t=t, i=i, q=q: e.indirect_dma_start(
                    out=GB[q], out_offset=None, in_=YS[:, :],
                    in_offset=bass.IndirectOffsetOnAxis(ap=sli[i][:, t:t + 1], axis=0)))
                gu[q] = xd = dve(lambda e, t=t, i=i, q=q: e.scalar_tensor_tensor(
                    out=X[:, t, :], in0=GB[q], scalar=wi[i][:, t:t + 1], in1=X[:, t, :], op0=ALU.mult, op1=ALU.add),
                    gt_, xd, tw)
        barrier()

    def l2_ffn(XT):
        hid, hp = 1024, 8
        o = S0 + 6250
        wr = at(o, 2, p=128)
        dma(sp, None, None, None, make=lambda e: e.dma_start(
            wr, inp["L2_ffn_wr"].rearrange("(k p) o -> p (k o)", p=128), allow_slow_non_contiguous=True))
        br, t0 = param_n("L2_ffn_br", o + 2, 1)
        b1, t0 = param_t("L2_ffn_b1", o + 4, 8)
        b2, t0 = param_n("L2_ffn_b2", o + 12)
        o += 268
        wN, r_, cf = at(o, T), at(o + 25, 4, T), at(o + 125, T)
        o += 150
        tmp = o
        o += 125
        wrow = at(o, N)
        o += 3125
        jk = at(o, N)
        o += 3125
        W1 = at(o, 2, hid, p=128)
        t1 = load(W1, inp["L2_ffn_w1"].rearrange("(k p) f -> p k f", p=128), "w0")
        o += 2048
        W2 = at(o, hp, D, p=128)
        t1 = load(W2, inp["L2_ffn_w2"].rearrange("(k p) f -> p k f", p=128), "w0")
        o += 2048
        Hb = [at(o + i * hp * 500, hp, 500, p=128) for i in range(2)]
        o += 8000
        Y = [at(o + i * D, D) for i in range(2)]
        o += 2 * D
        assert o <= K0
        bt = bank()
        for t in range(T):
            for k in range(2):
                a = pe(lambda e, t=t, k=k: e.matmul(banks[bt][0:P, t:t + 1], XT[:, k, t * P:(t + 1) * P],
                                                    wr[:, k:k + 1], start=(k == 0), stop=(k == 1)), t0, free[bt],
                       inc=(k == 1 and t == T - 1))
        free[bt] = a = dve(lambda e: e.tensor_scalar(wN, banks[bt][0:P, 0:T], br[:, 0:1], None, ALU.add), a)
        ro = rows_out(wN, T, 0, tmp, "ro", a)
        lw = row_bcast(wrow, 0, 0, N, "asr", ro)
        z = dve(lambda e: e.memset(r_, 0.0), lw)
        dve.wait(z)
        j0 = None
        for t in range(T):
            sc = wN[:, t:t + 1]
            lo, hi = t * P, (t + 1) * P
            if t:
                j0 = dve(lambda e, sc=sc, lo=lo, t=t: e.tensor_scalar(
                    jk[:, 0:lo], wrow[:, 0:lo], sc, None, ALU.is_ge, ALU.add, accum_out=r_[:, 0, t:t + 1]), j0)
            j0 = dve(lambda e, sc=sc, lo=lo, t=t: e.tensor_scalar(
                jk[:, lo:N], wrow[:, lo:N], sc, None, ALU.is_gt, ALU.add, accum_out=r_[:, 1, t:t + 1]), j0)
            j0 = dve(lambda e, sc=sc, lo=lo, hi=hi, t=t: e.scalar_tensor_tensor(
                out=jk[:, lo:hi], in0=wrow[:, lo:hi], scalar=sc, in1=tri, op0=ALU.is_equal, op1=ALU.mult,
                accum_out=r_[:, 2, t:t + 1]), j0)
        a = dve(lambda e: e.tensor_tensor(r_[:, 0, :], r_[:, 0, :], r_[:, 1, :], ALU.add), j0)
        a = dve(lambda e: e.tensor_tensor(r_[:, 0, :], r_[:, 0, :], r_[:, 2, :], ALU.add), a)
        a = dve(lambda e: e.tensor_scalar(r_[:, 0, :], r_[:, 0, :], 1560.5, None, ALU.is_lt), a)
        a = dve(lambda e: e.tensor_tensor(cf, r_[:, 0, :], wN, ALU.mult), a)
        a = dve(lambda e: e.tensor_tensor(X, X, XN, ALU.add), a)
        dve.wait(a)
        hu, yu = [None, None], [None, None]
        n = 0
        for ci, (n0, w) in enumerate(CH):
            i = ci % 2
            hl = []
            for oo in range(hp):
                b = bank()
                for kk in range(2):
                    a = pe(lambda e, b=b, oo=oo, kk=kk, n0=n0, w=w: e.matmul(
                        banks[b][:, 0:w], W1[:, kk, oo * 128:(oo + 1) * 128], XT[:, kk, n0:n0 + w],
                        start=(kk == 0), stop=(kk == 1)), free[b], t1, inc=(kk == 1))
                free[b] = act(lambda e, b=b, oo=oo, i=i, w=w: e.activation(
                    Hb[i][:, oo, 0:w], banks[b][:, 0:w], ACT.Gelu_apprx_tanh, bias=b1[:, oo:oo + 1]), a, t0, hu[i])
                hl.append(free[b])
            for j in range(w // P):
                t = n0 // P + j
                b = bank()
                for kk in range(hp):
                    a = pe(lambda e, b=b, kk=kk, i=i, j=j: e.matmul(
                        banks[b][0:P, 0:D], Hb[i][:, kk, j * P:(j + 1) * P], W2[:, kk, :],
                        start=(kk == 0), stop=(kk == hp - 1)), free[b], hl, inc=(kk == hp - 1))
                y = n % 2
                n += 1
                free[b] = d = dve(lambda e, b=b, y=y: e.tensor_tensor(Y[y], banks[b][0:P, 0:D], b2, ALU.add), a, yu[y])
                yu[y] = dve(lambda e, y=y, t=t: e.scalar_tensor_tensor(
                    out=X[:, t, :], in0=Y[y], scalar=cf[:, t:t + 1], in1=X[:, t, :], op0=ALU.mult, op1=ALU.add), d)
            hu[i] = a
        barrier()

    wtv = WT.rearrange("(s p) d -> p s d", p=P)
    c16v = C16.rearrange("(s p) d -> p s d", p=P)

    def aggregate(src, k, ro, counts, sink, *tokens):
        if counts:
            Lb = [at(ro + i * 1250, 5, 500, dt=U16) for i in range(2)]
            Vb = [at(ro + 2500 + i * 2500, 5, 500) for i in range(2)]
        else:
            Vb = [at(ro + i * 2500, 5, 500) for i in range(3)]
        nb = len(Vb)
        used = [None] * nb
        lu = [None, None]
        it = 0
        for ci, (n0, w) in enumerate(CH):
            bs = [(ci % 2) * k + kk for kk in range(k)]
            for s5 in range(5):
                i = it % nb
                if counts:
                    l = load(Lb[i][:, :, 0:w], c16v[:, s5 * 5:s5 * 5 + 5, n0:n0 + w], "lb%d" % i, lu[i])
                    l = copy_out(it, Vb[i][:, :, 0:w], Lb[i][:, :, 0:w], l, used[i])
                    lu[i] = l
                else:
                    l = load(Vb[i][:, :, 0:w], wtv[:, s5 * 5:s5 * 5 + 5, n0:n0 + w], "lb%d" % i, used[i])
                it += 1
                for s in range(5):
                    for kk in range(k):
                        a = pe(lambda e, i=i, s=s, s5=s5, kk=kk, b=bs[kk], w=w: e.matmul(
                            banks[b][:, 0:w], src[:, s5 * 5 + s, kk * 128:(kk + 1) * 128], Vb[i][:, s, 0:w],
                            start=(s5 == 0 and s == 0), stop=(s5 == 4 and s == 4)), l, free[bs[kk]], *tokens)
                used[i] = a
            ends = sink(ci, n0, w, bs, a)
            for kk in range(k):
                free[bs[kk]] = ends[kk]

    def bn(v, g, bb, o, relu, *tokens):
        s = at(o, 2 * T, 6, p=128)
        m = at(o + 300, 2, 2, p=128)
        sc, sh, tm = at(o + 304, 2, p=128), at(o + 306, 2, p=128), at(o + 308, 2, p=128)
        dve.wait(*tokens)
        for k in range(2):
            for c in range(T):
                a = dve(lambda e, k=k, c=c: e.bn_stats(s[:, k * T + c, :], v[:, k, c * P:(c + 1) * P]))
        dve.wait(a)
        for k in range(2):
            a = dve(lambda e, k=k: e.bn_aggr(m[:, k, :], s[:, k * T:(k + 1) * T, :].rearrange("p a b -> p (a b)")))
        a = rstd(m[:, :, 1], sc, tm, a)
        a = dve(lambda e: e.tensor_tensor(sc, sc, g, ALU.mult), a)
        for k in range(2):
            a = dve(lambda e, k=k: e.tensor_scalar(v[:, k, :], v[:, k, :], m[:, k, 0:1], sc[:, k:k + 1],
                                                   ALU.subtract, ALU.mult), a)
        for k in range(2):
            a = act(lambda e, k=k: e.activation(v[:, k, :], v[:, k, :], ACT.Relu if relu else ACT.Identity,
                                                bias=bb[:, k:k + 1]), a)
        return a

    def l1_gnn(XT):
        hN = at(S0 + 6250, T, D)
        ro = S0 + 12650
        ag = [at(S0 + 20150 + i * 1000, 2, 500, p=128) for i in range(2)]
        h2 = at(S0 + 22150, 2, N, p=128)
        o = S0 + 28400
        w1, t1 = weight("L1_gnn_c1_w1", o, 2, D)
        w2, t1 = weight("L1_gnn_c1_w2", o + 512, 2, D)
        w3, t1 = weight("L1_gnn_c2_w1", o + 1024, 2, D)
        w4, t1 = weight("L1_gnn_c2_w2", o + 1536, 2, D)
        o += 2048
        b1, t0 = param_n("L1_gnn_c1_b1", o)
        b3, t0 = param_n("L1_gnn_c2_b1", o + 256)
        o += 512
        pt = {}
        for nme in ("c1_b2", "c1_g", "c1_b", "bn1_g", "bn1_b", "c2_b2", "c2_g", "c2_b", "bn2_g", "bn2_b"):
            pt[nme], t0 = param_t("L1_gnn_" + nme, o)
            o += 2
        bo = o
        assert o + 310 <= K0

        def conv(srcT, wa, ba, wb, bb, ready):
            def sink(t, ps, a):
                a = dve(lambda e: e.tensor_tensor(hN[:, t, :], ps, ba, ALU.add), a, t0)
                relu.append(dve(lambda e: e.tensor_scalar(hN[:, t, :], hN[:, t, :], 0.0, None, ALU.max), a))
                return a
            relu = []
            lin_N(srcT, 2, wa, D, sink, t1, ready)
            agu = [None, None]
            fin = []

            def sink2(ci, n0, w, bs, a):
                i = ci % 2
                ends = [copy_out(kk, ag[i][:, kk, 0:w], banks[bs[kk]][:, 0:w], a, agu[i]) for kk in range(2)]
                for oo in range(2):
                    b = bank((4, 8))
                    for kk in range(2):
                        m = pe(lambda e, b=b, kk=kk, oo=oo, i=i, w=w: e.matmul(
                            banks[b][:, 0:w], wb[:, kk, oo * 128:(oo + 1) * 128], ag[i][:, kk, 0:w],
                            start=(kk == 0), stop=(kk == 1)), free[b], ends, inc=(kk == 1))
                    free[b] = act(lambda e, b=b, oo=oo, n0=n0, w=w: e.activation(
                        h2[:, oo, n0:n0 + w], banks[b][:, 0:w], ACT.Identity, bias=bb[:, oo:oo + 1]), m)
                    fin.append(free[b])
                agu[i] = m
                return ends

            aggregate(hN, 2, ro, False, sink2, relu)
            return fin

        f = conv(XT, w1, b1, w2, pt["c1_b2"], None)
        a = bn(h2, pt["c1_g"], pt["c1_b"], bo, True, f)
        a = bn(h2, pt["bn1_g"], pt["bn1_b"], bo, True, a)
        barrier()
        f = conv(h2, w3, b3, w4, pt["c2_b2"], None)
        a = bn(h2, pt["c2_g"], pt["c2_b"], bo, True, f)
        a = bn(h2, pt["bn2_g"], pt["bn2_b"], bo, False, a)
        a = dve(lambda e: e.tensor_tensor(h2, h2, XT, ALU.add), a)
        a = dve(lambda e: e.tensor_scalar(h2, h2, 0.0, None, ALU.max), a)
        add_from_T(h2, 2, 0, N, a)
        barrier()

    def l3_gnn():
        u = at(XN0, T, D)
        z2 = at(XN0, T, 512)
        hT = at(19200, 4, N, p=128)
        o = 31700
        ro = o
        o += 7500
        wt = at(o, 2048, p=128)
        o += 2048
        dvB = at(o, N, p=128)
        o += 3125
        ag = [at(o + i * 2000, 4, 500, p=128) for i in range(2)]
        o += 4000
        dvN = at(o, T)
        o += 25
        b1, t0 = param_t("L3_gnn_b1", o, 4)
        b2, t0 = param_t("L3_gnn_b2", o + 4, 4)
        b3, t0 = param_t("L3_gnn_b3", o + 8, 2)
        o += 10
        assert o <= K0
        l = load(dvB, DEG[0, :].partition_broadcast(128), "dg")
        l = dma(sp, None, None, "dg", make=lambda e: e.dma_start(
            dvN, DEG.rearrange("o (t p) -> p (o t)", p=P), allow_slow_non_contiguous=True))
        a = act(lambda e: e.activation(dvB, dvB, ACT.Sqrt), l)
        a = act(lambda e: e.activation(dvN, dvN, ACT.Sqrt), l)
        a = dve(lambda e: e.reciprocal(dvB, dvB), a)
        a = dve(lambda e: e.reciprocal(dvN, dvN), a)
        us = [dve(lambda e, t=t: e.tensor_scalar(u[:, t, :], u[:, t, :], dvN[:, t:t + 1], None, ALU.mult), a)
              for t in range(T)]
        W1 = wt[:, 0:1024].rearrange("p (k f) -> p k f", k=2)
        t1 = load(W1, inp["L3_gnn_W1"].rearrange("(k p) f -> p k f", p=128), None)
        agu = [None, None]

        def sink1(ci, n0, w, bs, a):
            i = ci % 2
            ends = [dve(lambda e, kk=kk, i=i: e.tensor_tensor(ag[i][:, kk, 0:w], banks[bs[kk]][:, 0:w],
                                                              dvB[:, n0:n0 + w], ALU.mult), a, agu[i])
                    for kk in range(2)]
            for oo in range(4):
                b = bank((4, 8))
                for kk in range(2):
                    m = pe(lambda e, b=b, kk=kk, oo=oo: e.matmul(
                        banks[b][:, 0:w], W1[:, kk, oo * 128:(oo + 1) * 128], ag[i][:, kk, 0:w],
                        start=(kk == 0), stop=(kk == 1)), free[b], ends, t1, inc=(kk == 1))
                free[b] = act(lambda e, b=b, oo=oo: e.activation(
                    hT[:, oo, n0:n0 + w], banks[b][:, 0:w], ACT.Tanh, bias=b1[:, oo:oo + 1]), m, t0)
            agu[i] = m
            return ends

        aggregate(u, 2, ro, True, sink1, us)
        barrier()
        W2 = wt.rearrange("p (k f) -> p k f", k=4)
        t1 = load(W2, inp["L3_gnn_W2"].rearrange("(k p) f -> p k f", p=128), None)

        def sinkz(t, ps, a):
            return evac(t, lambda e: e.activation(z2[:, t, :], ps, ACT.Copy, scale=dvN[:, t:t + 1]),
                        lambda e: e.tensor_scalar(z2[:, t, :], ps, dvN[:, t:t + 1], None, ALU.mult), a)

        lin_N(hT, 4, W2, 512, sinkz, t1)
        barrier()

        def sink2(ci, n0, w, bs, a):
            i = ci % 2
            ends = []
            for kk in range(4):
                m = dve(lambda e, kk=kk: e.tensor_tensor(ag[i][:, kk, 0:w], banks[bs[kk]][:, 0:w],
                                                         dvB[:, n0:n0 + w], ALU.mult), a, agu[i])
                ends.append(m)
                m = act(lambda e, kk=kk: e.activation(hT[:, kk, n0:n0 + w], ag[i][:, kk, 0:w], ACT.Tanh,
                                                      bias=b2[:, kk:kk + 1]), m)
            agu[i] = m
            return ends

        agu = [None, None]
        aggregate(z2, 4, ro, True, sink2)
        barrier()
        W3 = wt[:, 0:1024].rearrange("p (k f) -> p k f", k=4)
        t1 = load(W3, inp["L3_gnn_W3"].rearrange("(k p) f -> p k f", p=128), None)

        def sinkz3(t, ps, a):
            return evac(t, lambda e: e.activation(u[:, t, :], ps, ACT.Copy, scale=dvN[:, t:t + 1]),
                        lambda e: e.tensor_scalar(u[:, t, :], ps, dvN[:, t:t + 1], None, ALU.mult), a)

        z3 = lin_N(hT, 4, W3, D, sinkz3, t1)
        agu = [None, None]

        def sink3(ci, n0, w, bs, a):
            i = ci % 2
            ends = []
            for kk in range(2):
                m = dve(lambda e, kk=kk: e.tensor_tensor(ag[i][:, kk, 0:w], banks[bs[kk]][:, 0:w],
                                                         dvB[:, n0:n0 + w], ALU.mult), a, agu[i])
                ends.append(m)
                m = act(lambda e, kk=kk: e.activation(ag[i][:, kk, 0:w], ag[i][:, kk, 0:w], ACT.Identity,
                                                      bias=b3[:, kk:kk + 1]), m)
            for j in range(w // P):
                t = n0 // P + j
                b = bank((4, 8))
                for kk in range(2):
                    x = pe(lambda e, kk=kk, j=j, b=b: e.transpose(
                        banks[b][0:P, kk * 128:(kk + 1) * 128], ag[i][:, kk, j * P:(j + 1) * P], ident[:, :]),
                        free[b], m, inc=(kk == 1))
                free[b] = dve(lambda e, t=t, b=b: e.tensor_tensor(X[:, t, :], banks[b][0:P, 0:D], X[:, t, :],
                                                                  ALU.add), x)
            agu[i] = x
            return ends

        aggregate(u, 2, ro, True, sink3, z3)
        barrier()

    XT = at(S0, 2, N, p=128)

    def norm_turn(end=None):
        nt = norm_tiles(X, XN)
        to_T(XN, XT, nt)
        (end or barrier)()

    def run():
        expert_consts()
        work = graph_pairs(None)
        next(work)
        dve.beside, dve.every = work, 4
        norm_turn(lambda: fence(*GRAPH))
        l0_mix(XT)
        gat_source("L0_gnn", 4, 64, XT)
        dve.beside = None
        for _ in work:
            pass
        barrier()
        asN, mx = gat_names(4, 64)[2], gat_names(4, 64)[5]
        graph_split(asN, mx)
        if stop == "graph":
            return
        gat_sum("L0_gnn", 4, 64, 1e-16)
        if stop == "g0":
            return
        norm_turn()
        ffn(XT, "L0_ffn", 512, ACT.Gelu, "all", "L0_ffn_gate_w", ["L0_ffn_gate_b"])
        if stop == "f0":
            return
        norm_turn()
        l1_mix(XT)
        if stop == "m1":
            return
        l1_gnn(XT)
        if stop == "g1":
            return
        norm_turn()
        ffn(XT, "L1_ffn", 512, ACT.Relu, "two", "L1_ffn_Wg", ["L1_ffn_bg", "L1_ffn_bias"])
        if stop == "f1":
            return
        norm_turn()
        l2_mix(XT)
        if stop == "m2":
            return
        gat_source("L2_gnn", 8, 32, XT)
        barrier()
        gat_largest(8, gat_names(8, 32)[2], gat_names(8, 32)[5])
        gat_sum("L2_gnn", 8, 32, 0.0)
        if stop == "g2":
            return
        norm_turn()
        l2_ffn(XT)
        if stop == "f2":
            return
        norm_turn()
        l3_mix(XT)
        if stop == "m3":
            return
        l3_gnn()
        if stop == "g3":
            return
        norm_turn()
        ffn(XT, "L3_ffn", 1024, ACT.Gelu, "share", "L3_ffn_Wr", ["L3_ffn_br"],
            affine=True, again=True)

    run()
    t = load(rows(out, P), X, "out", dve.last)
    sp.wait(t)
    with ctx:
        block = ctx.enter_context(nc.Block())

        @block.tensor
        def _(eng):
            pe.emit(eng)

        @block.scalar
        def _(eng):
            act.emit(eng)

        @block.vector
        def _(eng):
            dve.emit(eng)

        @block.gpsimd
        def _(eng):
            pool.emit(eng)

        @block.sync
        def _(eng):
            sp.emit(eng)


_DERIVED = {"L0_mix_w_qkv": "w", "L0_mix_b_qkv": "b", "L3_mix_wq": "wqT", "L3_mix_wk": "wkT", "L3_mix_wv": "wvT",
            "L3_mix_wo": "woT"}
_UNUSED = {"L2_ffn_attention_mask"}


def _layout(inputs):
    arrays = {}
    for name, value in inputs.items():
        a = np.asarray(value)
        if name in _UNUSED:
            continue
        if name == "L0_mix_w_qkv":
            v = a.reshape(D, 8, 3, 32)
            for i, c in enumerate("qkv"):
                arrays[f"w{c}0"] = np.ascontiguousarray(v[:, :, i, :].reshape(D, D))
        elif name == "L0_mix_b_qkv":
            v = a.reshape(8, 3, 32)
            for i, c in enumerate("qkv"):
                arrays[f"b{c}0"] = np.ascontiguousarray(v[:, i, :].reshape(D))
        elif name in _DERIVED:
            arrays[_DERIVED[name]] = np.ascontiguousarray(a.T)
        else:
            arrays[name] = np.ascontiguousarray(a)
    for pre, hid in (("L0_ffn", 512), ("L1_ffn", 512), ("L3_ffn", 1024)):
        def lanes(a, k):
            return a.reshape(8, k, 128, -1).transpose(0, 2, 1, 3).reshape(8, 128, -1)
        parts = [lanes(arrays.pop(pre + "_W1"), 2), lanes(arrays.pop(pre + "_W2"), hid // 128),
                 lanes(arrays.pop(pre + "_b1"), hid // 128)]
        if pre == "L3_ffn":
            parts += [lanes(arrays.pop(pre + "_ln_g"), 2), lanes(arrays.pop(pre + "_ln_b"), 2)]
        arrays[pre + "_pack"] = np.ascontiguousarray(np.concatenate(parts, axis=2))
    return arrays


STOP = None


def kernel(**inputs):
    import concourse.bacc as bacc
    from concourse.bass_utils import run_bass_kernel_spmd

    nc = bacc.Bacc("TRN2", target_bir_lowering=False, num_devices=1)
    arrays = _layout(inputs)
    aps = {n: nc.dram_tensor(n, a.shape, mybir.dt.from_np(a.dtype), kind="ExternalInput").ap()
           for n, a in arrays.items()}
    out = nc.dram_tensor("out", (N, D), F32, kind="ExternalOutput").ap()
    program(nc, aps, out, STOP)
    r = run_bass_kernel_spmd(nc, [arrays], core_ids=[0])
    return r.results[0]["out"]
```
